# Optimizing a Trainium2 kernel written in Bass

```python
import numpy as np
import jax
import jax.numpy as jnp

def _softmax(x, axis=-1):
    return jax.nn.softmax(x, axis=axis)

def _gelu(x):
    return jax.nn.gelu(x, approximate=True)

def _silu(x):
    return jax.nn.silu(x)

def _sigmoid(x):
    return jax.nn.sigmoid(x)

def _layernorm(x, axis=-1, eps=1e-05):
    m = jnp.mean(x, axis=axis, keepdims=True)
    v = jnp.var(x, axis=axis, keepdims=True)
    return (x - m) / jnp.sqrt(v + eps)

def _scatter_add(tgt, idx, src, axis=0):
    return tgt.at[idx].add(src)

def _segment_sum(src, seg, n):
    return jax.ops.segment_sum(src, seg, n)
kernel_name = 'mk_adj_ffn_d2_adj_r2_e082b6'

def setup_inputs(seed: int=0):
    np.random.seed(seed)
    _w = jnp.asarray

    def _rec_inputs():
        import jax
        import jax.numpy as jnp
        _gk = jax.random.key(seed)
        x = -0.0002928 + 1 * jax.random.normal(jax.random.fold_in(_gk, 1), (128, 128, 128), jnp.float32)
        _a = jax.random.bernoulli(jax.random.fold_in(_gk, 2), 0.0625, (128, 128, 128))
        _af = _a.astype(jnp.float32)
        adj = _af
        return (x, adj)
    x, adj = _rec_inputs()

    def _L0_gnn_setup():
        import jax, jax.numpy as jnp
        import numpy as np
        ALPHA = 0.2
        EPS = 1e-05
        NEG = -9000000000000000.0
        key = jax.random.key(seed)
        k1, k2, k3, k4 = jax.random.split(key, 4)
        B, N, F_in, F_out = (8, 1024, 128, 128)
        h = jax.random.normal(k1, (B, N, F_in), dtype=jnp.float32)
        adj = jax.random.randint(k2, (B, N, N), 0, 2).astype(jnp.float32)
        W = jax.random.normal(k3, (F_in, F_out), dtype=jnp.float32) * (1.414 * np.sqrt(2.0 / (F_in + F_out)))
        a = jax.random.normal(k4, (2 * F_out, 1), dtype=jnp.float32) * (1.414 * np.sqrt(2.0 / (2 * F_out + 1)))
        gamma = jnp.ones((F_out,), dtype=jnp.float32)
        beta = jnp.zeros((F_out,), dtype=jnp.float32)
        return {'h': h, 'adj': adj, 'W': W, 'a': a, 'gamma': gamma, 'beta': beta}
    _L0_gnn_all = _L0_gnn_setup()
    _L0_gnn_in = {k: v for k, v in _L0_gnn_all.items() if k in ('W', 'a', 'gamma', 'beta')}
    del _L0_gnn_all

    def _L0_ffn_setup():
        import jax, jax.numpy as jnp
        import numpy as np
        B, N, D = (16, 2048, 128)
        NUM_EXPERTS, TOP_K, HEADS = (4, 2, 4)
        N_EDGES = 524288
        LN_EPS = 1e-05

        def _layernorm(x, g, b):
            mu = x.mean(-1, keepdims=True)
            var = ((x - mu) ** 2).mean(-1, keepdims=True)
            return (x - mu) * jax.lax.rsqrt(var + LN_EPS) * g + b

        def _forward(x, edge_index, W_gat, att_src, att_dst, b_gat, ln_gamma, ln_beta, W1, b1, W2, b2):
            Bc, Nc, Dc = x.shape
            M = Bc * Nc
            x_flat = x.reshape(M, Dc)
            h = (x_flat @ W_gat).reshape(M, HEADS, NUM_EXPERTS)
            loops = jnp.arange(M, dtype=edge_index.dtype)
            src = jnp.concatenate([edge_index[0], loops])
            dst = jnp.concatenate([edge_index[1], loops])
            a_src = (h * att_src).sum(-1)
            a_dst = (h * att_dst).sum(-1)
            e = jax.nn.leaky_relu(a_src[src] + a_dst[dst], negative_slope=0.2)
            e_max = jax.ops.segment_max(e, dst, num_segments=M)
            ee = jnp.exp(e - e_max[dst])
            denom = jax.ops.segment_sum(ee, dst, num_segments=M)
            alpha = ee / (denom[dst] + 1e-16)
            msg = h[src] * alpha[:, :, None]
            agg = jax.ops.segment_sum(msg, dst, num_segments=M).reshape(M, HEADS * NUM_EXPERTS) + b_gat
            scores = _layernorm(agg, ln_gamma, ln_beta).reshape(M, HEADS, NUM_EXPERTS).mean(1)
            scores = scores.reshape(Bc, Nc, NUM_EXPERTS)
            topk_s, topk_i = jax.lax.top_k(scores, TOP_K)
            w = jax.nn.softmax(topk_s, axis=-1)
            out = jnp.zeros_like(x)
            for ei in range(NUM_EXPERTS):
                g = jnp.where(topk_i == ei, w, 0.0).sum(-1)
                hh = jax.nn.gelu(x @ W1[ei] + b1[ei], approximate=False)
                out = out + g[..., None] * (hh @ W2[ei] + b2[ei])
            return out
        key = jax.random.key(seed)
        ks = jax.random.split(key, 8)
        s = 0.05
        return {'x': jax.random.normal(ks[0], (B, N, D), jnp.float32), 'W_gat': jax.random.normal(ks[1], (D, HEADS * NUM_EXPERTS), jnp.float32) * s, 'att_src': jax.random.normal(ks[2], (HEADS, NUM_EXPERTS), jnp.float32) * s, 'att_dst': jax.random.normal(ks[3], (HEADS, NUM_EXPERTS), jnp.float32) * s, 'b_gat': jnp.zeros((HEADS * NUM_EXPERTS,), jnp.float32), 'ln_gamma': jnp.ones((HEADS * NUM_EXPERTS,), jnp.float32), 'ln_beta': jnp.zeros((HEADS * NUM_EXPERTS,), jnp.float32), 'W1': jax.random.normal(ks[4], (NUM_EXPERTS, D, 2 * D), jnp.float32) * s, 'b1': jnp.zeros((NUM_EXPERTS, 2 * D), jnp.float32), 'W2': jax.random.normal(ks[5], (NUM_EXPERTS, 2 * D, D), jnp.float32) * s, 'b2': jnp.zeros((NUM_EXPERTS, D), jnp.float32), 'edge_index': jax.random.randint(ks[6], (2, N_EDGES), 0, B * N, jnp.int32)}
    _L0_ffn_all = _L0_ffn_setup()
    _L0_ffn_in = {k: v for k, v in _L0_ffn_all.items() if k in ('W_gat', 'att_src', 'att_dst', 'b_gat', 'ln_gamma', 'ln_beta', 'W1', 'b1', 'W2', 'b2', 'edge_index')}
    del _L0_ffn_all

    def _L1_gnn_setup():
        import jax, jax.numpy as jnp
        import numpy as np
        GROUPS = [list(range(25)), [0, 1, 2, 3, 4, 5, 6, 7, 8], [0, 9, 10, 11, 12, 13, 14], [6, 7, 8, 12, 13, 14], [3, 4, 5, 9, 10, 11]]
        B, N, D_IN, D_HID = (4096, 25, 128, 256)

        def _graph_conv(x, adj, W, b):
            n = adj.shape[-1]
            A = adj + jnp.eye(n, dtype=adj.dtype)
            deg = jnp.sum(A, axis=-1)
            deg_safe = jnp.where(deg == 0, 1.0, deg)
            dinv = jnp.where(deg == 0, 0.0, deg_safe ** (-0.5))
            norm_adj = dinv[:, :, None] * A * dinv[:, None, :]
            support = jnp.einsum('bnd,de->bne', x, W)
            out = jnp.einsum('bnm,bme->bne', norm_adj, support) + b
            return jax.nn.relu(out)
        key = jax.random.key(seed)
        ks = jax.random.split(key, 7)
        s1 = float(np.sqrt(6.0 / (D_IN + D_HID)))
        s2 = float(np.sqrt(6.0 / (D_HID + D_IN)))
        return {'x': jax.random.normal(ks[0], (B, N, D_IN), dtype=jnp.float32), 'adj': jax.random.uniform(ks[1], (B, N, N), dtype=jnp.float32), 'W1': jax.random.uniform(ks[2], (5, D_IN, D_HID), jnp.float32, -s1, s1), 'b1': jnp.zeros((5, D_HID), dtype=jnp.float32), 'W2': jax.random.uniform(ks[3], (5, D_HID, D_IN), jnp.float32, -s2, s2), 'b2': jnp.zeros((5, D_IN), dtype=jnp.float32), 'fusion_w': jnp.ones((5,), dtype=jnp.float32)}
    _L1_gnn_all = _L1_gnn_setup()
    _L1_gnn_in = {k: v for k, v in _L1_gnn_all.items() if k in ('W1', 'b1', 'W2', 'b2', 'fusion_w')}
    del _L1_gnn_all

    def _L1_ffn_setup():
        import jax, jax.numpy as jnp
        import numpy as np
        B, S, H, F, E, K = (8, 2048, 128, 256, 16, 2)
        EPS = 1e-05
        key = jax.random.key(seed)
        ks = jax.random.split(key, 9)
        sc = 0.02
        return {'x': jax.random.normal(ks[0], (B, S, H), dtype=jnp.float32), 'gate_w': jax.random.normal(ks[1], (H, E), dtype=jnp.float32) * sc, 'gate_b': jnp.zeros((E,), dtype=jnp.float32), 'w1': jax.random.normal(ks[2], (E, H, F), dtype=jnp.float32) * sc, 'b1': jnp.zeros((E, F), dtype=jnp.float32), 'w2': jax.random.normal(ks[3], (E, F, H), dtype=jnp.float32) * sc, 'b2': jnp.zeros((E, H), dtype=jnp.float32), 'gamma': jnp.ones((H,), dtype=jnp.float32), 'beta': jnp.zeros((H,), dtype=jnp.float32)}
    _L1_ffn_all = _L1_ffn_setup()
    _L1_ffn_in = {k: v for k, v in _L1_ffn_all.items() if k in ('gate_w', 'gate_b', 'w1', 'b1', 'w2', 'b2', 'gamma', 'beta')}
    del _L1_ffn_all
    return {'x': x, 'adj': adj, 'L0_gnn_W': _L0_gnn_in['W'], 'L0_gnn_a': _L0_gnn_in['a'], 'L0_gnn_gamma': _L0_gnn_in['gamma'], 'L0_gnn_beta': _L0_gnn_in['beta'], 'L0_ffn_W_gat': _L0_ffn_in['W_gat'], 'L0_ffn_att_src': _L0_ffn_in['att_src'], 'L0_ffn_att_dst': _L0_ffn_in['att_dst'], 'L0_ffn_b_gat': _L0_ffn_in['b_gat'], 'L0_ffn_ln_gamma': _L0_ffn_in['ln_gamma'], 'L0_ffn_ln_beta': _L0_ffn_in['ln_beta'], 'L0_ffn_W1': _L0_ffn_in['W1'], 'L0_ffn_b1': _L0_ffn_in['b1'], 'L0_ffn_W2': _L0_ffn_in['W2'], 'L0_ffn_b2': _L0_ffn_in['b2'], 'L0_ffn_edge_index': _L0_ffn_in['edge_index'], 'L1_gnn_W1': _L1_gnn_in['W1'], 'L1_gnn_b1': _L1_gnn_in['b1'], 'L1_gnn_W2': _L1_gnn_in['W2'], 'L1_gnn_b2': _L1_gnn_in['b2'], 'L1_gnn_fusion_w': _L1_gnn_in['fusion_w'], 'L1_ffn_gate_w': _L1_ffn_in['gate_w'], 'L1_ffn_gate_b': _L1_ffn_in['gate_b'], 'L1_ffn_w1': _L1_ffn_in['w1'], 'L1_ffn_b1': _L1_ffn_in['b1'], 'L1_ffn_w2': _L1_ffn_in['w2'], 'L1_ffn_b2': _L1_ffn_in['b2'], 'L1_ffn_gamma': _L1_ffn_in['gamma'], 'L1_ffn_beta': _L1_ffn_in['beta']}

def reference(x, adj, L0_gnn_W, L0_gnn_a, L0_gnn_gamma, L0_gnn_beta, L0_ffn_W_gat, L0_ffn_att_src, L0_ffn_att_dst, L0_ffn_b_gat, L0_ffn_ln_gamma, L0_ffn_ln_beta, L0_ffn_W1, L0_ffn_b1, L0_ffn_W2, L0_ffn_b2, L0_ffn_edge_index, L1_gnn_W1, L1_gnn_b1, L1_gnn_W2, L1_gnn_b2, L1_gnn_fusion_w, L1_ffn_gate_w, L1_ffn_gate_b, L1_ffn_w1, L1_ffn_b1, L1_ffn_w2, L1_ffn_b2, L1_ffn_gamma, L1_ffn_beta):
    import jax
    import jax.numpy as jnp

    def _L0_gnn_ref(h, adj, W, a, gamma, beta):
        import jax, jax.numpy as jnp
        import numpy as np
        ALPHA = 0.2
        EPS = 1e-05
        NEG = -9000000000000000.0
        F_out = W.shape[1]
        Wh = jnp.matmul(h, W)
        a1 = a[:F_out, 0]
        a2 = a[F_out:, 0]
        s1 = jnp.einsum('bnf,f->bn', Wh, a1)
        s2 = jnp.einsum('bnf,f->bn', Wh, a2)
        e = s1[:, :, None] + s2[:, None, :]
        e = jnp.where(e > 0, e, ALPHA * e)
        e = jnp.where(adj > 0, e, NEG)
        attention = jax.nn.softmax(e, axis=2)
        h_prime = jnp.matmul(attention, Wh)
        mu = jnp.mean(h_prime, axis=-1, keepdims=True)
        var = jnp.mean(jnp.square(h_prime - mu), axis=-1, keepdims=True)
        hn = (h_prime - mu) / jnp.sqrt(var + EPS) * gamma + beta
        return jax.nn.gelu(hn, approximate=False)

    def _L0_ffn_ref(x, W_gat, att_src, att_dst, b_gat, ln_gamma, ln_beta, W1, b1, W2, b2, edge_index):
        import jax, jax.numpy as jnp
        import numpy as np
        B, N, D = (16, 2048, 128)
        NUM_EXPERTS, TOP_K, HEADS = (4, 2, 4)
        N_EDGES = 524288
        LN_EPS = 1e-05

        def _layernorm(x, g, b):
            mu = x.mean(-1, keepdims=True)
            var = ((x - mu) ** 2).mean(-1, keepdims=True)
            return (x - mu) * jax.lax.rsqrt(var + LN_EPS) * g + b

        def _forward(x, edge_index, W_gat, att_src, att_dst, b_gat, ln_gamma, ln_beta, W1, b1, W2, b2):
            Bc, Nc, Dc = x.shape
            M = Bc * Nc
            x_flat = x.reshape(M, Dc)
            h = (x_flat @ W_gat).reshape(M, HEADS, NUM_EXPERTS)
            loops = jnp.arange(M, dtype=edge_index.dtype)
            src = jnp.concatenate([edge_index[0], loops])
            dst = jnp.concatenate([edge_index[1], loops])
            a_src = (h * att_src).sum(-1)
            a_dst = (h * att_dst).sum(-1)
            e = jax.nn.leaky_relu(a_src[src] + a_dst[dst], negative_slope=0.2)
            e_max = jax.ops.segment_max(e, dst, num_segments=M)
            ee = jnp.exp(e - e_max[dst])
            denom = jax.ops.segment_sum(ee, dst, num_segments=M)
            alpha = ee / (denom[dst] + 1e-16)
            msg = h[src] * alpha[:, :, None]
            agg = jax.ops.segment_sum(msg, dst, num_segments=M).reshape(M, HEADS * NUM_EXPERTS) + b_gat
            scores = _layernorm(agg, ln_gamma, ln_beta).reshape(M, HEADS, NUM_EXPERTS).mean(1)
            scores = scores.reshape(Bc, Nc, NUM_EXPERTS)
            topk_s, topk_i = jax.lax.top_k(scores, TOP_K)
            w = jax.nn.softmax(topk_s, axis=-1)
            out = jnp.zeros_like(x)
            for ei in range(NUM_EXPERTS):
                g = jnp.where(topk_i == ei, w, 0.0).sum(-1)
                hh = jax.nn.gelu(x @ W1[ei] + b1[ei], approximate=False)
                out = out + g[..., None] * (hh @ W2[ei] + b2[ei])
            return out
        return _forward(x, edge_index, W_gat, att_src, att_dst, b_gat, ln_gamma, ln_beta, W1, b1, W2, b2)

    def _L1_gnn_ref(x, adj, W1, b1, W2, b2, fusion_w):
        import jax, jax.numpy as jnp
        import numpy as np
        GROUPS = [list(range(25)), [0, 1, 2, 3, 4, 5, 6, 7, 8], [0, 9, 10, 11, 12, 13, 14], [6, 7, 8, 12, 13, 14], [3, 4, 5, 9, 10, 11]]
        B, N, D_IN, D_HID = (4096, 25, 128, 256)

        def _graph_conv(x, adj, W, b):
            n = adj.shape[-1]
            A = adj + jnp.eye(n, dtype=adj.dtype)
            deg = jnp.sum(A, axis=-1)
            deg_safe = jnp.where(deg == 0, 1.0, deg)
            dinv = jnp.where(deg == 0, 0.0, deg_safe ** (-0.5))
            norm_adj = dinv[:, :, None] * A * dinv[:, None, :]
            support = jnp.einsum('bnd,de->bne', x, W)
            out = jnp.einsum('bnm,bme->bne', norm_adj, support) + b
            return jax.nn.relu(out)
        norm_w = jax.nn.softmax(fusion_w)
        fused = jnp.zeros_like(x)
        for g, idx_list in enumerate(GROUPS):
            idx = jnp.asarray(idx_list)
            x_g = x[:, idx, :]
            adj_g = adj[:, idx][:, :, idx]
            h = _graph_conv(x_g, adj_g, W1[g], b1[g])
            out_g = _graph_conv(h, adj_g, W2[g], b2[g])
            fused = fused.at[:, idx, :].add(norm_w[g] * out_g)
        return fused

    def _L1_ffn_ref(x, gate_w, gate_b, w1, b1, w2, b2, gamma, beta):
        import jax, jax.numpy as jnp
        import numpy as np
        B, S, H, F, E, K = (8, 2048, 128, 256, 16, 2)
        EPS = 1e-05
        gate_logits = x @ gate_w + gate_b
        topk_vals, topk_idx = jax.lax.top_k(gate_logits, K)
        topk_w = jax.nn.softmax(topk_vals, axis=-1)
        h = jax.nn.relu(jnp.einsum('bsh,ehf->bsef', x, w1) + b1)
        expert_out = jnp.einsum('bsef,efh->bseh', h, w2) + b2
        sel = jnp.take_along_axis(expert_out, topk_idx[:, :, :, None], axis=2)
        moe = jnp.sum(topk_w[..., None] * sel, axis=2)
        y = x + moe
        mu = jnp.mean(y, axis=-1, keepdims=True)
        var = jnp.var(y, axis=-1, keepdims=True)
        return (y - mu) / jnp.sqrt(var + EPS) * gamma + beta
    x = x + _L0_gnn_ref(_layernorm(x, axis=-1), adj, L0_gnn_W, L0_gnn_a, L0_gnn_gamma, L0_gnn_beta)
    x = x + _L0_ffn_ref(_layernorm(x, axis=-1), L0_ffn_W_gat, L0_ffn_att_src, L0_ffn_att_dst, L0_ffn_b_gat, L0_ffn_ln_gamma, L0_ffn_ln_beta, L0_ffn_W1, L0_ffn_b1, L0_ffn_W2, L0_ffn_b2, L0_ffn_edge_index)
    x = x + _L1_gnn_ref(_layernorm(x, axis=-1), adj, L1_gnn_W1, L1_gnn_b1, L1_gnn_W2, L1_gnn_b2, L1_gnn_fusion_w)
    x = x + _L1_ffn_ref(_layernorm(x, axis=-1), L1_ffn_gate_w, L1_ffn_gate_b, L1_ffn_w1, L1_ffn_b1, L1_ffn_w2, L1_ffn_b2, L1_ffn_gamma, L1_ffn_beta)
    return x

_drawn_inputs = setup_inputs


def setup_inputs(seed=0):
    import zlib

    import numpy as np

    out = dict(_drawn_inputs(seed))
    spreads = {'L0_gnn_gamma': (1.0, 0.2),
     'L0_gnn_beta': (0.0, 0.1),
     'L0_ffn_b_gat': (0.0, 0.1),
     'L0_ffn_ln_gamma': (1.0, 0.2),
     'L0_ffn_ln_beta': (0.0, 0.1),
     'L0_ffn_b1': (0.0, 0.269),
     'L0_ffn_b2': (0.0, 0.1),
     'L1_gnn_b1': (0.0, 0.8),
     'L1_gnn_b2': (0.0, 0.8),
     'L1_gnn_fusion_w': (1.0, 0.6),
     'L1_ffn_gate_b': (0.0, 0.307),
     'L1_ffn_b1': (0.0, 0.8),
     'L1_ffn_b2': (0.0, 0.279),
     'L1_ffn_gamma': (1.0, 0.2),
     'L1_ffn_beta': (0.0, 0.1)}
    factors = {'L0_ffn_att_src': 4.136, 'L0_ffn_att_dst': 6.283, 'L1_ffn_w1': 4.079, 'L1_ffn_w2': 3.197}
    for name, (base, spread) in spreads.items():
        noise = np.random.default_rng([zlib.crc32(name.encode()), seed]).standard_normal(out[name].shape)
        drawn = base * np.exp(spread * noise) if base else spread * noise
        out[name] = jnp.asarray(drawn.astype(out[name].dtype))
    for name, factor in factors.items():
        out[name] = (out[name] * factor).astype(out[name].dtype)
    return out
```

```python
import concourse.bass as bass
import concourse.mybir as mybir
from contextlib import ExitStack

F32 = mybir.dt.float32
BF16 = mybir.dt.bfloat16
I32 = mybir.dt.int32
ALU = mybir.AluOpType
ACT = mybir.ActivationFunctionType
AX = mybir.AxisListType

P = 128
B = 128
F = 128
M = P * B
class Buffers:
    pass


U = 4
STEPS = B // U
EPS = 1e-5
HEADS = 4
GE = 4
HE = HEADS * GE
ROW = HEADS + HE
E2 = 16
HID = 256
G = 16
NEG = -9000000000000000.0
GROUPS = [list(range(25)), [0, 1, 2, 3, 4, 5, 6, 7, 8], [0, 9, 10, 11, 12, 13, 14], [6, 7, 8, 12, 13, 14],
          [3, 4, 5, 9, 10, 11]]
NG = len(GROUPS)
NN = len(GROUPS[0])
GUN = NG * U * NN


def const_layout():
    at, out = 0, {}
    for name, width in (("ident", P), ("upto", P), ("iota", P), ("part", 1), ("trash", 1),
                        ("member", NG), ("groups", NG * NN), ("eye", NN), ("ones", P)):
        out[name] = (at, width)
        at += width
    return out, at


def cast_col(t, b):
    return t[:, bass.ds(b, 1), :].rearrange("p a b -> p (a b)")


def layernorm_stage(nc, K, src, dst, parts, tag):
    with ExitStack() as ctx:
        stats = ctx.enter_context(nc.sbuf_tensor(tag + "_stats", [P, U, 6], F32))
        mv4 = ctx.enter_context(nc.sbuf_tensor(tag + "_mv4", [P, U, 2], F32))
        mv = ctx.enter_context(nc.sbuf_tensor(tag + "_mv", [P, B, 2], F32))
        std = ctx.enter_context(nc.sbuf_tensor(tag + "_std", [P, B], F32))
        stats_done = ctx.enter_context(nc.semaphore(tag + "_stats_done"))
        std_done = ctx.enter_context(nc.semaphore(tag + "_std_done"))
        block = ctx.enter_context(nc.Block())

        @block.vector
        def _(dve):
            with dve.Fori(0, STEPS) as i:
                for u in range(U):
                    dve.bn_stats(out=stats[0:parts, u, :], in_=cast_col(src[0:parts], U * i + u))
                dve.drain()
                for u in range(U):
                    dve.bn_aggr(out=mv4[0:parts, u, :], in_=stats[0:parts, u, :])
                dve.drain()
                dve.tensor_copy(mv[0:parts, bass.ds(U * i, U), :], mv4[0:parts])
            dve.drain().then_inc(stats_done, 1)
            dve.wait_ge(std_done, 1)
            dve.reciprocal(std[0:parts, :], std[0:parts, :])
            dve.drain()
            with dve.Fori(0, STEPS) as i:
                for u in range(U):
                    b = U * i + u
                    dve.tensor_scalar(cast_col(dst[0:parts], b), cast_col(src[0:parts], b),
                                      mv[0:parts, bass.ds(b, 1), 0], std[0:parts, bass.ds(b, 1)],
                                      ALU.subtract, ALU.mult)
            dve.drain()

        @block.scalar
        def _(act):
            act.wait_ge(stats_done, 1)
            act.activation(std[0:parts, :], mv[0:parts, :, 1], ACT.Sqrt,
                           bias=K.eps[0:parts, :]).then_inc(std_done, 1)


def load_stage(nc, K, D):
    with ExitStack() as ctx:
        loaded = ctx.enter_context(nc.semaphore("loaded"))
        mask_loaded = ctx.enter_context(nc.semaphore("mask_loaded"))
        block = ctx.enter_context(nc.Block())
        parts = 8
        nb = B // parts

        @block.sync
        def _(sp):
            for c in range(parts):
                sp.dma_start(K.X[:, c * nb:(c + 1) * nb, :],
                             D["x"][c * nb:(c + 1) * nb].rearrange("b n f -> n b f")).then_inc(loaded, 16)
            sp.wait_ge(loaded, 16 * (parts + 1))

        @block.scalar
        def _(act):
            act.dma_start(K.const[:, :], D["consts"]).then_inc(loaded, 16)
            for c in range(parts):
                act.dma_start(K.Y[:, c * nb:(c + 1) * nb, :],
                              D["adj"][c * nb:(c + 1) * nb].rearrange("b n f -> n b f")).then_inc(mask_loaded, 16)

        @block.gpsimd
        def _(pool):
            pool.memset(K.eps[:, :], EPS)
            pool.wait_ge(mask_loaded, 16 * parts)
            for c in range(parts):
                part = K.Y[:, c * nb:(c + 1) * nb, :].rearrange("p b m -> p (b m)")
                pool.tensor_scalar(part, part, 0.0, NEG, ALU.is_le, ALU.mult)


def dense_attention_stage(nc, K, D):
    with ExitStack() as ctx:
        sb = lambda n, s, d=F32: ctx.enter_context(nc.sbuf_tensor("ga_" + n, s, d))
        pb = lambda n, s: ctx.enter_context(nc.psum_tensor("ga_" + n, s, F32))
        sem = lambda n: ctx.enter_context(nc.semaphore("ga_" + n))
        stats, mv = sb("stats", [P, U, 6]), sb("mv", [P, U, 2])
        mvall, std = sb("mvall", [P, B, 2]), sb("std", [P, B])
        W, WT, a2 = sb("W", [P, F]), sb("WT", [P, F]), sb("a2", [P, 2])
        Wa, Wa1, Wa2 = sb("Wa", [P, 2]), sb("Wa1", [P, P]), sb("Wa2", [P, P])
        xn, xnT, Wh = sb("xn", [P, U, F]), sb("xnT", [P, U, P]), sb("Wh", [P, U, F])
        pos, e = sb("pos", [P, U, P]), sb("e", [P, U, P])
        negmax, rowsum, inv = sb("negmax", [P, U]), sb("rowsum", [P, U]), sb("inv", [P, U])
        prob, probT = sb("prob", [P, U, P]), sb("probT", [P, U, P])
        ps_xT, ps_wh, ps_e = pb("ps_xT", [P, U, P]), pb("ps_wh", [P, U, F]), pb("ps_e", [P, U, P])
        ps_pT, ps_out = pb("ps_pT", [P, U, P]), pb("ps_out", [P, U, F])
        (w_loaded, wT_done, wT_copied, wa_done, wa_ready, stats_done, std_done, xn_ready, xT_done, xT_copied,
         wh_done, e_done, wh_copied, pos_ready, max_ready, prob_ready, pT_done, pT_copied, out_done) = [
            sem(n) for n in ("w_loaded", "wT_done", "wT_copied", "wa_done", "wa_ready", "stats_done", "std_done",
                             "xn_ready", "xT_done", "xT_copied", "wh_done", "e_done", "wh_copied", "pos_ready",
                             "max_ready", "prob_ready", "pT_done", "pT_copied", "out_done")]
        block = ctx.enter_context(nc.Block())

        @block.sync
        def _(sp):
            sp.dma_start(W[:, :], D["gnn_W"]).then_inc(w_loaded, 16)
            sp.dma_start(a2[:, :], D["gnn_a"]).then_inc(w_loaded, 16)

        @block.tensor
        def _(pe):
            pe.wait_ge(w_loaded, 32)
            pe.transpose(ps_xT[:, 0, :], W[:, :], K.ident).then_inc(wT_done, 1)
            pe.wait_ge(wT_copied, 1)
            pe.matmul(ps_e[:, 0, 0:2], WT[:, :], a2[:, :], start=True, stop=True).then_inc(wa_done, 1)
            pe.wait_ge(wa_ready, 1)
            with pe.Fori(0, STEPS) as i:
                pe.wait_ge(xn_ready, i + 1)
                for u in range(U):
                    ins = pe.transpose(ps_xT[:, u, :], xn[:, u, :], K.ident)
                ins.then_inc(xT_done, 1)
                pe.wait_ge(xT_copied, i + 1)
                for u in range(U):
                    pe.matmul(ps_e[:, u, :], xnT[:, u, :], Wa1[:, :], start=True, stop=False)
                    ins = pe.matmul(ps_e[:, u, :], Wa2[:, :], xnT[:, u, :], start=False, stop=True)
                ins.then_inc(e_done, 1)
                for u in range(U):
                    ins = pe.matmul(ps_wh[:, u, :], xnT[:, u, :], W[:, :], start=True, stop=True)
                ins.then_inc(wh_done, 1)
                pe.wait_ge(prob_ready, i + 1)
                for u in range(U):
                    ins = pe.transpose(ps_pT[:, u, :], prob[:, u, :], K.ident)
                ins.then_inc(pT_done, 1)
                pe.wait_ge(wh_copied, i + 1)
                pe.wait_ge(pT_copied, i + 1)
                for u in range(U):
                    ins = pe.matmul(ps_out[:, u, :], probT[:, u, :], Wh[:, u, :], start=True, stop=True)
                ins.then_inc(out_done, 1)

        @block.scalar
        def _(act):
            act.wait_ge(stats_done, 1)
            act.activation(std[:, :], mvall[:, :, 1], ACT.Sqrt, bias=K.eps[:, :]).then_inc(std_done, 1)
            act.wait_ge(wT_done, 1)
            act.activation(WT[:, :], ps_xT[:, 0, :], ACT.Copy).then_inc(wT_copied, 1)
            with act.Fori(0, STEPS) as i:
                act.wait_ge(xT_done, i + 1)
                act.activation(xnT[:, :, :], ps_xT[:, :, :], ACT.Copy).then_inc(xT_copied, 1)
                act.wait_ge(e_done, i + 1)
                act.activation(pos[:, :, :], ps_e[:, :, :], ACT.Relu, scale=0.8).then_inc(pos_ready, 1)
                act.wait_ge(wh_done, i + 1)
                act.activation(Wh[:, :, :], ps_wh[:, :, :], ACT.Copy).then_inc(wh_copied, 1)
                act.wait_ge(max_ready, i + 1)
                for u in range(U):
                    ins = act.activation(prob[:, u, :], e[:, u, :], ACT.Exp, bias=negmax[:, u:u + 1],
                                         accum_out=rowsum[:, u:u + 1])
                ins.then_inc(prob_ready, 1)

        @block.vector
        def _(dve):
            with dve.Fori(0, STEPS) as i:
                for u in range(U):
                    dve.bn_stats(out=stats[:, u, :], in_=cast_col(K.X, U * i + u))
                dve.drain()
                for u in range(U):
                    dve.bn_aggr(out=mv[:, u, :], in_=stats[:, u, :])
                dve.drain()
                dve.tensor_copy(mvall[:, bass.ds(U * i, U), :], mv[:, :, :])
            dve.drain().then_inc(stats_done, 1)
            dve.wait_ge(std_done, 1)
            dve.reciprocal(std[:, :], std[:, :])
            dve.wait_ge(wa_done, 1)
            dve.tensor_copy(Wa[:, :], ps_e[:, 0, 0:2])
            dve.drain()
            dve.tensor_copy(Wa1[:, :], Wa[:, 0:1].to_broadcast([P, P]))
            dve.tensor_copy(Wa2[:, :], Wa[:, 1:2].to_broadcast([P, P]))
            dve.drain().then_inc(wa_ready, 1)
            with dve.Fori(0, STEPS) as i:
                for u in range(U):
                    b = U * i + u
                    ins = dve.tensor_scalar(xn[:, u, :], cast_col(K.X, b), mvall[:, bass.ds(b, 1), 0],
                                            std[:, bass.ds(b, 1)], ALU.subtract, ALU.mult)
                ins.then_inc(xn_ready, 1)
                dve.wait_ge(pos_ready, i + 1)
                dve.scalar_tensor_tensor(out=e[:, :, :], in0=ps_e[:, :, :], scalar=0.2, in1=pos[:, :, :],
                                         op0=ALU.mult, op1=ALU.add)
                dve.drain()
                dve.tensor_tensor(e[:, :, :], e[:, :, :], K.Y[:, bass.ds(U * i, U), :], ALU.add)
                dve.drain()
                dve.tensor_reduce(negmax[:, :], e[:, :, :], AX.X, ALU.max, negate=True).then_inc(max_ready, 1)
                dve.wait_ge(pT_done, i + 1)
                dve.tensor_copy(probT[:, :, :], ps_pT[:, :, :]).then_inc(pT_copied, 1)
                dve.wait_ge(prob_ready, i + 1)
                dve.reciprocal(inv[:, :], rowsum[:, :])
                dve.drain()
                dve.wait_ge(out_done, i + 1)
                dve.tensor_tensor(K.Y[:, bass.ds(U * i, U), :], ps_out[:, :, :],
                                  inv[:, :].unsqueeze(2).to_broadcast([P, U, F]), ALU.mult)
            dve.drain()


def gelu_residual_stage(nc, K, D):
    with ExitStack() as ctx:
        sb = lambda n, s, d=F32: ctx.enter_context(nc.sbuf_tensor("gr_" + n, s, d))
        sem = lambda n: ctx.enter_context(nc.semaphore("gr_" + n))
        gamma, beta = sb("gamma", [P, F]), sb("beta", [P, F])
        pre, post = sb("pre", [P, U, F]), sb("post", [P, U, F])
        loaded, pre_ready, post_ready = sem("loaded"), sem("pre_ready"), sem("post_ready")
        block = ctx.enter_context(nc.Block())

        @block.sync
        def _(sp):
            sp.dma_start(gamma[:, :], D["gnn_gamma"].partition_broadcast(P)).then_inc(loaded, 16)
            sp.dma_start(beta[:, :], D["gnn_beta"].partition_broadcast(P)).then_inc(loaded, 16)

        @block.vector
        def _(dve):
            dve.wait_ge(loaded, 32)
            with dve.Fori(0, STEPS) as i:
                dve.tensor_tensor(pre[:, :, :], K.Y[:, bass.ds(U * i, U), :],
                                  gamma[:, :].unsqueeze(1).to_broadcast([P, U, F]), ALU.mult)
                dve.drain()
                dve.tensor_tensor(pre[:, :, :], pre[:, :, :],
                                  beta[:, :].unsqueeze(1).to_broadcast([P, U, F]), ALU.add).then_inc(pre_ready, 1)
                dve.wait_ge(post_ready, i + 1)
                dve.tensor_tensor(K.X[:, bass.ds(U * i, U), :], K.X[:, bass.ds(U * i, U), :], post[:, :, :],
                                  ALU.add)
            dve.drain()

        @block.scalar
        def _(act):
            with act.Fori(0, STEPS) as i:
                act.wait_ge(pre_ready, i + 1)
                act.activation(post[:, :, :], pre[:, :, :], ACT.Gelu).then_inc(post_ready, 1)


def projection_stage(nc, K, D, tag, width, weights, emit):
    with ExitStack() as ctx:
        sb = lambda n, s, d=F32: ctx.enter_context(nc.sbuf_tensor(tag + n, s, d))
        sem = lambda n: ctx.enter_context(nc.semaphore(tag + n))
        y4, yT = sb("y4", [P, U, F]), sb("yT", [P, U, P])
        y4_ready = sem("y4_ready")
        ps_T = ctx.enter_context(nc.psum_tensor(tag + "ps_T", [P, U, P], F32))
        ps_o = ctx.enter_context(nc.psum_tensor(tag + "ps_o", [P, U, width], F32))
        yT_done, yT_copied, proj_done, proj_used = (sem("yT_done"), sem("yT_copied"), sem("proj_done"),
                                                    sem("proj_used"))
        block = ctx.enter_context(nc.Block())

        @block.gpsimd
        def _(pool):
            with pool.Fori(0, STEPS) as i:
                pool.wait_ge(yT_done, i + 1)
                pool.tensor_copy(y4[:, :, :], K.Y[:, bass.ds(U * i, U), :]).then_inc(y4_ready, 1)

        @block.tensor
        def _(pe):
            pe.sem_inc(yT_done, 1)
            with pe.Fori(0, STEPS) as i:
                pe.wait_ge(y4_ready, i + 1)
                for u in range(U):
                    ins = pe.transpose(ps_T[:, u, :], y4[:, u, :], K.ident)
                ins.then_inc(yT_done, 1)
                pe.wait_ge(yT_copied, i + 1)
                pe.wait_ge(proj_used, i + 1)
                for u in range(U):
                    ins = pe.matmul(ps_o[:, u, :], yT[:, u, :], weights, start=True, stop=True)
                ins.then_inc(proj_done, 1)

        @block.scalar
        def _(act):
            with act.Fori(0, STEPS) as i:
                act.wait_ge(yT_done, i + 2)
                act.activation(yT[:, :, :], ps_T[:, :, :], ACT.Copy).then_inc(yT_copied, 1)

        @block.vector
        def _(dve):
            dve.sem_inc(proj_used, 1)
            with dve.Fori(0, STEPS) as i:
                dve.wait_ge(proj_done, i + 1)
                emit(dve, ps_o, i)
                dve.drain().then_inc(proj_used, 1)


def gat_weights_stage(nc, K, D):
    with ExitStack() as ctx:
        att = ctx.enter_context(nc.sbuf_tensor("gw_att", [P, 2, HE], F32))
        tmp = ctx.enter_context(nc.sbuf_tensor("gw_tmp", [P, 2, HE], F32))
        loaded = ctx.enter_context(nc.semaphore("gw_loaded"))
        block = ctx.enter_context(nc.Block())

        @block.sync
        def _(sp):
            sp.dma_start(K.wgat[:, HEADS:HEADS + HE], D["W_gat"]).then_inc(loaded, 16)
            sp.dma_start(att[:, 0, :], D["att_src"].rearrange("h e -> (h e)").partition_broadcast(P)).then_inc(loaded, 16)
            sp.dma_start(att[:, 1, :], D["att_dst"].rearrange("h e -> (h e)").partition_broadcast(P)).then_inc(loaded, 16)

        @block.vector
        def _(dve):
            dve.wait_ge(loaded, 48)
            for t in range(2):
                dve.tensor_tensor(tmp[:, t, :], K.wgat[:, HEADS:HEADS + HE], att[:, t, :], ALU.mult)
            dve.drain()
            for t, at in ((0, 0), (1, HEADS + HE)):
                dve.tensor_reduce(K.wgat[:, at:at + HEADS], tmp[:, t, :].rearrange("p (h e) -> p h e", e=GE), AX.X,
                                  ALU.add)
            dve.drain()


def table_stage(nc, K, D):
    with ExitStack() as ctx:
        top = ctx.enter_context(nc.sbuf_tensor("tb_top", [P, HEADS], F32))
        stored = ctx.enter_context(nc.semaphore("tb_stored"))
        top_ready = ctx.enter_context(nc.semaphore("tb_top_ready"))
        block = ctx.enter_context(nc.Block())

        @block.sync
        def _(sp):
            sp.dma_start(D["table"].rearrange("(n b) c -> n b c", b=B), K.TA[:, :, :]).then_inc(stored, 16)
            sp.wait_ge(stored, 16)

        rest = ctx.enter_context(nc.sbuf_tensor("tb_rest", [P, HEADS, B], F32))

        @block.vector
        def _(dve):
            dve.tensor_copy(rest[:, :, :], K.TAD[:, :, :].rearrange("p b h -> p h b"))
            dve.drain()
            for t in range(3):
                dve.tensor_copy(K.AD[:, t, :, :], rest[:, :, :])
                dve.drain()
                if t < 2:
                    dve.tensor_tensor(rest[:, :, :], rest[:, :, :], K.AD[:, t, :, :], ALU.subtract)
                    dve.drain()
            dve.tensor_reduce(top[:, :], K.TA[:, :, 0:HEADS].rearrange("p b h -> p h b"), AX.X,
                              ALU.max).then_inc(top_ready, 1)

        @block.gpsimd
        def _(pool):
            pool.wait_ge(top_ready, 1)
            pool.partition_all_reduce(K.top[:, :], top[:, :], P, bass.bass_isa.ReduceOp.max)


def edge_index_stage(nc, K, D, C):
    NC = C.chunks
    with ExitStack() as ctx:
        sb = lambda n, s, d=F32: ctx.enter_context(nc.sbuf_tensor("ei_" + n, s, d))
        q = NC // 2
        a, b, c = sb("a", [P, q], I32), sb("b", [P, q], I32), sb("c", [P, q], I32)
        lo, hi = sb("lo", [P, q], BF16), sb("hi", [P, q], BF16)
        loaded, used, rows_ready, stored = (ctx.enter_context(nc.semaphore("ei_" + n)) for n in
                                            ("loaded", "used", "rows_ready", "stored"))
        block = ctx.enter_context(nc.Block())
        row_form = D["dst_row"].rearrange("(p t) e -> p (t e)", p=P)
        lo_form = D["lo_row"].rearrange("(p t) e -> p (t e)", p=P)
        hi_form = D["hi_row"].rearrange("(p t) e -> p (t e)", p=P)

        @block.sync
        def _(sp):
            n = 0
            for h in range(2):
                cols = slice(h * q, (h + 1) * q)
                for src in (D["src_col"], D["dst_col"], row_form):
                    if n:
                        sp.wait_ge(used, n)
                    sp.dma_start(a[:, :], src[:, cols]).then_inc(loaded, 16)
                    n += 1
                sp.wait_ge(rows_ready, h + 1)
                sp.dma_start(lo_form[:, cols], lo[:, :]).then_inc(stored, 16)
                sp.dma_start(hi_form[:, cols], hi[:, :]).then_inc(stored, 16)
                sp.wait_ge(stored, 32 * (h + 1))

        @block.vector
        def _(dve):
            def split():
                dve.tensor_scalar(b[:, :], a[:, :], P - 1, None, ALU.bitwise_and)
                dve.tensor_scalar(c[:, :], a[:, :], 7, None, ALU.logical_shift_right)
                dve.drain().then_inc(used, 1)

            for h in range(2):
                cols = slice(h * q, (h + 1) * q)
                dve.wait_ge(loaded, 16 * (3 * h + 1))
                dve.tensor_scalar(a[:, :], a[:, :], float(M - 1), None, ALU.min)
                dve.drain()
                split()
                dve.scalar_tensor_tensor(out=C.src[:, cols], in0=b[:, :], scalar=float(B), in1=c[:, :],
                                         op0=ALU.mult, op1=ALU.add)
                dve.drain()
                dve.wait_ge(loaded, 16 * (3 * h + 2))
                dve.tensor_copy(C.dst[:, cols], a[:, :])
                split()
                dve.scalar_tensor_tensor(out=C.where[:, cols], in0=b[:, :], scalar=float(B), in1=c[:, :],
                                         op0=ALU.mult, op1=ALU.add)
                dve.drain()
                dve.tensor_scalar(C.where[:, cols], C.where[:, cols], K.trash, None, ALU.subtract)
                dve.drain()
                dve.scalar_tensor_tensor(out=C.where[:, cols], in0=C.dst[:, cols], scalar=float(M),
                                         in1=C.where[:, cols], op0=ALU.is_lt, op1=ALU.mult)
                dve.wait_ge(loaded, 16 * (3 * h + 3))
                split()
                if h:
                    dve.wait_ge(stored, 32 * h)
                dve.tensor_copy(lo[:, :], b[:, :])
                dve.tensor_copy(hi[:, :], c[:, :])
                dve.drain().then_inc(rows_ready, 1)


def at_least(engine, semaphore, value):
    if not isinstance(value, int) or value > 0:
        engine.wait_ge(semaphore, value)


def edge_stage(nc, K, D, C):
    STEPS_E = C.chunks // G
    QUAD = 4
    PAIR = 2
    UNITS = G // QUAD * (HEADS // PAIR)
    RING = 3
    with ExitStack() as ctx:
        sb = lambda n, s, d=F32: ctx.enter_context(nc.sbuf_tensor("ed_" + n, s, d))
        pb = lambda n, s: ctx.enter_context(nc.psum_tensor("ed_" + n, s, F32))
        sem = lambda n: ctx.enter_context(nc.semaphore("ed_" + n))
        pair = lambda n, s, d=F32: [sb(f"{n}{k}", s, d) for k in range(2)]
        src_idx, put_idx = pair("src_idx", [P, G], I32), pair("put_idx", [P, G], I32)
        dcol, wcol = pair("dcol", [P, G]), pair("wcol", [P, G])
        drow = pair("drow", [P, G, P], I32)
        lrow, hrow = pair("lrow", [P, G, P], BF16), pair("hrow", [P, G, P], BF16)
        same = pair("same", [P, G, P])
        hot, hot_b = sb("hot", [P, G, P], BF16), sb("hot_b", [P, G, P], BF16)
        prod = pair("prod", [P, PAIR, QUAD * P])
        got, put = pair("got", [P, G, ROW]), pair("put", [P, G, ROW])
        adst, rank = pair("adst", [P, G, HEADS]), pair("rank", [P, G])
        msg = sb("msg", [P, G, ROW])
        sc, bound, diff = sb("sc", [P, G, HEADS]), sb("bound", [P, G, HEADS]), sb("diff", [P, G, HEADS])
        ZP = 5
        zeros = sb("zeros", [P, (M + P) * ROW // P // ZP])
        ps_a = [pb(f"ps_a{k}", [P, PAIR, QUAD * P]) for k in range(RING)]
        ps_d, ps_m = pb("ps_d", [P, G, HEADS]), pb("ps_m", [P, G, ROW])
        rows_in, gathered, added = ([sem(f"{n}{k}") for k in range(2)] for n in ("rows_in", "gathered", "added"))
        (zero_ready, zeroed, cols_ready, hot_ready, same_ready, sel_done, prod_ready, sum_done, adst_ready, diff_ready,
         w_ready, msg_ready, merged, put_ready, put_idx_ready, gathers, landed) = [
            sem(n) for n in ("zero_ready", "zeroed", "cols_ready", "hot_ready", "same_ready", "sel_done",
                             "prod_ready", "sum_done", "adst_ready", "diff_ready", "w_ready", "msg_ready", "merged",
                             "put_ready", "put_idx_ready", "gathers", "landed")]
        block = ctx.enter_context(nc.Block())
        unit_at = lambda n: (n // (HEADS // PAIR) * QUAD, n % (HEADS // PAIR) * PAIR)

        @block.sync
        def _(sp):
            def rows(it, u):
                for to, of in ((drow, D["dst_row"]), (lrow, D["lo_row"]), (hrow, D["hi_row"])):
                    sp.dma_start(to[u][:, :, :],
                                 of[bass.ds(it * G, G), :].partition_broadcast(P)).then_inc(rows_in[u], 16)

            rows(0, 0)
            rows(1, 1)
            sp.wait_ge(zero_ready, 1)
            for k in range(G):
                pieces = D["acc"][k].rearrange("(p t) c -> p (t c)", p=P)
                n = zeros.shape[1]
                for j in range(ZP):
                    sp.dma_start(pieces[:, j * n:(j + 1) * n], zeros[:, :]).then_inc(zeroed, 16)
            with sp.Fori(0, STEPS_E // 2 - 1) as i:
                for u in range(2):
                    sp.wait_ge(same_ready, 2 * i + u + 1)
                    rows(2 * i + u + 2, u)

        @block.gpsimd
        def _(pool):
            def gather(it, u):
                pool.wait_ge(cols_ready, it + 1)
                pool.sem_inc(gathers, 1)
                for c in range(G):
                    pool.indirect_dma_start(got[u][:, c, :], None, D["table"],
                                            bass.IndirectOffsetOnAxis(ap=src_idx[u][:, c:c + 1], axis=0)
                                            ).then_inc(gathered[u], 16)

            def scatter(it, u, k):
                pool.wait_ge(put_ready, it + 2)
                pool.wait_ge(put_idx_ready, it + 1)
                if k is not None:
                    pool.wait_ge(added[1 - u], 16 * G * (k + u))
                pool.sem_inc(landed, 1)
                for c in range(G):
                    pool.indirect_dma_start(D["acc"][c],
                                            bass.IndirectOffsetOnAxis(ap=put_idx[u][:, c:c + 1], axis=0),
                                            put[u][:, c, :], None, compute_op=ALU.add).then_inc(added[u], 16)

            pool.memset(zeros[:, :], 0.0).then_inc(zero_ready, 1)
            pool.sem_inc(landed, 1)
            gather(0, 0)
            gather(1, 1)
            pool.wait_ge(zeroed, 16 * G * ZP)
            scatter(0, 0, None)
            with pool.Fori(0, STEPS_E // 2 - 1) as i:
                gather(2 * i + 2, 0)
                scatter(2 * i + 1, 1, i)
                gather(2 * i + 3, 1)
                scatter(2 * i + 2, 0, i + 1)
            scatter(STEPS_E - 1, 1, STEPS_E // 2 - 1)
            pool.wait_ge(added[1], 16 * G * STEPS_E // 2)

        @block.scalar
        def _(act):
            def columns(it, u):
                cols = bass.ds(it * G, G)
                act.activation(src_idx[u][:, :], C.src[:, cols], ACT.Copy)
                act.activation(dcol[u][:, :], C.dst[:, cols], ACT.Copy)
                act.activation(wcol[u][:, :], C.where[:, cols], ACT.Copy)
                act.drain().then_inc(cols_ready, 1)

            def keep_adst(it, u):
                act.wait_ge(sum_done, UNITS * (it + 1))
                act.activation(adst[u][:, :, :], ps_d[:, :, :], ACT.Copy).then_inc(adst_ready, 1)

            def weigh(it, u):
                act.wait_ge(diff_ready, it + 1)
                act.activation(msg[:, :, 0:HEADS], diff[:, :, :], ACT.Exp).then_inc(w_ready, 1)
                act.wait_ge(merged, it + 1)
                act.wait_ge(landed, it + 1)
                act.activation(put[u][:, :, :], ps_m[:, :, :], ACT.Copy).then_inc(put_ready, 1)

            act.sem_inc(put_ready, 1)
            columns(0, 0)
            columns(1, 1)
            keep_adst(0, 0)
            with act.Fori(0, STEPS_E // 2 - 1) as i:
                for u in range(2):
                    keep_adst(2 * i + u + 1, 1 - u)
                    weigh(2 * i + u, u)
                    columns(2 * i + u + 2, u)
            keep_adst(STEPS_E - 1, 1)
            weigh(STEPS_E - 2, 0)
            weigh(STEPS_E - 1, 1)

        @block.tensor
        def _(pe):
            def total(it, n):
                at_least(pe, prod_ready, UNITS * it + n + 1)
                c0, h0 = unit_at(n)
                for j in range(PAIR):
                    for c in range(QUAD):
                        ins = pe.matmul(ps_d[:, c0 + c, h0 + j:h0 + j + 1], prod[n % 2][:, j, c * P:(c + 1) * P],
                                        K.ones[:, 0:1], start=True, stop=True)
                ins.then_inc(sum_done, 1)

            def select(it, u):
                at_least(pe, adst_ready, it)
                pe.wait_ge(hot_ready, it + 1)
                for n in range(UNITS):
                    at_least(pe, prod_ready, UNITS * it + n - RING + 1)
                    c0, h0 = unit_at(n)
                    for j in range(PAIR):
                        for t in range(3):
                            ins = pe.matmul(ps_a[n % RING][:, j, :], K.AD[:, t, h0 + j, :],
                                            hot[:, c0:c0 + QUAD, :].rearrange("p c e -> p (c e)"), start=t == 0,
                                            stop=t == 2)
                    ins.then_inc(sel_done, 1)
                    if n:
                        total(it, n - 1)
                total(it, UNITS - 1)

            def merge(it, u):
                pe.wait_ge(msg_ready, it + 1)
                pe.wait_ge(put_ready, it + 1)
                for c in range(G):
                    ins = pe.matmul(ps_m[:, c, :], same[u][:, c, :], msg[:, c, :], start=True, stop=True)
                ins.then_inc(merged, 1)

            select(0, 0)
            with pe.Fori(0, STEPS_E // 2 - 1) as i:
                select(2 * i + 1, 1)
                merge(2 * i, 0)
                select(2 * i + 2, 0)
                merge(2 * i + 1, 1)
            select(STEPS_E - 1, 1)
            merge(STEPS_E - 2, 0)
            merge(STEPS_E - 1, 1)

        @block.vector
        def _(dve):
            def prepare(it, u, k):
                dve.wait_ge(rows_in[u], 48 * (k + 1))
                at_least(dve, sel_done, UNITS * it)
                dve.tensor_scalar(hot[:, :, :], lrow[u][:, :, :], K.part, None, ALU.is_equal)
                dve.tensor_scalar(hot_b[:, :, :], hrow[u][:, :, :], K.part, None, ALU.is_equal)
                dve.drain().then_inc(hot_ready, 1)
                dve.wait_ge(cols_ready, it + 1)
                at_least(dve, merged, it - 1)
                for n in range(UNITS):
                    for c in range(2 * n, 2 * n + 2):
                        ins = dve.scalar_tensor_tensor(out=same[u][:, c, :], in0=drow[u][:, c, :],
                                                       scalar=dcol[u][:, c:c + 1], in1=K.upto, op0=ALU.is_equal,
                                                       op1=ALU.mult, accum_out=rank[u][:, c:c + 1])
                    dve.wait_ge(sel_done, UNITS * it + n + 1)
                    at_least(dve, sum_done, UNITS * it + n - 1)
                    c0, _ = unit_at(n)
                    dve.tensor_tensor(prod[n % 2][:, :, :], ps_a[n % RING][:, :, :],
                                      hot_b[:, c0:c0 + QUAD, :].rearrange("p c e -> p (c e)").unsqueeze(1)
                                      .to_broadcast([P, PAIR, QUAD * P]), ALU.mult).then_inc(prod_ready, 1)
                dve.drain().then_inc(same_ready, 1)

            def weigh(it, u, k):
                dve.scalar_tensor_tensor(out=rank[u][:, :], in0=rank[u][:, :], scalar=1.0, in1=wcol[u][:, :],
                                         op0=ALU.is_equal, op1=ALU.mult)
                top = K.top[:, :].unsqueeze(1).to_broadcast([P, G, HEADS])
                dve.wait_ge(adst_ready, it + 1)
                dve.tensor_tensor(bound[:, :, :], adst[u][:, :, :], top, ALU.add)
                dve.wait_ge(gathered[u], 16 * G * (k + 1))
                dve.tensor_tensor(sc[:, :, :], adst[u][:, :, :], got[u][:, :, 0:HEADS], ALU.add)
                dve.drain()
                for t in (bound, sc):
                    dve.scalar_tensor_tensor(out=t[:, :, :], in0=t[:, :, :], scalar=0.2, in1=t[:, :, :],
                                             op0=ALU.mult, op1=ALU.max)
                dve.drain()
                dve.tensor_tensor(diff[:, :, :], sc[:, :, :], bound[:, :, :], ALU.subtract).then_inc(diff_ready, 1)
                dve.wait_ge(w_ready, it + 1)
                dve.tensor_tensor(msg[:, :, HEADS:ROW].rearrange("p c (h e) -> p c h e", e=GE),
                                  got[u][:, :, HEADS:ROW].rearrange("p c (h e) -> p c h e", e=GE),
                                  msg[:, :, 0:HEADS].unsqueeze(3).to_broadcast([P, G, HEADS, GE]),
                                  ALU.mult).then_inc(msg_ready, 1)
                dve.wait_ge(landed, it + 1)
                dve.tensor_scalar(put_idx[u][:, :], rank[u][:, :], K.trash, None, ALU.add).then_inc(put_idx_ready, 1)

            prepare(0, 0, 0)
            prepare(1, 1, 0)
            weigh(0, 0, 0)
            with dve.Fori(0, STEPS_E // 2 - 1) as i:
                prepare(2 * i + 2, 0, i + 1)
                weigh(2 * i + 1, 1, i)
                prepare(2 * i + 3, 1, i + 1)
                weigh(2 * i + 2, 0, i + 1)
            weigh(STEPS_E - 1, 1, STEPS_E // 2 - 1)
            dve.drain()


def combine_stage(nc, K, D):
    with ExitStack() as ctx:
        sb = lambda n, s, d=F32: ctx.enter_context(nc.sbuf_tensor("cb_" + n, s, d))
        sem = lambda n: ctx.enter_context(nc.semaphore("cb_" + n))
        total = sb("total", [P, B, ROW])
        part = [sb(f"part{k}", [P, B, ROW]) for k in range(2)]
        e, bound = sb("e", [P, B, HEADS]), sb("bound", [P, B, HEADS])
        w = sb("w", [P, B, HEADS])
        agg, sq = sb("agg", [P, B, HE]), sb("sq", [P, B, HE])
        mean, var = sb("mean", [P, B]), sb("var", [P, B])
        rows = sb("rows", [P, 3, HE])
        in_sem, summed, diff_ready, w_ready, var_ready, std_ready = [
            sem(n) for n in ("in", "summed", "diff_ready", "w_ready", "var_ready", "std_ready")]
        block = ctx.enter_context(nc.Block())
        rows_in = sem("rows_in")

        @block.sync
        def _(sp):
            for t, v in enumerate((D["b_gat"], D["ln_gamma"], D["ln_beta"])):
                sp.dma_start(rows[:, t, :], v.partition_broadcast(P)).then_inc(rows_in, 16)
            for k in range(G):
                if k >= 2:
                    sp.wait_ge(summed, k - 1)
                sp.dma_start(part[k % 2][:, :, :].rearrange("p b c -> p (b c)"),
                             D["acc"][k][0:M, :].rearrange("(n b) c -> n (b c)", b=B)).then_inc(in_sem, 16)
                sp.wait_ge(in_sem, 16 * (k + 1))

        @block.scalar
        def _(act):
            act.wait_ge(diff_ready, 1)
            act.activation(w[:, :, :], e[:, :, :], ACT.Exp).then_inc(w_ready, 1)
            act.wait_ge(var_ready, 1)
            act.activation(var[:, :], var[:, :], ACT.Sqrt, bias=K.eps[:, :], scale=1.0 / HE).then_inc(std_ready, 1)

        @block.vector
        def _(dve):
            def step(ins):
                dve.drain()
            h_view = lambda t: t.rearrange("p b (h e) -> p b h e", e=GE)
            over_e = lambda t: t.unsqueeze(3).to_broadcast([P, B, HEADS, GE])
            over_c = lambda t: t.unsqueeze(2).to_broadcast([P, B, HE])
            over_b = lambda t, n: t.unsqueeze(1).to_broadcast([P, B, n])
            dve.tensor_tensor(bound[:, :, :], K.TAD[:, :, :], over_b(K.top[:, :], HEADS), ALU.add)
            step(dve.tensor_tensor(e[:, :, :], K.TAD[:, :, :], K.TA[:, :, 0:HEADS], ALU.add))
            for t in (bound, e):
                step(dve.scalar_tensor_tensor(out=t[:, :, :], in0=t[:, :, :], scalar=0.2, in1=t[:, :, :],
                                              op0=ALU.mult, op1=ALU.max))
            dve.tensor_tensor(e[:, :, :], e[:, :, :], bound[:, :, :], ALU.subtract).then_inc(diff_ready, 1)
            dve.wait_ge(w_ready, 1)
            dve.tensor_copy(total[:, :, 0:HEADS], w[:, :, :])
            step(dve.tensor_tensor(h_view(total[:, :, HEADS:ROW]), h_view(K.TA[:, :, HEADS:ROW]), over_e(w[:, :, :]),
                                   ALU.mult))
            for k in range(G):
                dve.wait_ge(in_sem, 16 * (k + 1))
                dve.tensor_tensor(total[:, :, :], total[:, :, :], part[k % 2][:, :, :], ALU.add)
                dve.drain().then_inc(summed, 1)
            step(dve.tensor_scalar(w[:, :, :], total[:, :, 0:HEADS], 1e-16, None, ALU.add))
            step(dve.reciprocal(w[:, :, :], w[:, :, :]))
            step(dve.tensor_tensor(h_view(agg[:, :, :]), h_view(total[:, :, HEADS:ROW]), over_e(w[:, :, :]),
                                   ALU.mult))
            dve.wait_ge(rows_in, 48)
            step(dve.tensor_tensor(agg[:, :, :], agg[:, :, :], over_b(rows[:, 0, :], HE), ALU.add))
            step(dve.tensor_reduce(mean[:, :], agg[:, :, :], AX.X, ALU.add))
            step(dve.tensor_scalar(mean[:, :], mean[:, :], 1.0 / HE, None, ALU.mult))
            step(dve.tensor_tensor(agg[:, :, :], agg[:, :, :], over_c(mean[:, :]), ALU.subtract))
            step(dve.tensor_tensor(sq[:, :, :], agg[:, :, :], agg[:, :, :], ALU.mult))
            dve.tensor_reduce(var[:, :], sq[:, :, :], AX.X, ALU.add).then_inc(var_ready, 1)
            dve.wait_ge(std_ready, 1)
            step(dve.reciprocal(var[:, :], var[:, :]))
            step(dve.tensor_tensor(agg[:, :, :], agg[:, :, :], over_c(var[:, :]), ALU.mult))
            step(dve.tensor_tensor(agg[:, :, :], agg[:, :, :], over_b(rows[:, 1, :], HE), ALU.mult))
            step(dve.tensor_tensor(agg[:, :, :], agg[:, :, :], over_b(rows[:, 2, :], HE), ALU.add))
            step(dve.tensor_reduce(K.gates4[:, :, :], agg[:, :, :].rearrange("p b (h e) -> p b e h", e=GE), AX.X,
                                   ALU.add))
            step(dve.tensor_scalar(K.gates4[:, :, :], K.gates4[:, :, :], 1.0 / HEADS, None, ALU.mult))


def top2_stage(nc, K, gates, E, tag):
    with ExitStack() as ctx:
        sb = lambda n, s, d=F32: ctx.enter_context(nc.sbuf_tensor(tag + n, s, d))
        key, rest, first = sb("key", [P, B, E]), sb("rest", [P, B, E]), sb("first", [P, B, E])
        m1, m2, k1 = sb("m1", [P, B]), sb("m2", [P, B]), sb("k1", [P, B])
        rev = sb("rev", [P, E])
        gap_ready = ctx.enter_context(nc.semaphore(tag + "gap_ready"))
        exp_ready = ctx.enter_context(nc.semaphore(tag + "exp_ready"))
        block = ctx.enter_context(nc.Block())
        BIG = 1e30

        @block.scalar
        def _(act):
            act.wait_ge(gap_ready, 1)
            act.activation(m2[:, :], m2[:, :], ACT.Exp).then_inc(exp_ready, 1)

        @block.vector
        def _(dve):
            over = lambda t: t[:, :].unsqueeze(2).to_broadcast([P, B, E])

            def pick(scores, top, out):
                dve.tensor_reduce(top[:, :], scores[:, :, :], AX.X, ALU.max)
                dve.drain()
                dve.tensor_tensor(key[:, :, :], scores[:, :, :], over(top), ALU.is_ge)
                dve.drain()
                dve.tensor_tensor(key[:, :, :], key[:, :, :], rev[:, :].unsqueeze(1).to_broadcast([P, B, E]),
                                  ALU.mult)
                dve.drain()
                dve.tensor_reduce(k1[:, :], key[:, :, :], AX.X, ALU.max)
                dve.drain()
                dve.tensor_tensor(out[:, :, :], key[:, :, :], over(k1), ALU.is_equal)
                dve.drain()

            dve.tensor_scalar(rev[:, :], K.iota[:, 0:E], -1.0, float(E), ALU.mult, ALU.add)
            dve.drain()
            pick(gates, m1, first)
            dve.scalar_tensor_tensor(out=rest[:, :, :], in0=first[:, :, :], scalar=-BIG, in1=gates[:, :, :],
                                     op0=ALU.mult, op1=ALU.add)
            dve.drain()
            pick(rest, m2, rest)
            dve.tensor_tensor(m2[:, :], m2[:, :], m1[:, :], ALU.subtract).then_inc(gap_ready, 1)
            dve.wait_ge(exp_ready, 1)
            dve.tensor_scalar(m1[:, :], m2[:, :], 1.0, None, ALU.add)
            dve.drain()
            dve.reciprocal(m1[:, :], m1[:, :])
            dve.drain()
            dve.tensor_tensor(m2[:, :], m2[:, :], m1[:, :], ALU.mult)
            dve.tensor_tensor(first[:, :, :], first[:, :, :], over(m1), ALU.mult)
            dve.drain()
            dve.tensor_tensor(rest[:, :, :], rest[:, :, :], over(m2), ALU.mult)
            dve.drain()
            dve.tensor_tensor(gates[:, :, :], first[:, :, :], rest[:, :, :], ALU.add)
            dve.drain()


def experts_stage(nc, K, gates, E, w1, b1, w2, b2, func, out, tag):
    with ExitStack() as ctx:
        sb = lambda n, s, d=F32: ctx.enter_context(nc.sbuf_tensor(tag + n, s, d))
        pb = lambda n, s: ctx.enter_context(nc.psum_tensor(tag + n, s, F32))
        sem = lambda n: ctx.enter_context(nc.semaphore(tag + n))
        C2 = HID // P
        W1, W2 = sb("W1", [P, E, HID]), sb("W2", [P, E, C2, F])
        B1, B2 = sb("B1", [P, E, C2]), sb("B2", [E, F])
        y4, g4 = sb("y4", [P, U, F]), sb("g4", [P, U, E])
        y4_ready = sem("y4_ready")
        yT, gT = sb("yT", [P, U, P]), sb("gT", [E, U, P])
        hid = [sb(f"hid{k}", [P, C2, U * P]) for k in range(2)]
        ps_T, ps_gT = pb("ps_T", [P, U, P]), pb("ps_gT", [P, U, P])
        ps_h = [[pb(f"ps_h{k}{c}", [P, U * P]) for c in range(C2)] for k in range(2)]
        ps_o = [pb(f"ps_o{k}", [P, U, F]) for k in range(2)]
        (w_in, yT_done, yT_copied, h_done, h_ready, o_done, o_used, b_done, b_used) = [
            sem(n) for n in ("w_in", "yT_done", "yT_copied", "h_done", "h_ready", "o_done", "o_used", "b_done",
                             "b_used")]
        block = ctx.enter_context(nc.Block())

        @block.sync
        def _(sp):
            sp.dma_start(W1[:, :, :], w1.rearrange("e d f -> d e f")).then_inc(w_in, 16)
            for c in range(C2):
                sp.dma_start(W2[:, :, c, :], w2[:, c * P:(c + 1) * P, :].rearrange("e f d -> f e d")
                             ).then_inc(w_in, 16)
            sp.dma_start(B2[:, :], b2).then_inc(w_in, 16)
            sp.dma_start(B1[:, :, :], b1).then_inc(w_in, 16)

        @block.gpsimd
        def _(pool):
            with pool.Fori(0, STEPS) as i:
                pool.wait_ge(yT_done, i + 1)
                pool.tensor_copy(y4[:, :, :], K.Y[:, bass.ds(U * i, U), :])
                pool.tensor_copy(g4[:, :, :], gates[:, bass.ds(U * i, U), :]).then_inc(y4_ready, 1)

        @block.tensor
        def _(pe):
            pe.wait_ge(w_in, 16 * (3 + C2))
            pe.sem_inc(yT_done, 1)
            with pe.Fori(0, STEPS) as i:
                pe.wait_ge(y4_ready, i + 1)
                for u in range(U):
                    pe.transpose(ps_T[:, u, :], y4[:, u, :], K.ident)
                pe.wait_ge(b_used, i + 1)
                for u in range(U):
                    ins = pe.transpose(ps_gT[0:E, u, :], g4[:, u, :], K.ident)
                ins.then_inc(yT_done, 1)
                pe.wait_ge(yT_copied, i + 1)
                for u in range(U):
                    ins = pe.matmul(ps_gT[:, u, :], gT[:, u, :], B2[:, :], start=True, stop=True)
                ins.then_inc(b_done, 1)
                for e in range(E + 1):
                    if e < E:
                        if e >= 2:
                            pe.wait_ge(h_ready, E * i + e - 1)
                        for c in range(C2):
                            ins = pe.matmul(ps_h[e % 2][c][:, :], W1[:, e, c * P:(c + 1) * P],
                                            yT[:, :, :].rearrange("p u n -> p (u n)"), start=True, stop=True)
                        ins.then_inc(h_done, 1)
                    if e > 0:
                        n = E * i + e - 1
                        pe.wait_ge(h_ready, n + 1)
                        pe.wait_ge(o_used, n + 1)
                        for u in range(U):
                            for c in range(C2):
                                ins = pe.matmul(ps_o[(e - 1) % 2][:, u, :], hid[(e - 1) % 2][:, c, u * P:(u + 1) * P],
                                                W2[:, e - 1, c, :], start=c == 0, stop=c == C2 - 1)
                        ins.then_inc(o_done, 1)

        @block.scalar
        def _(act):
            act.wait_ge(w_in, 16 * (3 + C2))
            with act.Fori(0, STEPS) as i:
                act.wait_ge(yT_done, i + 2)
                act.activation(yT[:, :, :], ps_T[:, :, :], ACT.Copy)
                act.activation(gT[:, :, :], ps_gT[0:E, :, :], ACT.Copy)
                act.drain().then_inc(yT_copied, 1)
                for e in range(E):
                    n = E * i + e
                    act.wait_ge(h_done, n + 1)
                    if e >= 2:
                        act.wait_ge(o_done, n - 1)
                    for c in range(C2):
                        ins = act.activation(hid[e % 2][:, c, :], ps_h[e % 2][c][:, :], func,
                                             bias=B1[:, e, c:c + 1])
                    ins.then_inc(h_ready, 1)

        @block.vector
        def _(dve):
            dve.sem_inc(b_used, 1)
            dve.sem_inc(o_used, 2)
            with dve.Fori(0, STEPS) as i:
                dve.wait_ge(b_done, i + 1)
                o = out[:, bass.ds(U * i, U), :]
                dve.tensor_tensor(o, o, ps_gT[:, :, :], ALU.add)
                dve.drain().then_inc(b_used, 1)
                for e in range(E):
                    dve.wait_ge(o_done, E * i + e + 1)
                    for u in range(U):
                        ob = cast_col(out, U * i + u)
                        dve.scalar_tensor_tensor(out=ob, in0=ps_o[e % 2][:, u, :],
                                                 scalar=gates[:, bass.ds(U * i + u, 1), e], in1=ob,
                                                 op0=ALU.mult, op1=ALU.add)
                    dve.drain().then_inc(o_used, 1)


def grouped_gcn_stage(nc, K, D):
    with ExitStack() as ctx:
        sb = lambda n, s, d=F32: ctx.enter_context(nc.sbuf_tensor("gc_" + n, s, d))
        pb = lambda n, s: ctx.enter_context(nc.psum_tensor("gc_" + n, s, F32))
        sem = lambda n: ctx.enter_context(nc.semaphore("gc_" + n))
        C2 = HID // P
        adjn, adjt = sb("adjn", [NN, B, NN]), sb("adjt", [NN, B, NN])
        W1, W2 = sb("W1", [P, NG, HID]), sb("W2", [P, NG, C2, F])
        B1, B2 = sb("B1", [P, NG, C2]), sb("B2", [NN, NG, F])
        fw, fx = sb("fw", [NN, NG]), sb("fx", [NN, 4])
        wm = sb("wm", [NN, NG])
        tmp, an = sb("tmp", [NN, 2, U, NN]), sb("an", [NN, NG, U, NN])
        WIDE = 64
        at_pad = sb("at", [NN, GUN + WIDE - NN])
        at = at_pad[:, 0:GUN].rearrange("p (g u n) -> p g u n", g=NG, u=U)
        ND = GUN + NG * U
        deg, guard, root = sb("deg", [NN, ND]), sb("guard", [NN, ND]), sb("root", [NN, ND])
        y4 = sb("y4", [NN, U, F])
        y4_ready = sem("y4_ready")
        ax, hid = sb("ax", [P, GUN]), sb("hid", [P, C2, GUN])
        s2, z = sb("s2", [NN, NG, F]), sb("z", [NN, NG, F])
        fused = sb("fused", [NN, F])
        ps_deg, ps_ax = pb("ps_deg", [WIDE, 512]), pb("ps_ax", [P, 512])
        ps_h = [pb(f"ps_h{c}", [P, 512]) for c in range(C2)]
        ps_s, ps_o = pb("ps_s", [NN, 8, F]), pb("ps_o", [WIDE, 8, F])
        (w_in, adj_in, fw_shift, fw_exp, at_ready, deg_done, guard_ready, root_ready, norm_ready, ax_done, ax_ready,
         h_done, h_ready, s_done, s_ready, o_done, o_used, fexp) = [
            sem(n) for n in ("w_in", "adj_in", "fw_shift", "fw_exp", "at_ready", "deg_done", "guard_ready",
                             "root_ready", "norm_ready", "ax_done", "ax_ready", "h_done", "h_ready", "s_done",
                             "s_ready", "o_done", "o_used", "fexp")]
        block = ctx.enter_context(nc.Block())
        gun = "p g u n -> p (g u n)"
        mask = K.groups[0:NN, :].rearrange("p (g n) -> p g n", g=NG)
        by_gun = lambda t: t[:, 0:GUN].rearrange("p (g u n) -> p g u n", g=NG, u=U)

        @block.sync
        def _(sp):
            sp.dma_start(adjn[:, :, :], D["adj"][:, 0:NN, 0:NN].rearrange("b n m -> n b m")).then_inc(adj_in, 16)
            sp.dma_start(adjt[:, :, :], D["adjT"][:, 0:NN, 0:NN].rearrange("b m n -> m b n")).then_inc(adj_in, 16)
            sp.dma_start(fw[:, :], D["fusion_w"].partition_broadcast(NN)).then_inc(adj_in, 16)
            sp.dma_start(W1[:, :, :], D["gW1"].rearrange("e d f -> d e f")).then_inc(w_in, 16)
            for c in range(C2):
                sp.dma_start(W2[:, :, c, :], D["gW2"][:, c * P:(c + 1) * P, :].rearrange("e f d -> f e d")
                             ).then_inc(w_in, 16)
            sp.dma_start(B2[:, :, :], D["gb2"].partition_broadcast(NN)).then_inc(w_in, 16)
            sp.dma_start(B1[:, :, :], D["gb1"]).then_inc(w_in, 16)

        @block.vector
        def _(dve):
            dve.wait_ge(adj_in, 48)
            dve.tensor_reduce(fx[:, 0:1], fw[:, :], AX.X, ALU.max, negate=True).then_inc(fw_shift, 1)
            dve.wait_ge(fw_exp, 1)
            dve.reciprocal(fx[:, 2:3], fx[:, 1:2])
            dve.drain()
            dve.scalar_tensor_tensor(out=wm[:, :], in0=fw[:, :], scalar=fx[:, 2:3], in1=K.member[0:NN, :],
                                     op0=ALU.mult, op1=ALU.mult)
            dve.drain()
            dve.wait_ge(w_in, 16 * (3 + C2))
            dve.sem_inc(o_used, 1)
            dve.memset(at_pad[:, GUN:GUN + WIDE - NN], 0.0)
            with dve.Fori(0, STEPS) as i:
                eye = K.eye[0:NN, :].unsqueeze(1).to_broadcast([NN, U, NN])
                for t, a in enumerate((adjt, adjn)):
                    dve.tensor_tensor(tmp[:, t], a[:, bass.ds(U * i, U), :], eye, ALU.add)
                dve.drain()
                for g in range(NG):
                    mg = mask[:, g, :].unsqueeze(1).to_broadcast([NN, U, NN])
                    dve.tensor_tensor(at[:, g], tmp[:, 0], mg, ALU.mult)
                    dve.tensor_tensor(an[:, g], tmp[:, 1], mg, ALU.mult)
                dve.drain().then_inc(at_ready, 1)
                dve.tensor_reduce(deg[:, GUN:ND], an[:, :, :, :].rearrange("p g u n -> p (g u) n"), AX.X, ALU.add)
                dve.wait_ge(deg_done, i + 1)
                dve.tensor_copy(deg[:, 0:GUN], ps_deg[0:NN, 0:GUN])
                dve.drain()
                dve.scalar_tensor_tensor(out=guard[:, :], in0=deg[:, :], scalar=0.0, in1=deg[:, :],
                                         op0=ALU.is_equal, op1=ALU.add)
                dve.drain().then_inc(guard_ready, 1)
                dve.wait_ge(root_ready, i + 1)
                dve.reciprocal(root[:, :], root[:, :])
                dve.drain()
                dve.scalar_tensor_tensor(out=root[:, :], in0=deg[:, :], scalar=0.0, in1=root[:, :],
                                         op0=ALU.not_equal, op1=ALU.mult)
                dve.drain()
                flat = at[:, :, :, :].rearrange(gun)
                dve.tensor_tensor(flat, flat, root[:, 0:GUN], ALU.mult)
                dve.drain()
                fl3 = at[:, :, :, :].rearrange("p g u n -> p (g u) n")
                dve.tensor_tensor(fl3, fl3, root[:, GUN:ND].unsqueeze(2).to_broadcast([NN, NG * U, NN]), ALU.mult)
                dve.drain().then_inc(norm_ready, 1)
                for u in range(U):
                    dve.wait_ge(o_done, U * i + u + 1)
                    dve.tensor_tensor(z[:, :, :], ps_o[0:NN, 0:NG, :], B2[:, :, :], ALU.add)
                    dve.drain().then_inc(o_used, 1)
                    dve.scalar_tensor_tensor(out=z[:, :, :], in0=z[:, :, :], scalar=0.0,
                                             in1=wm[:, :].unsqueeze(2).to_broadcast([NN, NG, F]),
                                             op0=ALU.max, op1=ALU.mult)
                    dve.drain()
                    dve.tensor_reduce(fused[:, :], z[:, :, :].rearrange("p g f -> p f g"), AX.X, ALU.add)
                    dve.drain()
                    xb = cast_col(K.X[0:NN], U * i + u)
                    dve.tensor_tensor(xb, xb, fused[:, :], ALU.add)
            dve.drain()

        @block.scalar
        def _(act):
            act.wait_ge(fw_shift, 1)
            act.activation(fw[:, :], fw[:, :], ACT.Exp, bias=fx[:, 0:1], accum_out=fx[:, 1:2])
            act.drain().then_inc(fw_exp, 1)
            act.wait_ge(w_in, 16 * (3 + C2))
            with act.Fori(0, STEPS) as i:
                act.wait_ge(guard_ready, i + 1)
                act.activation(root[:, :], guard[:, :], ACT.Sqrt).then_inc(root_ready, 1)
                act.wait_ge(ax_done, i + 2)
                act.activation(ax[:, :], ps_ax[:, 0:GUN], ACT.Copy).then_inc(ax_ready, 1)
                act.wait_ge(h_done, i + 1)
                for g in range(NG):
                    cols = slice(g * U * NN, (g + 1) * U * NN)
                    for c in range(C2):
                        ins = act.activation(hid[:, c, cols], ps_h[c][:, cols], ACT.Relu, bias=B1[:, g, c:c + 1])
                ins.then_inc(h_ready, 1)
                for u in range(U):
                    act.wait_ge(s_done, U * i + u + 1)
                    act.activation(s2[:, :, :], ps_s[:, 0:NG, :], ACT.Copy).then_inc(s_ready, 1)

        @block.gpsimd
        def _(pool):
            with pool.Fori(0, STEPS) as i:
                pool.wait_ge(ax_done, i + 1)
                pool.tensor_copy(y4[:, :, :], K.Y[0:NN, bass.ds(U * i, U), :]).then_inc(y4_ready, 1)

        @block.tensor
        def _(pe):
            pe.wait_ge(w_in, 16 * (3 + C2))
            pe.sem_inc(ax_done, 1)
            with pe.Fori(0, STEPS) as i:
                pe.wait_ge(at_ready, i + 1)
                pe.matmul(ps_deg[:, 0:GUN], K.ones[0:NN, 0:WIDE], at[:, :, :, :].rearrange(gun), start=True,
                          stop=True).then_inc(deg_done, 1)
                pe.wait_ge(norm_ready, i + 1)
                pe.wait_ge(y4_ready, i + 1)
                for u in range(U):
                    ins = pe.matmul(by_gun(ps_ax)[:, :, u, :], y4[:, u, :], at[:, :, u, :],
                                    start=True, stop=True)
                ins.then_inc(ax_done, 1)
                pe.wait_ge(ax_ready, i + 1)
                for g in range(NG):
                    cols = slice(g * U * NN, (g + 1) * U * NN)
                    for c in range(C2):
                        ins = pe.matmul(ps_h[c][:, cols], W1[:, g, c * P:(c + 1) * P], ax[:, cols], start=True,
                                        stop=True)
                ins.then_inc(h_done, 1)
                pe.wait_ge(h_ready, i + 1)
                for u in range(U):
                    for g in range(NG):
                        for c in range(C2):
                            ins = pe.matmul(ps_s[:, g, :], hid[:, c, (g * U + u) * NN:(g * U + u + 1) * NN],
                                            W2[:, g, c, :], start=c == 0, stop=c == C2 - 1)
                    ins.then_inc(s_done, 1)
                    pe.wait_ge(s_ready, U * i + u + 1)
                    pe.wait_ge(o_used, U * i + u + 1)
                    for g in range(NG):
                        ins = pe.matmul(ps_o[:, g, :], at_pad[:, (g * U + u) * NN:(g * U + u) * NN + WIDE], s2[:, g, :], start=True, stop=True)
                    ins.then_inc(o_done, 1)


def output_stage(nc, K, D):
    with ExitStack() as ctx:
        gb = ctx.enter_context(nc.sbuf_tensor("of_gb", [P, 2, F], F32))
        loaded = ctx.enter_context(nc.semaphore("of_loaded"))
        ready = ctx.enter_context(nc.semaphore("of_ready"))
        stored = ctx.enter_context(nc.semaphore("of_stored"))
        block = ctx.enter_context(nc.Block())
        parts = 8
        nb = B // parts

        @block.sync
        def _(sp):
            sp.dma_start(gb[:, 0, :], D["f_gamma"].partition_broadcast(P)).then_inc(loaded, 16)
            sp.dma_start(gb[:, 1, :], D["f_beta"].partition_broadcast(P)).then_inc(loaded, 16)
            for c in range(parts):
                sp.wait_ge(ready, c + 1)
                sp.dma_start(D["out"][c * nb:(c + 1) * nb].rearrange("b n f -> n b f"),
                             K.X[:, c * nb:(c + 1) * nb, :]).then_inc(stored, 16)
            sp.wait_ge(stored, 16 * parts)

        @block.vector
        def _(dve):
            dve.wait_ge(loaded, 32)
            for c in range(parts):
                y, x = K.Y[:, c * nb:(c + 1) * nb, :], K.X[:, c * nb:(c + 1) * nb, :]
                over = lambda t: gb[:, t, :].unsqueeze(1).to_broadcast([P, nb, F])
                dve.tensor_tensor(y, y, over(0), ALU.mult)
                dve.tensor_tensor(x, x, over(1), ALU.add)
                dve.drain()
                dve.tensor_tensor(x, x, y, ALU.add)
                dve.drain().then_inc(ready, 1)


def store_x(nc, K, D):
    with ExitStack() as ctx:
        stored = ctx.enter_context(nc.semaphore("sx_stored"))
        block = ctx.enter_context(nc.Block())

        @block.sync
        def _(sp):
            sp.dma_start(D["out"].rearrange("b n f -> n b f"), K.X[:, :, :]).then_inc(stored, 16)
            sp.wait_ge(stored, 16)


def build(nc, D, upto=9, skip_to=0):
    with ExitStack() as ctx:
        sb = lambda n, s, d=F32: ctx.enter_context(nc.sbuf_tensor(n, s, d))
        K = Buffers()
        K.X = sb("X", [P, B, F])
        layout, width = const_layout()
        K.const = sb("const", [P, width])
        view = {name: K.const[:, at:at + n] for name, (at, n) in layout.items()}
        K.ident, K.upto, K.iota, K.part, K.trash = (view[n] for n in ("ident", "upto", "iota", "part", "trash"))
        K.member, K.groups, K.eye, K.ones = (view[n] for n in ("member", "groups", "eye", "ones"))
        K.eps = sb("eps", [P, 1])
        K.gates4 = sb("gates4", [P, B, GE])
        D["table"] = nc.dram_tensor("source_table", [M, ROW], F32, kind="Internal").ap()
        D["acc"] = [nc.dram_tensor(f"accumulator{k}", [M + P, ROW], F32, kind="Internal").ap() for k in range(G)]
        D["hi_row"] = nc.dram_tensor("hi_row", list(D["dst_row"].shape), BF16, kind="Internal").ap()
        D["lo_row"] = nc.dram_tensor("lo_row", list(D["dst_row"].shape), BF16, kind="Internal").ap()
        with ExitStack() as gat:
            gb = lambda n, s, d=F32: gat.enter_context(nc.sbuf_tensor(n, s, d))
            K.wgat, K.top = gb("wgat", [P, ROW + HEADS]), gb("top", [P, HEADS])
            K.TA, K.AD, K.TAD = gb("TA", [P, B, ROW]), gb("AD", [P, 3, HEADS, B], BF16), gb("TAD", [P, B, HEADS])
            with nc.sbuf_tensor("Y", [P, B, F], F32) as K.Y:
                load_stage(nc, K, D)
                if skip_to < 1:
                    dense_attention_stage(nc, K, D)
                    layernorm_stage(nc, K, K.Y, K.Y, P, "l1")
                    gelu_residual_stage(nc, K, D)
                if upto == 1:
                    return store_x(nc, K, D)
                if skip_to < 2:
                    layernorm_stage(nc, K, K.X, K.Y, P, "l2")
                    gat_weights_stage(nc, K, D)

                    def keep(dve, ps, i):
                        dve.tensor_copy(K.TA[:, bass.ds(U * i, U), :], ps[:, :, 0:ROW])
                        dve.tensor_copy(K.TAD[:, bass.ds(U * i, U), :], ps[:, :, ROW:ROW + HEADS])

                    projection_stage(nc, K, D, "pa_", ROW + HEADS, K.wgat[:, :], keep)
                    table_stage(nc, K, D)
            if skip_to < 2:
                with ExitStack() as edges:
                    eb = lambda n, d=F32: edges.enter_context(nc.sbuf_tensor(n, [P, D["dst_col"].shape[1]], d))
                    C = Buffers()
                    C.src, C.dst, C.where = eb("e_src", I32), eb("e_dst"), eb("e_where")
                    C.chunks = D["dst_col"].shape[1]
                    edge_index_stage(nc, K, D, C)
                    edge_stage(nc, K, D, C)
                combine_stage(nc, K, D)
        K.Y = sb("Y2", [P, B, F])
        if skip_to < 2:
            top2_stage(nc, K, K.gates4, GE, "t4_")
            layernorm_stage(nc, K, K.X, K.Y, P, "l3")
            experts_stage(nc, K, K.gates4, GE, D["W1"], D["b1"], D["W2"], D["b2"], ACT.Gelu, K.X, "x4_")
        if upto == 2:
            return store_x(nc, K, D)
        if skip_to < 3:
            layernorm_stage(nc, K, K.X, K.Y, NN, "l4")
            grouped_gcn_stage(nc, K, D)
        if upto == 3:
            return store_x(nc, K, D)
        layernorm_stage(nc, K, K.X, K.Y, P, "l5")
        with ExitStack() as moe:
            gates = moe.enter_context(nc.sbuf_tensor("gates16", [P, B, E2], F32))
            gw = moe.enter_context(nc.sbuf_tensor("gate_w", [P, E2], F32))
            gbias = moe.enter_context(nc.sbuf_tensor("gate_b", [P, E2], F32))
            with nc.semaphore("gate_loaded") as gate_loaded, nc.Block() as block:
                @block.sync
                def _(sp):
                    sp.dma_start(gw[:, :], D["gate_w"]).then_inc(gate_loaded, 16)
                    sp.dma_start(gbias[:, :], D["gate_b"].partition_broadcast(P)).then_inc(gate_loaded, 16)
                    sp.wait_ge(gate_loaded, 32)

            def keep_scores(dve, ps, i):
                dve.tensor_tensor(gates[:, bass.ds(U * i, U), :], ps[:, :, :],
                                  gbias[:, :].unsqueeze(1).to_broadcast([P, U, E2]), ALU.add)

            projection_stage(nc, K, D, "pg_", E2, gw[:, :], keep_scores)
            top2_stage(nc, K, gates, E2, "t16_")
            experts_stage(nc, K, gates, E2, D["fw1"], D["fb1"], D["fw2"], D["fb2"], ACT.Relu, K.Y, "x16_")
        layernorm_stage(nc, K, K.Y, K.Y, P, "l6")
        output_stage(nc, K, D)


NAMES = {"x": "x", "adj": "adj", "gnn_W": "L0_gnn_W", "gnn_a": "L0_gnn_a", "gnn_gamma": "L0_gnn_gamma",
         "gnn_beta": "L0_gnn_beta", "W_gat": "L0_ffn_W_gat", "att_src": "L0_ffn_att_src",
         "att_dst": "L0_ffn_att_dst", "b_gat": "L0_ffn_b_gat", "ln_gamma": "L0_ffn_ln_gamma",
         "ln_beta": "L0_ffn_ln_beta", "W1": "L0_ffn_W1", "b1": "L0_ffn_b1", "W2": "L0_ffn_W2", "b2": "L0_ffn_b2",
         "gW1": "L1_gnn_W1", "gb1": "L1_gnn_b1", "gW2": "L1_gnn_W2", "gb2": "L1_gnn_b2",
         "fusion_w": "L1_gnn_fusion_w", "gate_w": "L1_ffn_gate_w", "gate_b": "L1_ffn_gate_b", "fw1": "L1_ffn_w1",
         "fb1": "L1_ffn_b1", "fw2": "L1_ffn_w2", "fb2": "L1_ffn_b2", "f_gamma": "L1_ffn_gamma",
         "f_beta": "L1_ffn_beta"}


def host_arrays(inputs):
    import numpy as np
    arrays = {k: np.ascontiguousarray(inputs[v]) for k, v in NAMES.items()}
    arrays["adjT"] = np.ascontiguousarray(np.transpose(arrays["adj"], (0, 2, 1)))
    arrays["gnn_a"] = np.ascontiguousarray(arrays["gnn_a"].reshape(2, F).T)
    for name in ("b1", "gb1", "fb1"):
        b = arrays[name]
        arrays[name] = np.ascontiguousarray(b.reshape(len(b), HID // P, P).transpose(2, 0, 1))
    edges = np.ascontiguousarray(inputs["L0_ffn_edge_index"])
    arrays["src_col"] = np.ascontiguousarray(edges[0].reshape(P, -1))
    arrays["dst_col"] = np.ascontiguousarray(edges[1].reshape(P, -1))
    arrays["dst_row"] = np.ascontiguousarray(edges[1].reshape(P, -1).T)
    layout, width = const_layout()
    consts = np.zeros((P, width), np.float32)
    put = lambda name, v: consts.__setitem__((slice(0, len(v)), slice(layout[name][0], sum(layout[name]))), v)
    put("ident", np.eye(P))
    put("upto", np.tril(np.ones((P, P))))
    put("iota", np.tile(np.arange(P), (P, 1)))
    put("part", np.arange(P)[:, None])
    put("trash", M + np.arange(P)[:, None])
    member = np.array([[float(n in g) for g in GROUPS] for n in range(NN)])
    put("member", member)
    put("groups", np.einsum("mg,ng->mgn", member, member).reshape(NN, NG * NN))
    put("eye", np.eye(NN))
    put("ones", np.ones((P, P)))
    arrays["consts"] = consts
    return arrays


def kernel(**inputs):
    import numpy as np
    import concourse.bacc as bacc
    from concourse.bass_utils import run_bass_kernel_spmd

    nc = bacc.Bacc("TRN2", target_bir_lowering=False, num_devices=1)
    arrays = host_arrays(inputs)
    D = {name: nc.dram_tensor(f"in_{name}", a.shape, mybir.dt.from_np(a.dtype), kind="ExternalInput").ap()
         for name, a in arrays.items()}
    D["out"] = nc.dram_tensor("out_x", [B, P, F], F32, kind="ExternalOutput").ap()
    build(nc, D)
    result = run_bass_kernel_spmd(nc, [{f"in_{k}": a for k, a in arrays.items()}], core_ids=[0])
    return np.asarray(result.results[0]["out_x"])
```

```python
import concourse.bass as bass
import concourse.mybir as mybir
from contextlib import ExitStack

F32 = mybir.dt.float32
BF16 = mybir.dt.bfloat16
I32 = mybir.dt.int32
ALU = mybir.AluOpType
ACT = mybir.ActivationFunctionType
AX = mybir.AxisListType

P = 128
B = 128
F = 128
M = P * B
class Buffers:
    pass


U = 4
STEPS = B // U
EPS = 1e-5
HEADS = 4
GE = 4
HE = HEADS * GE
ROW = HEADS + HE
E2 = 16
HID = 256
G = 16
NEG = -9000000000000000.0
GROUPS = [list(range(25)), [0, 1, 2, 3, 4, 5, 6, 7, 8], [0, 9, 10, 11, 12, 13, 14], [6, 7, 8, 12, 13, 14],
          [3, 4, 5, 9, 10, 11]]
NG = len(GROUPS)
NN = len(GROUPS[0])
GUN = NG * U * NN


def const_layout():
    at, out = 0, {}
    for name, width in (("ident", P), ("upto", P), ("iota", P), ("part", 1), ("trash", 1),
                        ("member", NG), ("groups", NG * NN), ("eye", NN), ("ones", P)):
        out[name] = (at, width)
        at += width
    return out, at


def cast_col(t, b):
    return t[:, bass.ds(b, 1), :].rearrange("p a b -> p (a b)")


def layernorm_stage(nc, K, src, dst, parts, tag):
    with ExitStack() as ctx:
        stats = ctx.enter_context(nc.sbuf_tensor(tag + "_stats", [P, U, 6], F32))
        mv4 = ctx.enter_context(nc.sbuf_tensor(tag + "_mv4", [P, U, 2], F32))
        mv = ctx.enter_context(nc.sbuf_tensor(tag + "_mv", [P, B, 2], F32))
        std = ctx.enter_context(nc.sbuf_tensor(tag + "_std", [P, B], F32))
        stats_done = ctx.enter_context(nc.semaphore(tag + "_stats_done"))
        std_done = ctx.enter_context(nc.semaphore(tag + "_std_done"))
        block = ctx.enter_context(nc.Block())

        @block.vector
        def _(dve):
            with dve.Fori(0, STEPS) as i:
                for u in range(U):
                    dve.bn_stats(out=stats[0:parts, u, :], in_=cast_col(src[0:parts], U * i + u))
                dve.drain()
                for u in range(U):
                    dve.bn_aggr(out=mv4[0:parts, u, :], in_=stats[0:parts, u, :])
                dve.drain()
                dve.tensor_copy(mv[0:parts, bass.ds(U * i, U), :], mv4[0:parts])
            dve.drain().then_inc(stats_done, 1)
            dve.wait_ge(std_done, 1)
            dve.reciprocal(std[0:parts, :], std[0:parts, :])
            dve.drain()
            with dve.Fori(0, STEPS) as i:
                for u in range(U):
                    b = U * i + u
                    dve.tensor_scalar(cast_col(dst[0:parts], b), cast_col(src[0:parts], b),
                                      mv[0:parts, bass.ds(b, 1), 0], std[0:parts, bass.ds(b, 1)],
                                      ALU.subtract, ALU.mult)
            dve.drain()

        @block.scalar
        def _(act):
            act.wait_ge(stats_done, 1)
            act.activation(std[0:parts, :], mv[0:parts, :, 1], ACT.Sqrt,
                           bias=K.eps[0:parts, :]).then_inc(std_done, 1)


def load_stage(nc, K, D):
    with ExitStack() as ctx:
        loaded = ctx.enter_context(nc.semaphore("loaded"))
        mask_loaded = ctx.enter_context(nc.semaphore("mask_loaded"))
        block = ctx.enter_context(nc.Block())
        parts = 8
        nb = B // parts

        @block.sync
        def _(sp):
            for c in range(parts):
                sp.dma_start(K.X[:, c * nb:(c + 1) * nb, :],
                             D["x"][c * nb:(c + 1) * nb].rearrange("b n f -> n b f")).then_inc(loaded, 16)
            sp.wait_ge(loaded, 16 * (parts + 1))

        @block.scalar
        def _(act):
            act.dma_start(K.const[:, :], D["consts"]).then_inc(loaded, 16)
            for c in range(parts):
                act.dma_start(K.Y[:, c * nb:(c + 1) * nb, :],
                              D["adj"][c * nb:(c + 1) * nb].rearrange("b n f -> n b f")).then_inc(mask_loaded, 16)

        @block.gpsimd
        def _(pool):
            pool.memset(K.eps[:, :], EPS)
            pool.wait_ge(mask_loaded, 16 * parts)
            for c in range(parts):
                part = K.Y[:, c * nb:(c + 1) * nb, :].rearrange("p b m -> p (b m)")
                pool.tensor_scalar(part, part, 0.0, NEG, ALU.is_le, ALU.mult)


def dense_attention_stage(nc, K, D):
    with ExitStack() as ctx:
        sb = lambda n, s, d=F32: ctx.enter_context(nc.sbuf_tensor("ga_" + n, s, d))
        pb = lambda n, s: ctx.enter_context(nc.psum_tensor("ga_" + n, s, F32))
        sem = lambda n: ctx.enter_context(nc.semaphore("ga_" + n))
        stats, mv = sb("stats", [P, U, 6]), sb("mv", [P, U, 2])
        mvall, std = sb("mvall", [P, B, 2]), sb("std", [P, B])
        W, WT, a2 = sb("W", [P, F]), sb("WT", [P, F]), sb("a2", [P, 2])
        Wa, Wa1, Wa2 = sb("Wa", [P, 2]), sb("Wa1", [P, P]), sb("Wa2", [P, P])
        xn, xnT, Wh = sb("xn", [P, U, F]), sb("xnT", [P, U, P]), sb("Wh", [P, U, F])
        pos, e = sb("pos", [P, U, P]), sb("e", [P, U, P])
        negmax, rowsum, inv = sb("negmax", [P, U]), sb("rowsum", [P, U]), sb("inv", [P, U])
        prob, probT = sb("prob", [P, U, P]), sb("probT", [P, U, P])
        ps_xT, ps_wh, ps_e = pb("ps_xT", [P, U, P]), pb("ps_wh", [P, U, F]), pb("ps_e", [P, U, P])
        ps_pT, ps_out = pb("ps_pT", [P, U, P]), pb("ps_out", [P, U, F])
        (w_loaded, wT_done, wT_copied, wa_done, wa_ready, stats_done, std_done, xn_ready, xT_done, xT_copied,
         wh_done, e_done, wh_copied, pos_ready, max_ready, prob_ready, pT_done, pT_copied, out_done) = [
            sem(n) for n in ("w_loaded", "wT_done", "wT_copied", "wa_done", "wa_ready", "stats_done", "std_done",
                             "xn_ready", "xT_done", "xT_copied", "wh_done", "e_done", "wh_copied", "pos_ready",
                             "max_ready", "prob_ready", "pT_done", "pT_copied", "out_done")]
        block = ctx.enter_context(nc.Block())

        @block.sync
        def _(sp):
            sp.dma_start(W[:, :], D["gnn_W"]).then_inc(w_loaded, 16)
            sp.dma_start(a2[:, :], D["gnn_a"]).then_inc(w_loaded, 16)

        @block.tensor
        def _(pe):
            pe.wait_ge(w_loaded, 32)
            pe.transpose(ps_xT[:, 0, :], W[:, :], K.ident).then_inc(wT_done, 1)
            pe.wait_ge(wT_copied, 1)
            pe.matmul(ps_e[:, 0, 0:2], WT[:, :], a2[:, :], start=True, stop=True).then_inc(wa_done, 1)
            pe.wait_ge(wa_ready, 1)
            with pe.Fori(0, STEPS) as i:
                pe.wait_ge(xn_ready, i + 1)
                for u in range(U):
                    ins = pe.transpose(ps_xT[:, u, :], xn[:, u, :], K.ident)
                ins.then_inc(xT_done, 1)
                pe.wait_ge(xT_copied, i + 1)
                for u in range(U):
                    pe.matmul(ps_e[:, u, :], xnT[:, u, :], Wa1[:, :], start=True, stop=False)
                    ins = pe.matmul(ps_e[:, u, :], Wa2[:, :], xnT[:, u, :], start=False, stop=True)
                ins.then_inc(e_done, 1)
                for u in range(U):
                    ins = pe.matmul(ps_wh[:, u, :], xnT[:, u, :], W[:, :], start=True, stop=True)
                ins.then_inc(wh_done, 1)
                pe.wait_ge(prob_ready, i + 1)
                for u in range(U):
                    ins = pe.transpose(ps_pT[:, u, :], prob[:, u, :], K.ident)
                ins.then_inc(pT_done, 1)
                pe.wait_ge(wh_copied, i + 1)
                pe.wait_ge(pT_copied, i + 1)
                for u in range(U):
                    ins = pe.matmul(ps_out[:, u, :], probT[:, u, :], Wh[:, u, :], start=True, stop=True)
                ins.then_inc(out_done, 1)

        @block.scalar
        def _(act):
            act.wait_ge(stats_done, 1)
            act.activation(std[:, :], mvall[:, :, 1], ACT.Sqrt, bias=K.eps[:, :]).then_inc(std_done, 1)
            act.wait_ge(wT_done, 1)
            act.activation(WT[:, :], ps_xT[:, 0, :], ACT.Copy).then_inc(wT_copied, 1)
            with act.Fori(0, STEPS) as i:
                act.wait_ge(xT_done, i + 1)
                act.activation(xnT[:, :, :], ps_xT[:, :, :], ACT.Copy).then_inc(xT_copied, 1)
                act.wait_ge(e_done, i + 1)
                act.activation(pos[:, :, :], ps_e[:, :, :], ACT.Relu, scale=0.8).then_inc(pos_ready, 1)
                act.wait_ge(wh_done, i + 1)
                act.activation(Wh[:, :, :], ps_wh[:, :, :], ACT.Copy).then_inc(wh_copied, 1)
                act.wait_ge(max_ready, i + 1)
                for u in range(U):
                    ins = act.activation(prob[:, u, :], e[:, u, :], ACT.Exp, bias=negmax[:, u:u + 1],
                                         accum_out=rowsum[:, u:u + 1])
                ins.then_inc(prob_ready, 1)

        @block.vector
        def _(dve):
            with dve.Fori(0, STEPS) as i:
                for u in range(U):
                    dve.bn_stats(out=stats[:, u, :], in_=cast_col(K.X, U * i + u))
                dve.drain()
                for u in range(U):
                    dve.bn_aggr(out=mv[:, u, :], in_=stats[:, u, :])
                dve.drain()
                dve.tensor_copy(mvall[:, bass.ds(U * i, U), :], mv[:, :, :])
            dve.drain().then_inc(stats_done, 1)
            dve.wait_ge(std_done, 1)
            dve.reciprocal(std[:, :], std[:, :])
            dve.wait_ge(wa_done, 1)
            dve.tensor_copy(Wa[:, :], ps_e[:, 0, 0:2])
            dve.drain()
            dve.tensor_copy(Wa1[:, :], Wa[:, 0:1].to_broadcast([P, P]))
            dve.tensor_copy(Wa2[:, :], Wa[:, 1:2].to_broadcast([P, P]))
            dve.drain().then_inc(wa_ready, 1)
            with dve.Fori(0, STEPS) as i:
                for u in range(U):
                    b = U * i + u
                    ins = dve.tensor_scalar(xn[:, u, :], cast_col(K.X, b), mvall[:, bass.ds(b, 1), 0],
                                            std[:, bass.ds(b, 1)], ALU.subtract, ALU.mult)
                ins.then_inc(xn_ready, 1)
                dve.wait_ge(pos_ready, i + 1)
                dve.scalar_tensor_tensor(out=e[:, :, :], in0=ps_e[:, :, :], scalar=0.2, in1=pos[:, :, :],
                                         op0=ALU.mult, op1=ALU.add)
                dve.drain()
                dve.tensor_tensor(e[:, :, :], e[:, :, :], K.Y[:, bass.ds(U * i, U), :], ALU.add)
                dve.drain()
                dve.tensor_reduce(negmax[:, :], e[:, :, :], AX.X, ALU.max, negate=True).then_inc(max_ready, 1)
                dve.wait_ge(pT_done, i + 1)
                dve.tensor_copy(probT[:, :, :], ps_pT[:, :, :]).then_inc(pT_copied, 1)
                dve.wait_ge(prob_ready, i + 1)
                dve.reciprocal(inv[:, :], rowsum[:, :])
                dve.drain()
                dve.wait_ge(out_done, i + 1)
                dve.tensor_tensor(K.Y[:, bass.ds(U * i, U), :], ps_out[:, :, :],
                                  inv[:, :].unsqueeze(2).to_broadcast([P, U, F]), ALU.mult)
            dve.drain()


def gelu_residual_stage(nc, K, D):
    with ExitStack() as ctx:
        sb = lambda n, s, d=F32: ctx.enter_context(nc.sbuf_tensor("gr_" + n, s, d))
        sem = lambda n: ctx.enter_context(nc.semaphore("gr_" + n))
        gamma, beta = sb("gamma", [P, F]), sb("beta", [P, F])
        pre, post = sb("pre", [P, U, F]), sb("post", [P, U, F])
        loaded, pre_ready, post_ready = sem("loaded"), sem("pre_ready"), sem("post_ready")
        block = ctx.enter_context(nc.Block())

        @block.sync
        def _(sp):
            sp.dma_start(gamma[:, :], D["gnn_gamma"].partition_broadcast(P)).then_inc(loaded, 16)
            sp.dma_start(beta[:, :], D["gnn_beta"].partition_broadcast(P)).then_inc(loaded, 16)

        @block.vector
        def _(dve):
            dve.wait_ge(loaded, 32)
            with dve.Fori(0, STEPS) as i:
                dve.tensor_tensor(pre[:, :, :], K.Y[:, bass.ds(U * i, U), :],
                                  gamma[:, :].unsqueeze(1).to_broadcast([P, U, F]), ALU.mult)
                dve.drain()
                dve.tensor_tensor(pre[:, :, :], pre[:, :, :],
                                  beta[:, :].unsqueeze(1).to_broadcast([P, U, F]), ALU.add).then_inc(pre_ready, 1)
                dve.wait_ge(post_ready, i + 1)
                dve.tensor_tensor(K.X[:, bass.ds(U * i, U), :], K.X[:, bass.ds(U * i, U), :], post[:, :, :],
                                  ALU.add)
            dve.drain()

        @block.scalar
        def _(act):
            with act.Fori(0, STEPS) as i:
                act.wait_ge(pre_ready, i + 1)
                act.activation(post[:, :, :], pre[:, :, :], ACT.Gelu).then_inc(post_ready, 1)


def projection_stage(nc, K, D, tag, width, weights, emit):
    with ExitStack() as ctx:
        sb = lambda n, s, d=F32: ctx.enter_context(nc.sbuf_tensor(tag + n, s, d))
        sem = lambda n: ctx.enter_context(nc.semaphore(tag + n))
        y4, yT = sb("y4", [P, U, F]), sb("yT", [P, U, P])
        y4_ready = sem("y4_ready")
        ps_T = ctx.enter_context(nc.psum_tensor(tag + "ps_T", [P, U, P], F32))
        ps_o = ctx.enter_context(nc.psum_tensor(tag + "ps_o", [P, U, width], F32))
        yT_done, yT_copied, proj_done, proj_used = (sem("yT_done"), sem("yT_copied"), sem("proj_done"),
                                                    sem("proj_used"))
        block = ctx.enter_context(nc.Block())

        @block.gpsimd
        def _(pool):
            with pool.Fori(0, STEPS) as i:
                pool.wait_ge(yT_done, i + 1)
                pool.tensor_copy(y4[:, :, :], K.Y[:, bass.ds(U * i, U), :]).then_inc(y4_ready, 1)

        @block.tensor
        def _(pe):
            pe.sem_inc(yT_done, 1)
            with pe.Fori(0, STEPS) as i:
                pe.wait_ge(y4_ready, i + 1)
                for u in range(U):
                    ins = pe.transpose(ps_T[:, u, :], y4[:, u, :], K.ident)
                ins.then_inc(yT_done, 1)
                pe.wait_ge(yT_copied, i + 1)
                pe.wait_ge(proj_used, i + 1)
                for u in range(U):
                    ins = pe.matmul(ps_o[:, u, :], yT[:, u, :], weights, start=True, stop=True)
                ins.then_inc(proj_done, 1)

        @block.scalar
        def _(act):
            with act.Fori(0, STEPS) as i:
                act.wait_ge(yT_done, i + 2)
                act.activation(yT[:, :, :], ps_T[:, :, :], ACT.Copy).then_inc(yT_copied, 1)

        @block.vector
        def _(dve):
            dve.sem_inc(proj_used, 1)
            with dve.Fori(0, STEPS) as i:
                dve.wait_ge(proj_done, i + 1)
                emit(dve, ps_o, i)
                dve.drain().then_inc(proj_used, 1)


def gat_weights_stage(nc, K, D):
    with ExitStack() as ctx:
        att = ctx.enter_context(nc.sbuf_tensor("gw_att", [P, 2, HE], F32))
        tmp = ctx.enter_context(nc.sbuf_tensor("gw_tmp", [P, 2, HE], F32))
        loaded = ctx.enter_context(nc.semaphore("gw_loaded"))
        block = ctx.enter_context(nc.Block())

        @block.sync
        def _(sp):
            sp.dma_start(K.wgat[:, HEADS:HEADS + HE], D["W_gat"]).then_inc(loaded, 16)
            sp.dma_start(att[:, 0, :], D["att_src"].rearrange("h e -> (h e)").partition_broadcast(P)).then_inc(loaded, 16)
            sp.dma_start(att[:, 1, :], D["att_dst"].rearrange("h e -> (h e)").partition_broadcast(P)).then_inc(loaded, 16)

        @block.vector
        def _(dve):
            dve.wait_ge(loaded, 48)
            for t in range(2):
                dve.tensor_tensor(tmp[:, t, :], K.wgat[:, HEADS:HEADS + HE], att[:, t, :], ALU.mult)
            dve.drain()
            for t, at in ((0, 0), (1, HEADS + HE)):
                dve.tensor_reduce(K.wgat[:, at:at + HEADS], tmp[:, t, :].rearrange("p (h e) -> p h e", e=GE), AX.X,
                                  ALU.add)
            dve.drain()


def table_stage(nc, K, D):
    with ExitStack() as ctx:
        top = ctx.enter_context(nc.sbuf_tensor("tb_top", [P, HEADS], F32))
        stored = ctx.enter_context(nc.semaphore("tb_stored"))
        top_ready = ctx.enter_context(nc.semaphore("tb_top_ready"))
        block = ctx.enter_context(nc.Block())

        @block.sync
        def _(sp):
            sp.dma_start(D["table"].rearrange("(n b) c -> n b c", b=B), K.TA[:, :, :]).then_inc(stored, 16)
            sp.wait_ge(stored, 16)

        rest = ctx.enter_context(nc.sbuf_tensor("tb_rest", [P, HEADS, B], F32))

        @block.vector
        def _(dve):
            dve.tensor_copy(rest[:, :, :], K.TAD[:, :, :].rearrange("p b h -> p h b"))
            dve.drain()
            for t in range(3):
                dve.tensor_copy(K.AD[:, t, :, :], rest[:, :, :])
                dve.drain()
                if t < 2:
                    dve.tensor_tensor(rest[:, :, :], rest[:, :, :], K.AD[:, t, :, :], ALU.subtract)
                    dve.drain()
            dve.tensor_reduce(top[:, :], K.TA[:, :, 0:HEADS].rearrange("p b h -> p h b"), AX.X,
                              ALU.max).then_inc(top_ready, 1)

        @block.gpsimd
        def _(pool):
            pool.wait_ge(top_ready, 1)
            pool.partition_all_reduce(K.top[:, :], top[:, :], P, bass.bass_isa.ReduceOp.max)


def edge_index_stage(nc, K, D, C):
    NC = C.chunks
    with ExitStack() as ctx:
        sb = lambda n, s, d=F32: ctx.enter_context(nc.sbuf_tensor("ei_" + n, s, d))
        q = NC // 2
        a, b, c = sb("a", [P, q], I32), sb("b", [P, q], I32), sb("c", [P, q], I32)
        lo, hi = sb("lo", [P, q], BF16), sb("hi", [P, q], BF16)
        loaded, used, rows_ready, stored = (ctx.enter_context(nc.semaphore("ei_" + n)) for n in
                                            ("loaded", "used", "rows_ready", "stored"))
        block = ctx.enter_context(nc.Block())
        row_form = D["dst_row"].rearrange("(p t) e -> p (t e)", p=P)
        lo_form = D["lo_row"].rearrange("(p t) e -> p (t e)", p=P)
        hi_form = D["hi_row"].rearrange("(p t) e -> p (t e)", p=P)

        @block.sync
        def _(sp):
            n = 0
            for h in range(2):
                cols = slice(h * q, (h + 1) * q)
                for src in (D["src_col"], D["dst_col"], row_form):
                    if n:
                        sp.wait_ge(used, n)
                    sp.dma_start(a[:, :], src[:, cols]).then_inc(loaded, 16)
                    n += 1
                sp.wait_ge(rows_ready, h + 1)
                sp.dma_start(lo_form[:, cols], lo[:, :]).then_inc(stored, 16)
                sp.dma_start(hi_form[:, cols], hi[:, :]).then_inc(stored, 16)
                sp.wait_ge(stored, 32 * (h + 1))

        @block.vector
        def _(dve):
            def split():
                dve.tensor_scalar(b[:, :], a[:, :], P - 1, None, ALU.bitwise_and)
                dve.tensor_scalar(c[:, :], a[:, :], 7, None, ALU.logical_shift_right)
                dve.drain().then_inc(used, 1)

            for h in range(2):
                cols = slice(h * q, (h + 1) * q)
                dve.wait_ge(loaded, 16 * (3 * h + 1))
                dve.tensor_scalar(a[:, :], a[:, :], float(M - 1), None, ALU.min)
                dve.drain()
                split()
                dve.scalar_tensor_tensor(out=C.src[:, cols], in0=b[:, :], scalar=float(B), in1=c[:, :],
                                         op0=ALU.mult, op1=ALU.add)
                dve.drain()
                dve.wait_ge(loaded, 16 * (3 * h + 2))
                dve.tensor_copy(C.dst[:, cols], a[:, :])
                split()
                dve.scalar_tensor_tensor(out=C.where[:, cols], in0=b[:, :], scalar=float(B), in1=c[:, :],
                                         op0=ALU.mult, op1=ALU.add)
                dve.drain()
                dve.tensor_scalar(C.where[:, cols], C.where[:, cols], K.trash, None, ALU.subtract)
                dve.drain()
                dve.scalar_tensor_tensor(out=C.where[:, cols], in0=C.dst[:, cols], scalar=float(M),
                                         in1=C.where[:, cols], op0=ALU.is_lt, op1=ALU.mult)
                dve.wait_ge(loaded, 16 * (3 * h + 3))
                split()
                if h:
                    dve.wait_ge(stored, 32 * h)
                dve.tensor_copy(lo[:, :], b[:, :])
                dve.tensor_copy(hi[:, :], c[:, :])
                dve.drain().then_inc(rows_ready, 1)


def at_least(engine, semaphore, value):
    if not isinstance(value, int) or value > 0:
        engine.wait_ge(semaphore, value)


def edge_stage(nc, K, D, C):
    STEPS_E = C.chunks // G
    QUAD = 4
    PAIR = 2
    UNITS = G // QUAD * (HEADS // PAIR)
    RING = 3
    with ExitStack() as ctx:
        sb = lambda n, s, d=F32: ctx.enter_context(nc.sbuf_tensor("ed_" + n, s, d))
        pb = lambda n, s: ctx.enter_context(nc.psum_tensor("ed_" + n, s, F32))
        sem = lambda n: ctx.enter_context(nc.semaphore("ed_" + n))
        pair = lambda n, s, d=F32: [sb(f"{n}{k}", s, d) for k in range(2)]
        src_idx, put_idx = pair("src_idx", [P, G], I32), pair("put_idx", [P, G], I32)
        dcol, wcol = pair("dcol", [P, G]), pair("wcol", [P, G])
        drow = pair("drow", [P, G, P], I32)
        lrow, hrow = pair("lrow", [P, G, P], BF16), pair("hrow", [P, G, P], BF16)
        same = pair("same", [P, G, P])
        hot, hot_b = sb("hot", [P, G, P], BF16), sb("hot_b", [P, G, P], BF16)
        prod = pair("prod", [P, PAIR, QUAD * P])
        got, put = pair("got", [P, G, ROW]), pair("put", [P, G, ROW])
        adst, rank = pair("adst", [P, G, HEADS]), pair("rank", [P, G])
        msg = sb("msg", [P, G, ROW])
        sc, bound, diff = sb("sc", [P, G, HEADS]), sb("bound", [P, G, HEADS]), sb("diff", [P, G, HEADS])
        ZP = 5
        zeros = sb("zeros", [P, (M + P) * ROW // P // ZP])
        ps_a = [pb(f"ps_a{k}", [P, PAIR, QUAD * P]) for k in range(RING)]
        ps_d, ps_m = pb("ps_d", [P, G, HEADS]), pb("ps_m", [P, G, ROW])
        rows_in, gathered, added = ([sem(f"{n}{k}") for k in range(2)] for n in ("rows_in", "gathered", "added"))
        (zero_ready, zeroed, cols_ready, hot_ready, same_ready, sel_done, prod_ready, sum_done, adst_ready, diff_ready,
         w_ready, msg_ready, merged, put_ready, put_idx_ready, gathers, landed) = [
            sem(n) for n in ("zero_ready", "zeroed", "cols_ready", "hot_ready", "same_ready", "sel_done",
                             "prod_ready", "sum_done", "adst_ready", "diff_ready", "w_ready", "msg_ready", "merged",
                             "put_ready", "put_idx_ready", "gathers", "landed")]
        block = ctx.enter_context(nc.Block())
        unit_at = lambda n: (n // (HEADS // PAIR) * QUAD, n % (HEADS // PAIR) * PAIR)

        @block.sync
        def _(sp):
            def rows(it, u):
                for to, of in ((drow, D["dst_row"]), (lrow, D["lo_row"]), (hrow, D["hi_row"])):
                    sp.dma_start(to[u][:, :, :],
                                 of[bass.ds(it * G, G), :].partition_broadcast(P)).then_inc(rows_in[u], 16)

            rows(0, 0)
            rows(1, 1)
            sp.wait_ge(zero_ready, 1)
            for k in range(G):
                pieces = D["acc"][k].rearrange("(p t) c -> p (t c)", p=P)
                n = zeros.shape[1]
                for j in range(ZP):
                    sp.dma_start(pieces[:, j * n:(j + 1) * n], zeros[:, :]).then_inc(zeroed, 16)
            with sp.Fori(0, STEPS_E // 2 - 1) as i:
                for u in range(2):
                    sp.wait_ge(same_ready, 2 * i + u + 1)
                    rows(2 * i + u + 2, u)

        @block.gpsimd
        def _(pool):
            def gather(it, u):
                pool.wait_ge(cols_ready, it + 1)
                pool.sem_inc(gathers, 1)
                for c in range(G):
                    pool.indirect_dma_start(got[u][:, c, :], None, D["table"],
                                            bass.IndirectOffsetOnAxis(ap=src_idx[u][:, c:c + 1], axis=0)
                                            ).then_inc(gathered[u], 16)

            def scatter(it, u, k):
                pool.wait_ge(put_ready, it + 2)
                pool.wait_ge(put_idx_ready, it + 1)
                if k is not None:
                    pool.wait_ge(added[1 - u], 16 * G * (k + u))
                pool.sem_inc(landed, 1)
                for c in range(G):
                    pool.indirect_dma_start(D["acc"][c],
                                            bass.IndirectOffsetOnAxis(ap=put_idx[u][:, c:c + 1], axis=0),
                                            put[u][:, c, :], None, compute_op=ALU.add).then_inc(added[u], 16)

            pool.memset(zeros[:, :], 0.0).then_inc(zero_ready, 1)
            pool.sem_inc(landed, 1)
            gather(0, 0)
            gather(1, 1)
            pool.wait_ge(zeroed, 16 * G * ZP)
            scatter(0, 0, None)
            with pool.Fori(0, STEPS_E // 2 - 1) as i:
                gather(2 * i + 2, 0)
                scatter(2 * i + 1, 1, i)
                gather(2 * i + 3, 1)
                scatter(2 * i + 2, 0, i + 1)
            scatter(STEPS_E - 1, 1, STEPS_E // 2 - 1)
            pool.wait_ge(added[1], 16 * G * STEPS_E // 2)

        @block.scalar
        def _(act):
            def columns(it, u):
                cols = bass.ds(it * G, G)
                act.activation(src_idx[u][:, :], C.src[:, cols], ACT.Copy)
                act.activation(dcol[u][:, :], C.dst[:, cols], ACT.Copy)
                act.activation(wcol[u][:, :], C.where[:, cols], ACT.Copy)
                act.drain().then_inc(cols_ready, 1)

            def keep_adst(it, u):
                act.wait_ge(sum_done, UNITS * (it + 1))
                act.activation(adst[u][:, :, :], ps_d[:, :, :], ACT.Copy).then_inc(adst_ready, 1)

            def weigh(it, u):
                act.wait_ge(diff_ready, it + 1)
                act.activation(msg[:, :, 0:HEADS], diff[:, :, :], ACT.Exp).then_inc(w_ready, 1)
                act.wait_ge(merged, it + 1)
                act.wait_ge(landed, it + 1)
                act.activation(put[u][:, :, :], ps_m[:, :, :], ACT.Copy).then_inc(put_ready, 1)

            act.sem_inc(put_ready, 1)
            columns(0, 0)
            columns(1, 1)
            keep_adst(0, 0)
            with act.Fori(0, STEPS_E // 2 - 1) as i:
                for u in range(2):
                    keep_adst(2 * i + u + 1, 1 - u)
                    weigh(2 * i + u, u)
                    columns(2 * i + u + 2, u)
            keep_adst(STEPS_E - 1, 1)
            weigh(STEPS_E - 2, 0)
            weigh(STEPS_E - 1, 1)

        @block.tensor
        def _(pe):
            def total(it, n):
                at_least(pe, prod_ready, UNITS * it + n + 1)
                c0, h0 = unit_at(n)
                for j in range(PAIR):
                    for c in range(QUAD):
                        ins = pe.matmul(ps_d[:, c0 + c, h0 + j:h0 + j + 1], prod[n % 2][:, j, c * P:(c + 1) * P],
                                        K.ones[:, 0:1], start=True, stop=True)
                ins.then_inc(sum_done, 1)

            def select(it, u):
                at_least(pe, adst_ready, it)
                pe.wait_ge(hot_ready, it + 1)
                for n in range(UNITS):
                    at_least(pe, prod_ready, UNITS * it + n - RING + 1)
                    c0, h0 = unit_at(n)
                    for j in range(PAIR):
                        for t in range(3):
                            ins = pe.matmul(ps_a[n % RING][:, j, :], K.AD[:, t, h0 + j, :],
                                            hot[:, c0:c0 + QUAD, :].rearrange("p c e -> p (c e)"), start=t == 0,
                                            stop=t == 2)
                    ins.then_inc(sel_done, 1)
                    if n:
                        total(it, n - 1)
                total(it, UNITS - 1)

            def merge(it, u):
                pe.wait_ge(msg_ready, it + 1)
                pe.wait_ge(put_ready, it + 1)
                for c in range(G):
                    ins = pe.matmul(ps_m[:, c, :], same[u][:, c, :], msg[:, c, :], start=True, stop=True)
                ins.then_inc(merged, 1)

            select(0, 0)
            with pe.Fori(0, STEPS_E // 2 - 1) as i:
                select(2 * i + 1, 1)
                merge(2 * i, 0)
                select(2 * i + 2, 0)
                merge(2 * i + 1, 1)
            select(STEPS_E - 1, 1)
            merge(STEPS_E - 2, 0)
            merge(STEPS_E - 1, 1)

        @block.vector
        def _(dve):
            def prepare(it, u, k):
                dve.wait_ge(rows_in[u], 48 * (k + 1))
                at_least(dve, sel_done, UNITS * it)
                dve.tensor_scalar(hot[:, :, :], lrow[u][:, :, :], K.part, None, ALU.is_equal)
                dve.tensor_scalar(hot_b[:, :, :], hrow[u][:, :, :], K.part, None, ALU.is_equal)
                dve.drain().then_inc(hot_ready, 1)
                dve.wait_ge(cols_ready, it + 1)
                at_least(dve, merged, it - 1)
                for n in range(UNITS):
                    for c in range(2 * n, 2 * n + 2):
                        ins = dve.scalar_tensor_tensor(out=same[u][:, c, :], in0=drow[u][:, c, :],
                                                       scalar=dcol[u][:, c:c + 1], in1=K.upto, op0=ALU.is_equal,
                                                       op1=ALU.mult, accum_out=rank[u][:, c:c + 1])
                    dve.wait_ge(sel_done, UNITS * it + n + 1)
                    at_least(dve, sum_done, UNITS * it + n - 1)
                    c0, _ = unit_at(n)
                    dve.tensor_tensor(prod[n % 2][:, :, :], ps_a[n % RING][:, :, :],
                                      hot_b[:, c0:c0 + QUAD, :].rearrange("p c e -> p (c e)").unsqueeze(1)
                                      .to_broadcast([P, PAIR, QUAD * P]), ALU.mult).then_inc(prod_ready, 1)
                dve.drain().then_inc(same_ready, 1)

            def weigh(it, u, k):
                dve.scalar_tensor_tensor(out=rank[u][:, :], in0=rank[u][:, :], scalar=1.0, in1=wcol[u][:, :],
                                         op0=ALU.is_equal, op1=ALU.mult)
                top = K.top[:, :].unsqueeze(1).to_broadcast([P, G, HEADS])
                dve.wait_ge(adst_ready, it + 1)
                dve.tensor_tensor(bound[:, :, :], adst[u][:, :, :], top, ALU.add)
                dve.wait_ge(gathered[u], 16 * G * (k + 1))
                dve.tensor_tensor(sc[:, :, :], adst[u][:, :, :], got[u][:, :, 0:HEADS], ALU.add)
                dve.drain()
                for t in (bound, sc):
                    dve.scalar_tensor_tensor(out=t[:, :, :], in0=t[:, :, :], scalar=0.2, in1=t[:, :, :],
                                             op0=ALU.mult, op1=ALU.max)
                dve.drain()
                dve.tensor_tensor(diff[:, :, :], sc[:, :, :], bound[:, :, :], ALU.subtract).then_inc(diff_ready, 1)
                dve.wait_ge(w_ready, it + 1)
                dve.tensor_tensor(msg[:, :, HEADS:ROW].rearrange("p c (h e) -> p c h e", e=GE),
                                  got[u][:, :, HEADS:ROW].rearrange("p c (h e) -> p c h e", e=GE),
                                  msg[:, :, 0:HEADS].unsqueeze(3).to_broadcast([P, G, HEADS, GE]),
                                  ALU.mult).then_inc(msg_ready, 1)
                dve.wait_ge(landed, it + 1)
                dve.tensor_scalar(put_idx[u][:, :], rank[u][:, :], K.trash, None, ALU.add).then_inc(put_idx_ready, 1)

            prepare(0, 0, 0)
            prepare(1, 1, 0)
            weigh(0, 0, 0)
            with dve.Fori(0, STEPS_E // 2 - 1) as i:
                prepare(2 * i + 2, 0, i + 1)
                weigh(2 * i + 1, 1, i)
                prepare(2 * i + 3, 1, i + 1)
                weigh(2 * i + 2, 0, i + 1)
            weigh(STEPS_E - 1, 1, STEPS_E // 2 - 1)
            dve.drain()


def combine_stage(nc, K, D):
    with ExitStack() as ctx:
        sb = lambda n, s, d=F32: ctx.enter_context(nc.sbuf_tensor("cb_" + n, s, d))
        sem = lambda n: ctx.enter_context(nc.semaphore("cb_" + n))
        total = sb("total", [P, B, ROW])
        part = [sb(f"part{k}", [P, B, ROW]) for k in range(2)]
        e, bound = sb("e", [P, B, HEADS]), sb("bound", [P, B, HEADS])
        w = sb("w", [P, B, HEADS])
        agg, sq = sb("agg", [P, B, HE]), sb("sq", [P, B, HE])
        mean, var = sb("mean", [P, B]), sb("var", [P, B])
        rows = sb("rows", [P, 3, HE])
        in_sem, summed, diff_ready, w_ready, var_ready, std_ready = [
            sem(n) for n in ("in", "summed", "diff_ready", "w_ready", "var_ready", "std_ready")]
        block = ctx.enter_context(nc.Block())
        rows_in = sem("rows_in")

        @block.sync
        def _(sp):
            for t, v in enumerate((D["b_gat"], D["ln_gamma"], D["ln_beta"])):
                sp.dma_start(rows[:, t, :], v.partition_broadcast(P)).then_inc(rows_in, 16)
            for k in range(G):
                if k >= 2:
                    sp.wait_ge(summed, k - 1)
                sp.dma_start(part[k % 2][:, :, :].rearrange("p b c -> p (b c)"),
                             D["acc"][k][0:M, :].rearrange("(n b) c -> n (b c)", b=B)).then_inc(in_sem, 16)
                sp.wait_ge(in_sem, 16 * (k + 1))

        @block.scalar
        def _(act):
            act.wait_ge(diff_ready, 1)
            act.activation(w[:, :, :], e[:, :, :], ACT.Exp).then_inc(w_ready, 1)
            act.wait_ge(var_ready, 1)
            act.activation(var[:, :], var[:, :], ACT.Sqrt, bias=K.eps[:, :], scale=1.0 / HE).then_inc(std_ready, 1)

        @block.vector
        def _(dve):
            def step(ins):
                dve.drain()
            h_view = lambda t: t.rearrange("p b (h e) -> p b h e", e=GE)
            over_e = lambda t: t.unsqueeze(3).to_broadcast([P, B, HEADS, GE])
            over_c = lambda t: t.unsqueeze(2).to_broadcast([P, B, HE])
            over_b = lambda t, n: t.unsqueeze(1).to_broadcast([P, B, n])
            dve.tensor_tensor(bound[:, :, :], K.TAD[:, :, :], over_b(K.top[:, :], HEADS), ALU.add)
            step(dve.tensor_tensor(e[:, :, :], K.TAD[:, :, :], K.TA[:, :, 0:HEADS], ALU.add))
            for t in (bound, e):
                step(dve.scalar_tensor_tensor(out=t[:, :, :], in0=t[:, :, :], scalar=0.2, in1=t[:, :, :],
                                              op0=ALU.mult, op1=ALU.max))
            dve.tensor_tensor(e[:, :, :], e[:, :, :], bound[:, :, :], ALU.subtract).then_inc(diff_ready, 1)
            dve.wait_ge(w_ready, 1)
            dve.tensor_copy(total[:, :, 0:HEADS], w[:, :, :])
            step(dve.tensor_tensor(h_view(total[:, :, HEADS:ROW]), h_view(K.TA[:, :, HEADS:ROW]), over_e(w[:, :, :]),
                                   ALU.mult))
            for k in range(G):
                dve.wait_ge(in_sem, 16 * (k + 1))
                dve.tensor_tensor(total[:, :, :], total[:, :, :], part[k % 2][:, :, :], ALU.add)
                dve.drain().then_inc(summed, 1)
            step(dve.tensor_scalar(w[:, :, :], total[:, :, 0:HEADS], 1e-16, None, ALU.add))
            step(dve.reciprocal(w[:, :, :], w[:, :, :]))
            step(dve.tensor_tensor(h_view(agg[:, :, :]), h_view(total[:, :, HEADS:ROW]), over_e(w[:, :, :]),
                                   ALU.mult))
            dve.wait_ge(rows_in, 48)
            step(dve.tensor_tensor(agg[:, :, :], agg[:, :, :], over_b(rows[:, 0, :], HE), ALU.add))
            step(dve.tensor_reduce(mean[:, :], agg[:, :, :], AX.X, ALU.add))
            step(dve.tensor_scalar(mean[:, :], mean[:, :], 1.0 / HE, None, ALU.mult))
            step(dve.tensor_tensor(agg[:, :, :], agg[:, :, :], over_c(mean[:, :]), ALU.subtract))
            step(dve.tensor_tensor(sq[:, :, :], agg[:, :, :], agg[:, :, :], ALU.mult))
            dve.tensor_reduce(var[:, :], sq[:, :, :], AX.X, ALU.add).then_inc(var_ready, 1)
            dve.wait_ge(std_ready, 1)
            step(dve.reciprocal(var[:, :], var[:, :]))
            step(dve.tensor_tensor(agg[:, :, :], agg[:, :, :], over_c(var[:, :]), ALU.mult))
            step(dve.tensor_tensor(agg[:, :, :], agg[:, :, :], over_b(rows[:, 1, :], HE), ALU.mult))
            step(dve.tensor_tensor(agg[:, :, :], agg[:, :, :], over_b(rows[:, 2, :], HE), ALU.add))
            step(dve.tensor_reduce(K.gates4[:, :, :], agg[:, :, :].rearrange("p b (h e) -> p b e h", e=GE), AX.X,
                                   ALU.add))
            step(dve.tensor_scalar(K.gates4[:, :, :], K.gates4[:, :, :], 1.0 / HEADS, None, ALU.mult))


def top2(dve, K, gates, E, T, gap_ready, exp_ready, count, nb=B):
    over = lambda t: t[:, :].unsqueeze(2).to_broadcast([P, nb, E])

    def pick(scores, top, out):
        dve.tensor_reduce(top[:, :], scores[:, :, :], AX.X, ALU.max)
        dve.drain()
        dve.tensor_tensor(T.key[:, :, :], scores[:, :, :], over(top), ALU.is_ge)
        dve.drain()
        dve.tensor_tensor(T.key[:, :, :], T.key[:, :, :], T.rev[:, :].unsqueeze(1).to_broadcast([P, nb, E]), ALU.mult)
        dve.drain()
        dve.tensor_reduce(T.k1[:, :], T.key[:, :, :], AX.X, ALU.max)
        dve.drain()
        dve.tensor_tensor(out[:, :, :], T.key[:, :, :], over(T.k1), ALU.is_equal)
        dve.drain()

    pick(gates, T.m1, T.first)
    dve.scalar_tensor_tensor(out=T.rest[:, :, :], in0=T.first[:, :, :], scalar=-1e30, in1=gates[:, :, :],
                             op0=ALU.mult, op1=ALU.add)
    dve.drain()
    pick(T.rest, T.m2, T.rest)
    dve.tensor_tensor(T.m2[:, :], T.m2[:, :], T.m1[:, :], ALU.subtract).then_inc(gap_ready, 1)
    dve.wait_ge(exp_ready, count)
    dve.tensor_scalar(T.m1[:, :], T.m2[:, :], 1.0, None, ALU.add)
    dve.drain()
    dve.reciprocal(T.m1[:, :], T.m1[:, :])
    dve.drain()
    dve.tensor_tensor(T.m2[:, :], T.m2[:, :], T.m1[:, :], ALU.mult)
    dve.tensor_tensor(T.first[:, :, :], T.first[:, :, :], over(T.m1), ALU.mult)
    dve.drain()
    dve.tensor_tensor(T.rest[:, :, :], T.rest[:, :, :], over(T.m2), ALU.mult)
    dve.drain()
    dve.tensor_tensor(gates[:, :, :], T.first[:, :, :], T.rest[:, :, :], ALU.add)


def top2_scratch(sb, E, nb=B):
    T = Buffers()
    T.key, T.rest, T.first = (sb(n, [P, nb, E]) for n in ("key", "rest", "first"))
    T.m1, T.m2, T.k1 = (sb(n, [P, nb]) for n in ("m1", "m2", "k1"))
    T.rev = sb("rev", [P, E])
    return T


def top2_stage(nc, K, gates, E, tag):
    with ExitStack() as ctx:
        T = top2_scratch(lambda n, s: ctx.enter_context(nc.sbuf_tensor(tag + n, s, F32)), E)
        gap_ready = ctx.enter_context(nc.semaphore(tag + "gap_ready"))
        exp_ready = ctx.enter_context(nc.semaphore(tag + "exp_ready"))
        block = ctx.enter_context(nc.Block())

        @block.scalar
        def _(act):
            act.wait_ge(gap_ready, 1)
            act.activation(T.m2[:, :], T.m2[:, :], ACT.Exp).then_inc(exp_ready, 1)

        @block.vector
        def _(dve):
            dve.tensor_scalar(T.rev[:, :], K.iota[:, 0:E], -1.0, float(E), ALU.mult, ALU.add)
            dve.drain()
            top2(dve, K, gates, E, T, gap_ready, exp_ready, 1)
            dve.drain()


def experts_stage(nc, K, D, tag, E, w1, b1, w2, b2, func, gates=None, router=None, affine=None):
    with ExitStack() as ctx:
        sb = lambda n, s, d=F32: ctx.enter_context(nc.sbuf_tensor(tag + n, s, d))
        pb = lambda n, s: ctx.enter_context(nc.psum_tensor(tag + n, s, F32))
        sem = lambda n: ctx.enter_context(nc.semaphore(tag + n))
        pair = lambda n, s: [sb(f"{n}{k}", s) for k in range(2)]
        C2 = HID // P
        W1, W2 = sb("W1", [P, E, HID]), sb("W2", [P, E, C2, F])
        B1, B2 = sb("B1", [P, E, C2]), sb("B2", [E, F])
        y, yT = pair("y", [P, U, F]), pair("yT", [P, U, P])
        g, gT = pair("g", [P, U, E]), pair("gT", [E, U, P])
        stats, mv, std = sb("stats", [P, U, 6]), pair("mv", [P, U, 2]), pair("std", [P, U])
        hid = pair("hid", [P, C2, U * P])
        ps_T, ps_b = pb("ps_T", [P, U, P]), pb("ps_b", [P, U, P])
        ps_h = [[pb(f"ps_h{k}{c}", [P, U * P]) for c in range(C2)] for k in range(2)]
        ps_o = [pb(f"ps_o{k}", [P, U, F]) for k in range(2)]
        (w_in, stats_done, std_ready, y_ready, yT_done, yT_ready, g_ready, gT_done, gT_ready, b_done, b_used,
         h_done, h_ready, o_done, o_used) = [
            sem(n) for n in ("w_in", "stats_done", "std_ready", "y_ready", "yT_done", "yT_ready", "g_ready",
                             "gT_done", "gT_ready", "b_done", "b_used", "h_done", "h_ready", "o_done", "o_used")]
        loads = 3 + C2
        if router:
            gw, gb = sb("gw", [P, E]), sb("gb", [P, E])
            T = top2_scratch(sb, E, U)
            logits_done, gap_ready, exp_ready = sem("logits_done"), sem("gap_ready"), sem("exp_ready")
            loads += 2
        if affine:
            gamma, beta = sb("gamma", [P, F]), sb("beta", [P, F])
            z, fmv, fstd = sb("z", [P, U, F]), sb("fmv", [P, U, 2]), sb("fstd", [P, U])
            fstats_done, fstd_ready, z_ready, out_ready, stored = (
                sem(n) for n in ("fstats_done", "fstd_ready", "z_ready", "out_ready", "stored"))
            loads += 2
        at = [1, 2, 3, 4, 5, 6, 8, 10] if router else [0, 1, 2, 3, 9, 9, 2, 3]
        STATS, NORM, TRANSPOSE, COPY, SCORE, PICK, GATES_T, GATES_COPY = at
        last = STEPS - 1
        block = ctx.enter_context(nc.Block())

        @block.sync
        def _(sp):
            sp.dma_start(W1[:, :, :], w1.rearrange("e d f -> d e f")).then_inc(w_in, 16)
            for c in range(C2):
                sp.dma_start(W2[:, :, c, :], w2[:, c * P:(c + 1) * P, :].rearrange("e f d -> f e d")
                             ).then_inc(w_in, 16)
            sp.dma_start(B2[:, :], b2).then_inc(w_in, 16)
            sp.dma_start(B1[:, :, :], b1).then_inc(w_in, 16)
            if router:
                sp.dma_start(gw[:, :], router[0]).then_inc(w_in, 16)
                sp.dma_start(gb[:, :], router[1].partition_broadcast(P)).then_inc(w_in, 16)
            if affine:
                sp.dma_start(gamma[:, :], affine[0].partition_broadcast(P)).then_inc(w_in, 16)
                sp.dma_start(beta[:, :], affine[1].partition_broadcast(P)).then_inc(w_in, 16)
                sp.sem_inc(stored, 16)
                with sp.Fori(0, STEPS) as i:
                    sp.wait_ge(out_ready, i + 1)
                    sp.dma_start(D["out"][bass.ds(U * i, U)].rearrange("b n f -> n b f"),
                                 z[:, :, :]).then_inc(stored, 16)
                sp.wait_ge(stored, 16 * (STEPS + 1))

        @block.gpsimd
        def _(pool):
            if gates is not None:
                def gates_of(it, k):
                    at_least(pool, gT_done, it - 1)
                    at_least(pool, o_used, E * (it - 1))
                    pool.tensor_copy(g[k][:, :, :], gates[:, bass.ds(U * it, U), :]).then_inc(g_ready, 1)

                gates_of(0, 0)
                gates_of(1, 1)
                with pool.Fori(0, STEPS // 2 - 1) as i:
                    gates_of(2 * i + 2, 0)
                    gates_of(2 * i + 3, 1)
            if affine:
                pool.wait_ge(w_in, 16 * loads)
                over = lambda t: t[:, :].unsqueeze(1).to_broadcast([P, U, F])
                with pool.Fori(0, STEPS) as i:
                    pool.wait_ge(z_ready, i + 1)
                    pool.tensor_tensor(z[:, :, :], z[:, :, :], over(gamma), ALU.mult)
                    pool.drain()
                    pool.tensor_tensor(z[:, :, :], z[:, :, :], over(beta), ALU.add)
                    pool.drain()
                    pool.tensor_tensor(z[:, :, :], z[:, :, :], K.X[:, bass.ds(U * i, U), :],
                                       ALU.add).then_inc(out_ready, 1)

        @block.tensor
        def _(pe):
            def transpose_rows(it, k):
                pe.wait_ge(y_ready, it + 1)
                if router:
                    at_least(pe, g_ready, it)
                for u in range(U):
                    ins = pe.transpose(ps_T[:, u, :], y[k][:, u, :], K.ident)
                ins.then_inc(yT_done, 1)

            def score(it, k):
                pe.wait_ge(yT_ready, it + 1)
                for u in range(U):
                    ins = pe.matmul(ps_T[:, u, 0:E], yT[k][:, u, :], gw[:, :], start=True, stop=True)
                ins.then_inc(logits_done, 1)

            def transpose_gates(it, k):
                pe.wait_ge(g_ready, it + 1)
                at_least(pe, b_used, it)
                for u in range(U):
                    ins = pe.transpose(ps_b[0:E, u, :], g[k][:, u, :], K.ident)
                ins.then_inc(gT_done, 1)

            def second(it, e):
                n = E * it + e
                pe.wait_ge(h_ready, n + 1)
                at_least(pe, o_used, n - 1)
                for u in range(U):
                    for c in range(C2):
                        ins = pe.matmul(ps_o[e % 2][:, u, :], hid[e % 2][:, c, u * P:(u + 1) * P],
                                        W2[:, e % E, c, :], start=c == 0, stop=c == C2 - 1)
                ins.then_inc(o_done, 1)

            def step(it, k, more=True, former=True):
                pe.wait_ge(yT_ready, it + 1)
                pe.wait_ge(gT_ready, it + 1)
                for u in range(U):
                    ins = pe.matmul(ps_b[:, u, :], gT[k][:, u, :], B2[:, :], start=True, stop=True)
                ins.then_inc(b_done, 1)
                for e in range(E):
                    at_least(pe, h_ready, E * it + e - 1)
                    for c in range(C2):
                        ins = pe.matmul(ps_h[e % 2][c][:, :], W1[:, e, c * P:(c + 1) * P],
                                        yT[k][:, :, :].rearrange("p u n -> p (u n)"), start=True, stop=True)
                    ins.then_inc(h_done, 1)
                    if e or former:
                        second(it, e - 1)
                    if more and e == TRANSPOSE:
                        transpose_rows(it + 1, 1 - k)
                    if more and router and e == SCORE:
                        score(it + 1, 1 - k)
                    if more and e == GATES_T:
                        transpose_gates(it + 1, 1 - k)

            pe.wait_ge(w_in, 16 * loads)
            transpose_rows(0, 0)
            if router:
                score(0, 0)
            transpose_gates(0, 0)
            step(0, 0, former=False)
            with pe.Fori(0, STEPS // 2 - 1) as i:
                step(2 * i + 1, 1)
                step(2 * i + 2, 0)
            step(last, 1, more=False)
            second(last, E - 1)

        @block.scalar
        def _(act):
            def root(it, k):
                act.wait_ge(stats_done, it + 1)
                act.activation(std[k][:, :], mv[k][:, :, 1], ACT.Sqrt, bias=K.eps[:, :]).then_inc(std_ready, 1)

            def copy_rows(it, k):
                act.wait_ge(yT_done, it + 1)
                act.activation(yT[k][:, :, :], ps_T[:, :, :], ACT.Copy).then_inc(yT_ready, 1)

            def exponential(it, k):
                act.wait_ge(gap_ready, it + 1)
                act.activation(T.m2[:, :], T.m2[:, :], ACT.Exp).then_inc(exp_ready, 1)

            def copy_gates(it, k):
                act.wait_ge(gT_done, it + 1)
                act.activation(gT[k][:, :, :], ps_b[0:E, :, :], ACT.Copy).then_inc(gT_ready, 1)

            def final_root(it):
                act.wait_ge(fstats_done, it + 1)
                act.activation(fstd[:, :], fmv[:, :, 1], ACT.Sqrt, bias=K.eps[:, :]).then_inc(fstd_ready, 1)

            def step(it, k, more=True, former=True):
                for e in range(E):
                    if more and e == NORM:
                        root(it + 1, 1 - k)
                    if affine and former and e == 1:
                        final_root(it - 1)
                    if more and e == COPY:
                        copy_rows(it + 1, 1 - k)
                    if more and router and e == PICK + 1:
                        exponential(it + 1, 1 - k)
                    if more and e == GATES_COPY:
                        copy_gates(it + 1, 1 - k)
                    n = E * it + e
                    act.wait_ge(h_done, n + 1)
                    at_least(act, o_done, n - 1)
                    for c in range(C2):
                        ins = act.activation(hid[e % 2][:, c, :], ps_h[e % 2][c][:, :], func,
                                             bias=B1[:, e, c:c + 1])
                    ins.then_inc(h_ready, 1)

            act.wait_ge(w_in, 16 * loads)
            root(0, 0)
            copy_rows(0, 0)
            if router:
                exponential(0, 0)
            copy_gates(0, 0)
            step(0, 0, former=False)
            with act.Fori(0, STEPS // 2 - 1) as i:
                step(2 * i + 1, 1)
                step(2 * i + 2, 0)
            step(last, 1, more=False)
            if affine:
                final_root(last)

        @block.vector
        def _(dve):
            def row_stats(it, k):
                for u in range(U):
                    dve.bn_stats(out=stats[:, u, :], in_=cast_col(K.X, U * it + u))
                dve.drain()
                for u in range(U):
                    dve.bn_aggr(out=mv[k][:, u, :], in_=stats[:, u, :])
                dve.drain().then_inc(stats_done, 1)

            def normalise(it, k):
                dve.wait_ge(std_ready, it + 1)
                dve.reciprocal(std[k][:, :], std[k][:, :])
                dve.drain()
                for u in range(U):
                    dve.tensor_scalar(y[k][:, u, :], cast_col(K.X, U * it + u), mv[k][:, u, 0:1], std[k][:, u:u + 1],
                                      ALU.subtract, ALU.mult)
                dve.drain().then_inc(y_ready, 1)

            def gate(it, k):
                dve.wait_ge(logits_done, it + 1)
                dve.tensor_tensor(g[k][:, :, :], ps_T[:, :, 0:E], gb[:, :].unsqueeze(1).to_broadcast([P, U, E]),
                                  ALU.add)
                dve.drain()
                top2(dve, K, g[k], E, T, gap_ready, exp_ready, it + 1, U)
                dve.drain().then_inc(g_ready, 1)

            def final_stats(it, k):
                for u in range(U):
                    dve.bn_stats(out=stats[:, u, :], in_=y[k][:, u, :])
                dve.drain()
                for u in range(U):
                    dve.bn_aggr(out=fmv[:, u, :], in_=stats[:, u, :])
                dve.drain().then_inc(fstats_done, 1)

            def final_rows(it, k):
                dve.wait_ge(fstd_ready, it + 1)
                dve.reciprocal(fstd[:, :], fstd[:, :])
                dve.drain()
                dve.wait_ge(stored, 16 * (it + 1))
                for u in range(U):
                    dve.tensor_scalar(z[:, u, :], y[k][:, u, :], fmv[:, u, 0:1], fstd[:, u:u + 1], ALU.subtract,
                                      ALU.mult)
                dve.drain().then_inc(z_ready, 1)

            def step(it, k, more=True, former=True):
                total = lambda u: y[k][:, u, :] if affine else cast_col(K.X, U * it + u)
                dve.wait_ge(b_done, it + 1)
                whole = y[k][:, :, :] if affine else K.X[:, bass.ds(U * it, U), :]
                dve.tensor_tensor(whole, whole, ps_b[:, :, :], ALU.add)
                dve.drain().then_inc(b_used, 1)
                for e in range(E):
                    if affine and former and e == 1:
                        final_rows(it - 1, 1 - k)
                    if more and e == STATS:
                        row_stats(it + 1, 1 - k)
                    if more and e == NORM:
                        normalise(it + 1, 1 - k)
                    if more and router and e == PICK:
                        gate(it + 1, 1 - k)
                    dve.wait_ge(o_done, E * it + e + 1)
                    for u in range(U):
                        dve.scalar_tensor_tensor(out=total(u), in0=ps_o[e % 2][:, u, :], scalar=g[k][:, u, e:e + 1],
                                                 in1=total(u), op0=ALU.mult, op1=ALU.add)
                    dve.drain().then_inc(o_used, 1)
                if affine:
                    final_stats(it, k)

            if router:
                dve.tensor_scalar(T.rev[:, :], K.iota[:, 0:E], -1.0, float(E), ALU.mult, ALU.add)
                dve.wait_ge(w_in, 16 * loads)
            else:
                dve.wait_ge(g_ready, 2)
            row_stats(0, 0)
            normalise(0, 0)
            if router:
                gate(0, 0)
            step(0, 0, former=False)
            with dve.Fori(0, STEPS // 2 - 1) as i:
                step(2 * i + 1, 1)
                step(2 * i + 2, 0)
            step(last, 1, more=False)
            if affine:
                final_rows(last, 1)


def grouped_gcn_stage(nc, K, D):
    with ExitStack() as ctx:
        sb = lambda n, s, d=F32: ctx.enter_context(nc.sbuf_tensor("gc_" + n, s, d))
        pb = lambda n, s: ctx.enter_context(nc.psum_tensor("gc_" + n, s, F32))
        sem = lambda n: ctx.enter_context(nc.semaphore("gc_" + n))
        pair = lambda n, s: [sb(f"{n}{k}", s) for k in range(2)]
        C2 = HID // P
        GU, UN = NG * U, U * NN
        WIDE = 64
        adjn, adjt = sb("adjn", [NN, B, NN]), sb("adjt", [NN, B, NN])
        W1, W2 = sb("W1", [P, NG, HID]), sb("W2", [P, NG, C2, F])
        B1, B2 = sb("B1", [P, NG, C2]), sb("B2", [NN, NG, F])
        fw, fx, wm = sb("fw", [NN, NG]), sb("fx", [NN, 4]), sb("wm", [NN, NG])
        tmp, an = sb("tmp", [NN, 2, U, NN]), sb("an", [NN, NG, U, NN])
        at_pad = pair("at", [NN, GUN + WIDE - NN])
        at = [t[:, 0:GUN].rearrange("p (g u n) -> p g u n", g=NG, u=U) for t in at_pad]
        deg, dinv, diag = sb("deg", [NN, GU]), sb("dinv", [NN, GU]), sb("diag", [NN, NG, U, NN])
        stats, mv, std = sb("stats", [NN, U, 6]), sb("mv", [NN, U, 2]), sb("std", [NN, U])
        y = pair("y", [NN, U, F])
        ax, hid = sb("ax", [P, GUN]), sb("hid", [P, C2, GUN])
        s2, t2, r2 = pair("s2", [NN, U, F]), pair("t2", [NN, U, F]), pair("r2", [NN, U, F])
        fused = sb("fused", [NN, U, F])
        ps_dd, ps_ax = pb("ps_dd", [WIDE, 512]), pb("ps_ax", [P, 512])
        ps_h = [pb(f"ps_h{c}", [P, 512]) for c in range(C2)]
        ps_s = [pb(f"ps_s{k}", [NN, U, F]) for k in range(2)]
        ps_o = [pb(f"ps_o{k}", [WIDE, U, F]) for k in range(2)]
        (w_in, adj_in, fw_shift, fw_exp, deg_ready, root_ready, diag_ready, diag_done, norm_ready, ax_done, ax_ready,
         h_done, h_ready, s_done, s_ready, o_done, t_ready, r_ready, r_used) = [
            sem(n) for n in ("w_in", "adj_in", "fw_shift", "fw_exp", "deg_ready", "root_ready", "diag_ready",
                             "diag_done", "norm_ready", "ax_done", "ax_ready", "h_done", "h_ready", "s_done",
                             "s_ready", "o_done", "t_ready", "r_ready", "r_used")]
        loads = 3 + C2
        last = STEPS - 1
        block = ctx.enter_context(nc.Block())
        gun = "p g u n -> p (g u n)"
        mask = K.groups[0:NN, :].rearrange("p (g n) -> p g n", g=NG)
        cols = lambda g: slice(g * UN, (g + 1) * UN)
        buf = lambda k, g: (k * NG + g) % 2

        @block.sync
        def _(sp):
            sp.dma_start(adjn[:, :, :], D["adj"][:, 0:NN, 0:NN].rearrange("b n m -> n b m")).then_inc(adj_in, 16)
            sp.dma_start(adjt[:, :, :], D["adjT"][:, 0:NN, 0:NN].rearrange("b m n -> m b n")).then_inc(adj_in, 16)
            sp.dma_start(fw[:, :], D["fusion_w"].partition_broadcast(NN)).then_inc(adj_in, 16)
            sp.dma_start(W1[:, :, :], D["gW1"].rearrange("e d f -> d e f")).then_inc(w_in, 16)
            for c in range(C2):
                sp.dma_start(W2[:, :, c, :], D["gW2"][:, c * P:(c + 1) * P, :].rearrange("e f d -> f e d")
                             ).then_inc(w_in, 16)
            sp.dma_start(B2[:, :, :], D["gb2"].partition_broadcast(NN)).then_inc(w_in, 16)
            sp.dma_start(B1[:, :, :], D["gb1"]).then_inc(w_in, 16)

        @block.vector
        def _(dve):
            def degrees(it, k):
                eye = K.eye[0:NN, :].unsqueeze(1).to_broadcast([NN, U, NN])
                for t, a in enumerate((adjt, adjn)):
                    dve.tensor_tensor(tmp[:, t], a[:, bass.ds(U * it, U), :], eye, ALU.add)
                for u in range(U):
                    dve.bn_stats(out=stats[:, u, :], in_=cast_col(K.X[0:NN], U * it + u))
                dve.drain()
                for u in range(U):
                    dve.bn_aggr(out=mv[:, u, :], in_=stats[:, u, :])
                wide = [NN, NG, U, NN]
                dve.tensor_tensor(an[:, :, :, :], tmp[:, 1].unsqueeze(1).to_broadcast(wide),
                                  mask.unsqueeze(2).to_broadcast(wide), ALU.mult)
                dve.tensor_tensor(at[k], tmp[:, 0].unsqueeze(1).to_broadcast(wide),
                                  mask.unsqueeze(2).to_broadcast(wide), ALU.mult)
                dve.drain()
                dve.tensor_reduce(deg[:, :], an[:, :, :, :].rearrange("p g u n -> p (g u) n"), AX.X, ALU.add)
                dve.drain()
                dve.scalar_tensor_tensor(out=dinv[:, :], in0=deg[:, :], scalar=0.0, in1=deg[:, :],
                                         op0=ALU.is_equal, op1=ALU.add)
                dve.drain().then_inc(deg_ready, 1)

            def scale_rows(it, k):
                dve.wait_ge(root_ready, it + 1)
                dve.reciprocal(dinv[:, :], dinv[:, :])
                dve.reciprocal(std[:, :], std[:, :])
                dve.drain()
                dve.scalar_tensor_tensor(out=dinv[:, :], in0=deg[:, :], scalar=0.0, in1=dinv[:, :],
                                         op0=ALU.not_equal, op1=ALU.mult)
                for u in range(U):
                    dve.tensor_scalar(y[k][:, u, :], cast_col(K.X[0:NN], U * it + u), mv[:, u, 0:1], std[:, u:u + 1],
                                      ALU.subtract, ALU.mult)
                dve.drain()
                over = dinv[:, :].unsqueeze(2).to_broadcast([NN, GU, NN])
                dve.tensor_tensor(diag[:, :, :, :].rearrange("p g u n -> p (g u) n"),
                                  K.eye[0:NN, :].unsqueeze(1).to_broadcast([NN, GU, NN]), over,
                                  ALU.mult).then_inc(diag_ready, 1)
                rows = at[k].rearrange("p g u n -> p (g u) n")
                dve.tensor_tensor(rows, rows, over, ALU.mult)
                dve.drain()

            def scale_columns(it, k):
                dve.wait_ge(diag_done, it + 1)
                flat = at_pad[k][:, 0:GUN]
                dve.tensor_tensor(flat, flat, ps_dd[0:NN, 0:GUN], ALU.mult)
                dve.drain().then_inc(norm_ready, 1)

            def bias(it, k, g):
                n = NG * it + g
                dve.wait_ge(o_done, n + 1)
                at_least(dve, r_ready, n - 1)
                dve.tensor_tensor(t2[buf(k, g)][:, :, :], ps_o[buf(k, g)][0:NN, :, :],
                                  B2[:, g, :].unsqueeze(1).to_broadcast([NN, U, F]), ALU.add)
                dve.drain().then_inc(t_ready, 1)

            def add(it, k, g):
                n = NG * it + g
                dve.wait_ge(r_ready, n + 1)
                r = r2[buf(k, g)][:, :, :]
                if g == 0:
                    dve.tensor_copy(fused[:, :, :], r)
                else:
                    dve.tensor_tensor(fused[:, :, :], fused[:, :, :], r, ALU.add)
                dve.drain().then_inc(r_used, 1)

            def step(it, k, more=True):
                if more:
                    degrees(it + 1, 1 - k)
                bias(it, k, 0)
                bias(it, k, 1)
                add(it, k, 0)
                if more:
                    scale_rows(it + 1, 1 - k)
                bias(it, k, 2)
                add(it, k, 1)
                bias(it, k, 3)
                add(it, k, 2)
                if more:
                    scale_columns(it + 1, 1 - k)
                bias(it, k, 4)
                add(it, k, 3)
                add(it, k, 4)
                x4 = K.X[0:NN, bass.ds(U * it, U), :]
                dve.tensor_tensor(x4, x4, fused[:, :, :], ALU.add)
                dve.drain()

            dve.wait_ge(adj_in, 48)
            dve.tensor_reduce(fx[:, 0:1], fw[:, :], AX.X, ALU.max, negate=True).then_inc(fw_shift, 1)
            dve.wait_ge(fw_exp, 1)
            dve.reciprocal(fx[:, 2:3], fx[:, 1:2])
            dve.drain()
            dve.scalar_tensor_tensor(out=wm[:, :], in0=fw[:, :], scalar=fx[:, 2:3], in1=K.member[0:NN, :],
                                     op0=ALU.mult, op1=ALU.mult)
            for k in range(2):
                dve.memset(at_pad[k][:, GUN:GUN + WIDE - NN], 0.0)
            dve.drain()
            dve.wait_ge(w_in, 16 * loads)
            degrees(0, 0)
            scale_rows(0, 0)
            scale_columns(0, 0)
            step(0, 0)
            with dve.Fori(0, STEPS // 2 - 1) as i:
                step(2 * i + 1, 1)
                step(2 * i + 2, 0)
            step(last, 1, more=False)

        @block.scalar
        def _(act):
            def roots(it):
                act.wait_ge(deg_ready, it + 1)
                act.activation(dinv[:, :], dinv[:, :], ACT.Sqrt)
                act.activation(std[:, :], mv[:, :, 1], ACT.Sqrt, bias=K.eps[0:NN, :])
                act.drain().then_inc(root_ready, 1)

            def copy_ax(it):
                act.wait_ge(ax_done, it + 1)
                act.activation(ax[:, :], ps_ax[:, 0:GUN], ACT.Copy).then_inc(ax_ready, 1)

            def hidden(it, g):
                for c in range(C2):
                    ins = act.activation(hid[:, c, cols(g)], ps_h[c][:, cols(g)], ACT.Relu, bias=B1[:, g, c:c + 1])
                ins.then_inc(h_ready, 1)

            def copy_s(it, k, g):
                n = NG * it + g
                act.wait_ge(s_done, n + 1)
                at_least(act, o_done, n - 1)
                act.activation(s2[buf(k, g)][:, :, :], ps_s[buf(k, g)][:, :, :], ACT.Copy).then_inc(s_ready, 1)

            def weigh(it, k, g):
                n = NG * it + g
                act.wait_ge(t_ready, n + 1)
                at_least(act, r_used, n - 1)
                act.activation(r2[buf(k, g)][:, :, :], t2[buf(k, g)][:, :, :], ACT.Relu,
                               scale=wm[:, g:g + 1]).then_inc(r_ready, 1)

            def step(it, k, more=True):
                act.wait_ge(h_done, it + 1)
                for g in range(NG):
                    hidden(it, g)
                copy_s(it, k, 0)
                copy_s(it, k, 1)
                if more:
                    roots(it + 1)
                for g in range(2, NG):
                    weigh(it, k, g - 2)
                    copy_s(it, k, g)
                weigh(it, k, 3)
                weigh(it, k, 4)
                if more:
                    copy_ax(it + 1)

            act.wait_ge(fw_shift, 1)
            act.activation(fw[:, :], fw[:, :], ACT.Exp, bias=fx[:, 0:1], accum_out=fx[:, 1:2])
            act.drain().then_inc(fw_exp, 1)
            act.wait_ge(w_in, 16 * loads)
            roots(0)
            copy_ax(0)
            step(0, 0)
            with act.Fori(0, STEPS // 2 - 1) as i:
                step(2 * i + 1, 1)
                step(2 * i + 2, 0)
            step(last, 1, more=False)

        @block.tensor
        def _(pe):
            def diagonal(it):
                pe.wait_ge(diag_ready, it + 1)
                pe.matmul(ps_dd[:, 0:GUN], K.ones[0:NN, 0:WIDE], diag[:, :, :, :].rearrange(gun), start=True,
                          stop=True).then_inc(diag_done, 1)

            def aggregate(it, k):
                pe.wait_ge(norm_ready, it + 1)
                out = ps_ax[:, 0:GUN].rearrange("p (g u n) -> p g u n", g=NG, u=U)
                for u in range(U):
                    ins = pe.matmul(out[:, :, u, :], y[k][:, u, :], at[k][:, :, u, :], start=True, stop=True)
                ins.then_inc(ax_done, 1)

            def second(it, k, g):
                n = NG * it + g
                pe.wait_ge(h_ready, n + 1)
                at_least(pe, s_ready, n - 1)
                for u in range(U):
                    for c in range(C2):
                        ins = pe.matmul(ps_s[buf(k, g)][:, u, :], hid[:, c, (g * U + u) * NN:(g * U + u + 1) * NN],
                                        W2[:, g, c, :], start=c == 0, stop=c == C2 - 1)
                ins.then_inc(s_done, 1)

            def spread(it, k, g):
                n = NG * it + g
                pe.wait_ge(s_ready, n + 1)
                at_least(pe, t_ready, n - 1)
                for u in range(U):
                    ins = pe.matmul(ps_o[buf(k, g)][:, u, :], at_pad[k][:, (g * U + u) * NN:(g * U + u) * NN + WIDE],
                                    s2[buf(k, g)][:, u, :], start=True, stop=True)
                ins.then_inc(o_done, 1)

            def step(it, k, more=True):
                pe.wait_ge(ax_ready, it + 1)
                at_least(pe, h_ready, NG * it)
                for g in range(NG):
                    for c in range(C2):
                        ins = pe.matmul(ps_h[c][:, cols(g)], W1[:, g, c * P:(c + 1) * P], ax[:, cols(g)], start=True,
                                        stop=True)
                ins.then_inc(h_done, 1)
                second(it, k, 0)
                for g in range(1, NG):
                    second(it, k, g)
                    if g < NG - 1:
                        spread(it, k, g - 1)
                if more:
                    diagonal(it + 1)
                spread(it, k, NG - 2)
                spread(it, k, NG - 1)
                if more:
                    aggregate(it + 1, 1 - k)

            pe.wait_ge(w_in, 16 * loads)
            diagonal(0)
            aggregate(0, 0)
            step(0, 0)
            with pe.Fori(0, STEPS // 2 - 1) as i:
                step(2 * i + 1, 1)
                step(2 * i + 2, 0)
            step(last, 1, more=False)


def store_x(nc, K, D):
    with ExitStack() as ctx:
        stored = ctx.enter_context(nc.semaphore("sx_stored"))
        block = ctx.enter_context(nc.Block())

        @block.sync
        def _(sp):
            sp.dma_start(D["out"].rearrange("b n f -> n b f"), K.X[:, :, :]).then_inc(stored, 16)
            sp.wait_ge(stored, 16)


def build(nc, D, upto=9, skip_to=0):
    with ExitStack() as ctx:
        sb = lambda n, s, d=F32: ctx.enter_context(nc.sbuf_tensor(n, s, d))
        K = Buffers()
        K.X = sb("X", [P, B, F])
        layout, width = const_layout()
        K.const = sb("const", [P, width])
        view = {name: K.const[:, at:at + n] for name, (at, n) in layout.items()}
        K.ident, K.upto, K.iota, K.part, K.trash = (view[n] for n in ("ident", "upto", "iota", "part", "trash"))
        K.member, K.groups, K.eye, K.ones = (view[n] for n in ("member", "groups", "eye", "ones"))
        K.eps = sb("eps", [P, 1])
        K.gates4 = sb("gates4", [P, B, GE])
        D["table"] = nc.dram_tensor("source_table", [M, ROW], F32, kind="Internal").ap()
        D["acc"] = [nc.dram_tensor(f"accumulator{k}", [M + P, ROW], F32, kind="Internal").ap() for k in range(G)]
        D["hi_row"] = nc.dram_tensor("hi_row", list(D["dst_row"].shape), BF16, kind="Internal").ap()
        D["lo_row"] = nc.dram_tensor("lo_row", list(D["dst_row"].shape), BF16, kind="Internal").ap()
        with ExitStack() as gat:
            gb = lambda n, s, d=F32: gat.enter_context(nc.sbuf_tensor(n, s, d))
            K.wgat, K.top = gb("wgat", [P, ROW + HEADS]), gb("top", [P, HEADS])
            K.TA, K.AD, K.TAD = gb("TA", [P, B, ROW]), gb("AD", [P, 3, HEADS, B], BF16), gb("TAD", [P, B, HEADS])
            with nc.sbuf_tensor("Y", [P, B, F], F32) as K.Y:
                load_stage(nc, K, D)
                if skip_to < 1:
                    dense_attention_stage(nc, K, D)
                    layernorm_stage(nc, K, K.Y, K.Y, P, "l1")
                    gelu_residual_stage(nc, K, D)
                if upto == 1:
                    return store_x(nc, K, D)
                if skip_to < 2:
                    layernorm_stage(nc, K, K.X, K.Y, P, "l2")
                    gat_weights_stage(nc, K, D)

                    def keep(dve, ps, i):
                        dve.tensor_copy(K.TA[:, bass.ds(U * i, U), :], ps[:, :, 0:ROW])
                        dve.tensor_copy(K.TAD[:, bass.ds(U * i, U), :], ps[:, :, ROW:ROW + HEADS])

                    projection_stage(nc, K, D, "pa_", ROW + HEADS, K.wgat[:, :], keep)
                    table_stage(nc, K, D)
            if skip_to < 2:
                with ExitStack() as edges:
                    eb = lambda n, d=F32: edges.enter_context(nc.sbuf_tensor(n, [P, D["dst_col"].shape[1]], d))
                    C = Buffers()
                    C.src, C.dst, C.where = eb("e_src", I32), eb("e_dst"), eb("e_where")
                    C.chunks = D["dst_col"].shape[1]
                    edge_index_stage(nc, K, D, C)
                    edge_stage(nc, K, D, C)
                combine_stage(nc, K, D)
        if skip_to < 2:
            top2_stage(nc, K, K.gates4, GE, "t4_")
            experts_stage(nc, K, D, "x4_", GE, D["W1"], D["b1"], D["W2"], D["b2"], ACT.Gelu, gates=K.gates4)
        if upto == 2:
            return store_x(nc, K, D)
        if skip_to < 3:
            grouped_gcn_stage(nc, K, D)
        if upto == 3:
            return store_x(nc, K, D)
        experts_stage(nc, K, D, "x16_", E2, D["fw1"], D["fb1"], D["fw2"], D["fb2"], ACT.Relu,
                      router=(D["gate_w"], D["gate_b"]), affine=(D["f_gamma"], D["f_beta"]))


NAMES = {"x": "x", "adj": "adj", "gnn_W": "L0_gnn_W", "gnn_a": "L0_gnn_a", "gnn_gamma": "L0_gnn_gamma",
         "gnn_beta": "L0_gnn_beta", "W_gat": "L0_ffn_W_gat", "att_src": "L0_ffn_att_src",
         "att_dst": "L0_ffn_att_dst", "b_gat": "L0_ffn_b_gat", "ln_gamma": "L0_ffn_ln_gamma",
         "ln_beta": "L0_ffn_ln_beta", "W1": "L0_ffn_W1", "b1": "L0_ffn_b1", "W2": "L0_ffn_W2", "b2": "L0_ffn_b2",
         "gW1": "L1_gnn_W1", "gb1": "L1_gnn_b1", "gW2": "L1_gnn_W2", "gb2": "L1_gnn_b2",
         "fusion_w": "L1_gnn_fusion_w", "gate_w": "L1_ffn_gate_w", "gate_b": "L1_ffn_gate_b", "fw1": "L1_ffn_w1",
         "fb1": "L1_ffn_b1", "fw2": "L1_ffn_w2", "fb2": "L1_ffn_b2", "f_gamma": "L1_ffn_gamma",
         "f_beta": "L1_ffn_beta"}


def host_arrays(inputs):
    import numpy as np
    arrays = {k: np.ascontiguousarray(inputs[v]) for k, v in NAMES.items()}
    arrays["adjT"] = np.ascontiguousarray(np.transpose(arrays["adj"], (0, 2, 1)))
    arrays["gnn_a"] = np.ascontiguousarray(arrays["gnn_a"].reshape(2, F).T)
    for name in ("b1", "gb1", "fb1"):
        b = arrays[name]
        arrays[name] = np.ascontiguousarray(b.reshape(len(b), HID // P, P).transpose(2, 0, 1))
    edges = np.ascontiguousarray(inputs["L0_ffn_edge_index"])
    arrays["src_col"] = np.ascontiguousarray(edges[0].reshape(P, -1))
    arrays["dst_col"] = np.ascontiguousarray(edges[1].reshape(P, -1))
    arrays["dst_row"] = np.ascontiguousarray(edges[1].reshape(P, -1).T)
    layout, width = const_layout()
    consts = np.zeros((P, width), np.float32)
    put = lambda name, v: consts.__setitem__((slice(0, len(v)), slice(layout[name][0], sum(layout[name]))), v)
    put("ident", np.eye(P))
    put("upto", np.tril(np.ones((P, P))))
    put("iota", np.tile(np.arange(P), (P, 1)))
    put("part", np.arange(P)[:, None])
    put("trash", M + np.arange(P)[:, None])
    member = np.array([[float(n in g) for g in GROUPS] for n in range(NN)])
    put("member", member)
    put("groups", np.einsum("mg,ng->mgn", member, member).reshape(NN, NG * NN))
    put("eye", np.eye(NN))
    put("ones", np.ones((P, P)))
    arrays["consts"] = consts
    return arrays


def kernel(**inputs):
    import numpy as np
    import concourse.bacc as bacc
    from concourse.bass_utils import run_bass_kernel_spmd

    nc = bacc.Bacc("TRN2", target_bir_lowering=False, num_devices=1)
    arrays = host_arrays(inputs)
    D = {name: nc.dram_tensor(f"in_{name}", a.shape, mybir.dt.from_np(a.dtype), kind="ExternalInput").ap()
         for name, a in arrays.items()}
    D["out"] = nc.dram_tensor("out_x", [B, P, F], F32, kind="ExternalOutput").ap()
    build(nc, D)
    result = run_bass_kernel_spmd(nc, [{f"in_{k}": a for k, a in arrays.items()}], core_ids=[0])
    return np.asarray(result.results[0]["out_x"])
```

```python
import concourse.bass as bass
import concourse.mybir as mybir
from contextlib import ExitStack

F32 = mybir.dt.float32
BF16 = mybir.dt.bfloat16
I32 = mybir.dt.int32
ALU = mybir.AluOpType
ACT = mybir.ActivationFunctionType
AX = mybir.AxisListType

P = 128
B = 128
F = 128
M = P * B
U = 4
STEPS = B // U
EPS = 1e-5
HEADS = 4
GE = 4
HE = HEADS * GE
ROW = HEADS + HE
E2 = 16
HID = 256
G = 16
COPIES = G // 2
ZP = 5
NEG = -9000000000000000.0
GROUPS = [list(range(25)), [0, 1, 2, 3, 4, 5, 6, 7, 8], [0, 9, 10, 11, 12, 13, 14], [6, 7, 8, 12, 13, 14],
          [3, 4, 5, 9, 10, 11]]
NG = len(GROUPS)
NN = len(GROUPS[0])
GUN = NG * U * NN


class Buffers:
    pass


def const_layout():
    at, out = 0, {}
    for name, width in (("ident", P), ("upto", P), ("iota", P), ("part", 1), ("trash", 1),
                        ("member", NG), ("groups", NG * NN), ("eye", NN), ("ones", P)):
        out[name] = (at, width)
        at += width
    return out, at


def cast_col(t, b):
    return t[:, bass.ds(b, 1), :].rearrange("p a b -> p (a b)")


def at_least(engine, semaphore, value):
    if not isinstance(value, int) or value > 0:
        engine.wait_ge(semaphore, value)


def bring(sp, sem, loads):
    for to, of in loads:
        sp.dma_start(to, of).then_inc(sem, 16)
    sp.wait_ge(sem, 16 * len(loads))


def dense_attention_stage(nc, K, D):
    with ExitStack() as ctx:
        sb = lambda n, s, d=F32: ctx.enter_context(nc.sbuf_tensor("ga_" + n, s, d))
        pb = lambda n, s: ctx.enter_context(nc.psum_tensor("ga_" + n, s, F32))
        sem = lambda n: ctx.enter_context(nc.semaphore("ga_" + n))
        pair = lambda n, s: [sb(f"{n}{k}", s) for k in range(2)]
        row, mv, std = sb("stats", [P, U, 6]), sb("mv", [P, U, 2]), sb("std", [P, U])
        W, WT, a2 = sb("W", [P, F]), sb("WT", [P, F]), sb("a2", [P, 2])
        Wa, Wa1, Wa2 = sb("Wa", [P, 2]), sb("Wa1", [P, P]), sb("Wa2", [P, P])
        xn, xnT, Wh = sb("xn", [P, U, F]), sb("xnT", [P, U, P]), pair("Wh", [P, U, F])
        raw, e = sb("raw", [P, U, P]), pair("e", [P, U, P])
        negmax, rowsum, inv = pair("negmax", [P, U]), pair("rowsum", [P, U]), sb("inv", [P, U])
        prob, probT = sb("prob", [P, U, P]), sb("probT", [P, U, P])
        ps_xT, ps_wh, ps_e = pb("ps_xT", [P, U, P]), pb("ps_wh", [P, U, F]), pb("ps_e", [P, U, P])
        ps_pT, ps_out = pb("ps_pT", [P, U, P]), pb("ps_out", [P, U, F])
        parts = 8
        nb = B // parts
        x_part, adj_part = ([sem(f"{n}{k}") for k in range(2)] for n in ("x_part", "adj_part"))
        (x_in, adj_in, const_in, w_loaded, wT_done, wT_copied, wa_done, wa_ready, mask_ready, eps_ready, stats_done,
         std_ready, xn_ready, xT_done, xT_copied, e_done, e_copied, wh_done, wh_copied, max_ready, prob_ready,
         pT_done, pT_copied, out_done, out_used) = [
            sem(n) for n in ("x_in", "adj_in", "const_in", "w_loaded", "wT_done", "wT_copied", "wa_done",
                             "wa_ready", "mask_ready", "eps_ready", "stats_done", "std_ready", "xn_ready",
                             "xT_done", "xT_copied", "e_done", "e_copied", "wh_done", "wh_copied", "max_ready",
                             "prob_ready", "pT_done", "pT_copied", "out_done", "out_used")]
        last = STEPS - 1
        block = ctx.enter_context(nc.Block())

        def turns(body, engine):
            body(-1, 1, out=False)
            body(0, 0)
            with engine.Fori(0, (STEPS - 4) // 2) as i:
                body(2 * i + 1, 1)
                body(2 * i + 2, 0)
            body(last - 2, 1, stats=False)
            body(last - 1, 0, stats=False, norm=False)
            body(last, 1, stats=False, norm=False, score=False)

        @block.sync
        def _(sp):
            def bring(c):
                part = slice(c * nb, (c + 1) * nb)
                sp.dma_start(K.X[:, part, :], D["x"][part].rearrange("b n f -> n b f")).then_inc(x_part[c % 2], 16)
                sp.dma_start(K.Y[:, part, :], D["adj"][part].rearrange("b n f -> n b f")).then_inc(adj_part[c % 2], 16)

            sp.dma_start(K.const[:, :], D["consts"]).then_inc(const_in, 16)
            sp.dma_start(W[:, :], D["gnn_W"]).then_inc(w_loaded, 16)
            sp.dma_start(a2[:, :], D["gnn_a"]).then_inc(w_loaded, 16)
            bring(0)
            bring(1)
            for c in range(parts):
                sp.wait_ge(x_part[c % 2], 16 * (c // 2 + 1))
                sp.sem_inc(x_in, nb // U)
                sp.wait_ge(adj_part[c % 2], 16 * (c // 2 + 1))
                sp.sem_inc(adj_in, nb // U)
                if c + 2 < parts:
                    bring(c + 2)

        @block.gpsimd
        def _(pool):
            pool.memset(K.eps[:, :], EPS).then_inc(eps_ready, 1)
            for c in range(parts):
                pool.wait_ge(adj_in, nb // U * (c + 1))
                part = K.Y[:, c * nb:(c + 1) * nb, :].rearrange("p b m -> p (b m)")
                pool.tensor_scalar(part, part, 0.0, NEG, ALU.is_le, ALU.mult).then_inc(mask_ready, nb // U)

        @block.tensor
        def _(pe):
            def transpose_rows(it):
                pe.wait_ge(xn_ready, it + 1)
                for u in range(U):
                    ins = pe.transpose(ps_xT[:, u, :], xn[:, u, :], K.ident)
                ins.then_inc(xT_done, 1)

            def turn(it, k, out=True, norm=True, score=True, stats=True):
                if score:
                    n = it + 1
                    pe.wait_ge(xT_copied, n + 1)
                    at_least(pe, e_copied, n)
                    pe.matmul(ps_e[:, :, :].rearrange("p u n -> p (u n)"), Wa2[:, :],
                              xnT[:, :, :].rearrange("p u n -> p (u n)"), start=True, stop=False)
                    for u in range(U):
                        ins = pe.matmul(ps_e[:, u, :], xnT[:, u, :], Wa1[:, :], start=False,
                                        stop=u == U - 1)
                    ins.then_inc(e_done, 1)
                    at_least(pe, wh_copied, n)
                    for u in range(U):
                        ins = pe.matmul(ps_wh[:, u, :], xnT[:, u, :], W[:, :], start=True, stop=True)
                    ins.then_inc(wh_done, 1)
                if out:
                    pe.wait_ge(prob_ready, it + 1)
                    for u in range(U):
                        ins = pe.transpose(ps_pT[:, u, :], prob[:, u, :], K.ident)
                    ins.then_inc(pT_done, 1)
                if norm:
                    transpose_rows(it + 2)
                if out:
                    pe.wait_ge(pT_copied, it + 1)
                    at_least(pe, out_used, it)
                    for u in range(U):
                        ins = pe.matmul(ps_out[:, u, :], probT[:, u, :], Wh[k][:, u, :], start=True, stop=True)
                    ins.then_inc(out_done, 1)

            pe.wait_ge(w_loaded, 32)
            pe.wait_ge(const_in, 16)
            pe.transpose(ps_xT[:, 0, :], W[:, :], K.ident).then_inc(wT_done, 1)
            pe.wait_ge(wT_copied, 1)
            pe.matmul(ps_e[:, 0, 0:2], WT[:, :], a2[:, :], start=True, stop=True).then_inc(wa_done, 1)
            transpose_rows(0)
            pe.wait_ge(wa_ready, 1)
            turns(turn, pe)

        @block.scalar
        def _(act):
            def root(it):
                act.wait_ge(stats_done, it + 1)
                act.activation(std[:, :], mv[:, :, 1], ACT.Sqrt, bias=K.eps[:, :]).then_inc(std_ready, 1)

            def copy_rows(it):
                act.wait_ge(xT_done, it + 1)
                act.activation(xnT[:, :, :], ps_xT[:, :, :], ACT.Copy).then_inc(xT_copied, 1)

            def turn(it, k, out=True, norm=True, score=True, stats=True):
                if out:
                    act.wait_ge(max_ready, it + 1)
                    at_least(act, pT_done, it)
                    for u in range(U):
                        ins = act.activation(prob[:, u, :], e[k][:, u, :], ACT.Exp, bias=negmax[k][:, u:u + 1],
                                             accum_out=rowsum[k][:, u:u + 1])
                    ins.then_inc(prob_ready, 1)
                if score:
                    n = it + 1
                    act.wait_ge(e_done, n + 1)
                    act.activation(raw[:, :, :], ps_e[:, :, :], ACT.Copy).then_inc(e_copied, 1)
                if stats:
                    root(it + 3)
                if score:
                    act.wait_ge(wh_done, n + 1)
                    at_least(act, out_done, it)
                    act.activation(Wh[1 - k][:, :, :], ps_wh[:, :, :], ACT.Copy).then_inc(wh_copied, 1)
                if norm:
                    copy_rows(it + 2)

            act.wait_ge(eps_ready, 1)
            root(0)
            act.wait_ge(wT_done, 1)
            act.activation(WT[:, :], ps_xT[:, 0, :], ACT.Copy).then_inc(wT_copied, 1)
            root(1)
            copy_rows(0)
            turns(turn, act)

        @block.vector
        def _(dve):
            def row_stats(it):
                dve.wait_ge(x_in, it + 1)
                for u in range(U):
                    dve.bn_stats(out=row[:, u, :], in_=cast_col(K.X, U * it + u))
                dve.drain()
                for u in range(U):
                    dve.bn_aggr(out=mv[:, u, :], in_=row[:, u, :])
                dve.drain().then_inc(stats_done, 1)

            def normalise(it):
                dve.wait_ge(std_ready, it + 1)
                dve.reciprocal(std[:, :], std[:, :])
                dve.drain()
                at_least(dve, xT_done, it)
                for u in range(U):
                    dve.tensor_scalar(xn[:, u, :], cast_col(K.X, U * it + u), mv[:, u, 0:1], std[:, u:u + 1],
                                      ALU.subtract, ALU.mult)
                dve.drain().then_inc(xn_ready, 1)

            def turn(it, k, out=True, norm=True, score=True, stats=True):
                if norm:
                    normalise(it + 2)
                if stats:
                    row_stats(it + 3)
                if score:
                    n, s = it + 1, e[1 - k][:, :, :]
                    dve.wait_ge(e_copied, n + 1)
                    dve.scalar_tensor_tensor(out=s, in0=raw[:, :, :], scalar=0.2, in1=raw[:, :, :], op0=ALU.mult,
                                             op1=ALU.max)
                    dve.drain()
                    dve.wait_ge(mask_ready, n + 1)
                    dve.tensor_tensor(s, s, K.Y[:, bass.ds(U * n, U), :], ALU.add)
                    dve.drain()
                    dve.tensor_reduce(negmax[1 - k][:, :], s, AX.X, ALU.max, negate=True).then_inc(max_ready, 1)
                if out:
                    dve.wait_ge(pT_done, it + 1)
                    dve.tensor_copy(probT[:, :, :], ps_pT[:, :, :]).then_inc(pT_copied, 1)
                    dve.reciprocal(inv[:, :], rowsum[k][:, :])
                    dve.drain()
                    dve.wait_ge(out_done, it + 1)
                    dve.tensor_tensor(K.Y[:, bass.ds(U * it, U), :], ps_out[:, :, :],
                                      inv[:, :].unsqueeze(2).to_broadcast([P, U, F]), ALU.mult)
                    dve.drain().then_inc(out_used, 1)

            row_stats(0)
            dve.wait_ge(wa_done, 1)
            dve.tensor_copy(Wa[:, :], ps_e[:, 0, 0:2])
            dve.drain()
            dve.tensor_copy(Wa1[:, :], Wa[:, 0:1].to_broadcast([P, P]))
            dve.tensor_copy(Wa2[:, :], Wa[:, 1:2].to_broadcast([P, P]))
            dve.drain().then_inc(wa_ready, 1)
            normalise(0)
            row_stats(1)
            turns(turn, dve)


def gelu_and_projection_stage(nc, K, D):
    with ExitStack() as ctx:
        sb = lambda n, s, d=F32: ctx.enter_context(nc.sbuf_tensor("gp_" + n, s, d))
        sem = lambda n: ctx.enter_context(nc.semaphore("gp_" + n))
        pair = lambda n, s: [sb(f"{n}{k}", s) for k in range(2)]
        gamma, beta = sb("gamma", [P, F]), sb("beta", [P, F])
        stats, mv, std = sb("stats", [P, 2 * U, 6]), pair("mv", [P, 2 * U, 2]), pair("std", [P, 2 * U])
        pre, post = pair("pre", [P, U, F]), pair("post", [P, U, F])
        y, yT = sb("y", [P, U, F]), sb("yT", [P, U, P])
        ps_T = ctx.enter_context(nc.psum_tensor("gp_ps_T", [P, U, P], F32))
        ps_o = ctx.enter_context(nc.psum_tensor("gp_ps_o", [P, U, ROW + HEADS], F32))
        (loaded, zero_ready, zeroed, stats_done, std_ready, pre_normal, pre_ready, post_ready, y_ready, yT_done, yT_ready,
         proj_done) = [
            sem(n) for n in ("loaded", "zero_ready", "zeroed", "stats_done", "std_ready", "pre_normal", "pre_ready", "post_ready", "y_ready",
                             "yT_done", "yT_ready", "proj_done")]
        block = ctx.enter_context(nc.Block())
        DEPTH = 5
        alive = lambda it: not isinstance(it, int) or 0 <= it < STEPS
        used = lambda it: slice(0 if alive(it) else U, 2 * U if alive(it - 3) else U)

        def turns(body, engine):
            for it in range(DEPTH + 1):
                body(it, it % 2)
            with engine.Fori(0, (STEPS - DEPTH - 1) // 2) as i:
                body(2 * i + DEPTH + 1, 0)
                body(2 * i + DEPTH + 2, 1)
            for it in range(STEPS, STEPS + DEPTH):
                body(it, it % 2)

        @block.sync
        def _(sp):
            sp.dma_start(gamma[:, :], D["gnn_gamma"].partition_broadcast(P)).then_inc(loaded, 16)
            sp.dma_start(beta[:, :], D["gnn_beta"].partition_broadcast(P)).then_inc(loaded, 16)
            sp.wait_ge(zero_ready, 1)
            for k in range(COPIES):
                pieces = D["acc"][k].rearrange("(p t) c -> p (t c)", p=P)
                n = K.zeros.shape[1]
                for j in range(ZP):
                    sp.dma_start(pieces[:, j * n:(j + 1) * n], K.zeros[:, :]).then_inc(zeroed, 16)
            sp.wait_ge(zeroed, 16 * COPIES * ZP)

        @block.gpsimd
        def _(pool):
            pool.memset(K.zeros[:, :], 0.0).then_inc(zero_ready, 1)
            over = lambda t: t[:, :].unsqueeze(1).to_broadcast([P, U, F])
            pool.wait_ge(loaded, 32)
            with pool.Fori(0, STEPS // 2) as i:
                for k in range(2):
                    pool.wait_ge(pre_normal, 2 * i + k + 1)
                    pool.tensor_tensor(pre[k][:, :, :], pre[k][:, :, :], over(gamma), ALU.mult)
                    pool.drain()
                    pool.tensor_tensor(pre[k][:, :, :], pre[k][:, :, :], over(beta), ALU.add).then_inc(pre_ready, 1)

        @block.tensor
        def _(pe):
            with pe.Fori(0, STEPS) as i:
                pe.wait_ge(y_ready, i + 1)
                for u in range(U):
                    ins = pe.transpose(ps_T[:, u, :], y[:, u, :], K.ident)
                ins.then_inc(yT_done, 1)
                pe.wait_ge(yT_ready, i + 1)
                for u in range(U):
                    ins = pe.matmul(ps_o[:, u, :], yT[:, u, :], K.wgat[:, :], start=True, stop=True)
                ins.then_inc(proj_done, 1)

        @block.scalar
        def _(act):
            def turn(it, k):
                if alive(it - 5):
                    act.wait_ge(yT_done, it - 4)
                    act.activation(yT[:, :, :], ps_T[:, :, :], ACT.Copy).then_inc(yT_ready, 1)
                if alive(it) or alive(it - 3):
                    act.wait_ge(stats_done, it + 1)
                    act.activation(std[k][:, used(it)], mv[k][:, used(it), 1], ACT.Sqrt,
                                   bias=K.eps[:, :]).then_inc(std_ready, 1)
                if alive(it - 2):
                    act.wait_ge(pre_ready, it - 1)
                    act.activation(post[k][:, :, :], pre[k][:, :, :], ACT.Gelu).then_inc(post_ready, 1)

            turns(turn, act)

        @block.vector
        def _(dve):
            def aggregate(k, at):
                dve.drain()
                for u in range(U):
                    dve.bn_aggr(out=mv[k][:, at + u, :], in_=stats[:, at + u, :])

            def normalise(to, rows, at, mean, scale):
                for u in range(U):
                    dve.tensor_scalar(to[:, u, :], cast_col(rows, at + u), mean[:, u, 0:1], scale[:, u:u + 1],
                                      ALU.subtract, ALU.mult)

            def turn(it, k):
                if alive(it):
                    for u in range(U):
                        dve.bn_stats(out=stats[:, u, :], in_=cast_col(K.Y, U * it + u))
                    aggregate(k, 0)
                if alive(it - 3):
                    rows = K.X[:, bass.ds(U * (it - 3), U), :]
                    dve.wait_ge(post_ready, it - 2)
                    dve.tensor_tensor(rows, rows, post[1 - k][:, :, :], ALU.add)
                    dve.drain()
                    for u in range(U):
                        dve.bn_stats(out=stats[:, U + u, :], in_=cast_col(K.X, U * (it - 3) + u))
                    aggregate(k, U)
                if alive(it) or alive(it - 3):
                    dve.drain().then_inc(stats_done, 1)
                if alive(it - 5):
                    dve.wait_ge(proj_done, it - 4)
                    done = bass.ds(U * (it - 5), U)
                    dve.tensor_copy(K.TA[:, done, :], ps_o[:, :, 0:ROW])
                    dve.tensor_copy(K.TAD[:, done, :], ps_o[:, :, ROW:ROW + HEADS])
                if alive(it - 1) or alive(it - 4):
                    m, r = mv[1 - k], std[1 - k]
                    dve.wait_ge(std_ready, it)
                    dve.reciprocal(r[:, used(it - 1)], r[:, used(it - 1)])
                    dve.drain()
                if alive(it - 1):
                    normalise(pre[1 - k], K.Y, U * (it - 1), m[:, 0:U], r[:, 0:U])
                    dve.drain().then_inc(pre_normal, 1)
                if alive(it - 4):
                    normalise(y, K.X, U * (it - 4), m[:, U:2 * U], r[:, U:2 * U])
                    dve.drain().then_inc(y_ready, 1)

            turns(turn, dve)
            dve.drain()


def gat_weights_stage(nc, K, D):
    with ExitStack() as ctx:
        att = ctx.enter_context(nc.sbuf_tensor("gw_att", [P, 2, HE], F32))
        tmp = ctx.enter_context(nc.sbuf_tensor("gw_tmp", [P, 2, HE], F32))
        loaded = ctx.enter_context(nc.semaphore("gw_loaded"))
        block = ctx.enter_context(nc.Block())

        @block.sync
        def _(sp):
            sp.dma_start(K.wgat[:, HEADS:HEADS + HE], D["W_gat"]).then_inc(loaded, 16)
            sp.dma_start(att[:, 0, :], D["att_src"].rearrange("h e -> (h e)").partition_broadcast(P)).then_inc(loaded, 16)
            sp.dma_start(att[:, 1, :], D["att_dst"].rearrange("h e -> (h e)").partition_broadcast(P)).then_inc(loaded, 16)

        @block.vector
        def _(dve):
            dve.wait_ge(loaded, 48)
            for t in range(2):
                dve.tensor_tensor(tmp[:, t, :], K.wgat[:, HEADS:HEADS + HE], att[:, t, :], ALU.mult)
            dve.drain()
            for t, at in ((0, 0), (1, HEADS + HE)):
                dve.tensor_reduce(K.wgat[:, at:at + HEADS], tmp[:, t, :].rearrange("p (h e) -> p h e", e=GE), AX.X,
                                  ALU.add)
            dve.drain()


def table_stage(nc, K, D):
    with ExitStack() as ctx:
        top = ctx.enter_context(nc.sbuf_tensor("tb_top", [P, HEADS], F32))
        stored = ctx.enter_context(nc.semaphore("tb_stored"))
        top_ready = ctx.enter_context(nc.semaphore("tb_top_ready"))
        block = ctx.enter_context(nc.Block())

        @block.sync
        def _(sp):
            sp.dma_start(D["table"].rearrange("(n b) c -> n b c", b=B), K.TA[:, :, :]).then_inc(stored, 16)
            sp.wait_ge(stored, 16)

        rest = ctx.enter_context(nc.sbuf_tensor("tb_rest", [P, HEADS, B], F32))

        @block.vector
        def _(dve):
            dve.tensor_copy(rest[:, :, :], K.TAD[:, :, :].rearrange("p b h -> p h b"))
            dve.drain()
            for t in range(3):
                dve.tensor_copy(K.AD[:, t, :, :], rest[:, :, :])
                dve.drain()
                if t < 2:
                    dve.tensor_tensor(rest[:, :, :], rest[:, :, :], K.AD[:, t, :, :], ALU.subtract)
                    dve.drain()
            dve.tensor_reduce(top[:, :], K.TA[:, :, 0:HEADS].rearrange("p b h -> p h b"), AX.X,
                              ALU.max).then_inc(top_ready, 1)

        @block.gpsimd
        def _(pool):
            pool.wait_ge(top_ready, 1)
            pool.partition_all_reduce(K.top[:, :], top[:, :], P, bass.bass_isa.ReduceOp.max)


def edge_index_stage(nc, K, D, C):
    NC = C.chunks
    with ExitStack() as ctx:
        sb = lambda n, s, d=F32: ctx.enter_context(nc.sbuf_tensor("ei_" + n, s, d))
        q = NC // 2
        a, b, c = sb("a", [P, q], I32), sb("b", [P, q], I32), sb("c", [P, q], I32)
        lo, hi = sb("lo", [P, q], BF16), sb("hi", [P, q], BF16)
        loaded, used, rows_ready, stored = (ctx.enter_context(nc.semaphore("ei_" + n)) for n in
                                            ("loaded", "used", "rows_ready", "stored"))
        block = ctx.enter_context(nc.Block())
        row_form = D["dst_row"].rearrange("(p t) e -> p (t e)", p=P)
        lo_form = D["lo_row"].rearrange("(p t) e -> p (t e)", p=P)
        hi_form = D["hi_row"].rearrange("(p t) e -> p (t e)", p=P)

        @block.sync
        def _(sp):
            n = 0
            for h in range(2):
                cols = slice(h * q, (h + 1) * q)
                for src in (D["src_col"], D["dst_col"], row_form):
                    if n:
                        sp.wait_ge(used, n)
                    sp.dma_start(a[:, :], src[:, cols]).then_inc(loaded, 16)
                    n += 1
                sp.wait_ge(rows_ready, h + 1)
                sp.dma_start(lo_form[:, cols], lo[:, :]).then_inc(stored, 16)
                sp.dma_start(hi_form[:, cols], hi[:, :]).then_inc(stored, 16)
                sp.wait_ge(stored, 32 * (h + 1))

        @block.vector
        def _(dve):
            def split():
                dve.tensor_scalar(b[:, :], a[:, :], P - 1, None, ALU.bitwise_and)
                dve.tensor_scalar(c[:, :], a[:, :], 7, None, ALU.logical_shift_right)
                dve.drain().then_inc(used, 1)

            for h in range(2):
                cols = slice(h * q, (h + 1) * q)
                dve.wait_ge(loaded, 16 * (3 * h + 1))
                dve.tensor_scalar(a[:, :], a[:, :], float(M - 1), None, ALU.min)
                dve.drain()
                split()
                dve.scalar_tensor_tensor(out=C.src[:, cols], in0=b[:, :], scalar=float(B), in1=c[:, :],
                                         op0=ALU.mult, op1=ALU.add)
                dve.drain()
                dve.wait_ge(loaded, 16 * (3 * h + 2))
                dve.tensor_copy(C.dst[:, cols], a[:, :])
                split()
                dve.scalar_tensor_tensor(out=C.where[:, cols], in0=b[:, :], scalar=float(B), in1=c[:, :],
                                         op0=ALU.mult, op1=ALU.add)
                dve.drain()
                dve.tensor_scalar(C.where[:, cols], C.where[:, cols], K.trash, None, ALU.subtract)
                dve.drain()
                dve.scalar_tensor_tensor(out=C.where[:, cols], in0=C.dst[:, cols], scalar=float(M),
                                         in1=C.where[:, cols], op0=ALU.is_lt, op1=ALU.mult)
                dve.wait_ge(loaded, 16 * (3 * h + 3))
                split()
                if h:
                    dve.wait_ge(stored, 32 * h)
                dve.tensor_copy(lo[:, :], b[:, :])
                dve.tensor_copy(hi[:, :], c[:, :])
                dve.drain().then_inc(rows_ready, 1)


def edge_stage(nc, K, D, C):
    STEPS_E = C.chunks // G
    QUAD = 4
    PAIR = 2
    UNITS = G // QUAD * (HEADS // PAIR)
    RING = 3
    with ExitStack() as ctx:
        sb = lambda n, s, d=F32: ctx.enter_context(nc.sbuf_tensor("ed_" + n, s, d))
        pb = lambda n, s: ctx.enter_context(nc.psum_tensor("ed_" + n, s, F32))
        sem = lambda n: ctx.enter_context(nc.semaphore("ed_" + n))
        pair = lambda n, s, d=F32: [sb(f"{n}{k}", s, d) for k in range(2)]
        src_idx, put_idx = pair("src_idx", [P, G], I32), pair("put_idx", [P, G], I32)
        dcol, wcol = pair("dcol", [P, G]), pair("wcol", [P, G])
        drow = pair("drow", [P, G, P], I32)
        lrow, hrow = pair("lrow", [P, G, P], BF16), pair("hrow", [P, G, P], BF16)
        same = pair("same", [P, G, P])
        hot, hot_b = sb("hot", [P, G, P], BF16), sb("hot_b", [P, G, P], BF16)
        prod = pair("prod", [P, PAIR, QUAD * P])
        got, put = pair("got", [P, G, ROW]), pair("put", [P, G, ROW])
        adst, rank = pair("adst", [P, G, HEADS]), pair("rank", [P, G])
        msg = sb("msg", [P, G, ROW])
        sc, bound, diff = sb("sc", [P, G, HEADS]), sb("bound", [P, G, HEADS]), sb("diff", [P, G, HEADS])
        ps_a = [pb(f"ps_a{k}", [P, PAIR, QUAD * P]) for k in range(RING)]
        ps_d, ps_m = pb("ps_d", [P, G, HEADS]), pb("ps_m", [P, G, ROW])
        rows_in, gathered = ([sem(f"{n}{k}") for k in range(2)] for n in ("rows_in", "gathered"))
        added = [[sem(f"added{k}{h}") for h in range(2)] for k in range(2)]
        (cols_ready, hot_ready, same_ready, sel_done, prod_ready, sum_done, adst_ready, diff_ready,
         w_ready, msg_ready, merged, put_ready, put_idx_ready, gathers, landed, half_landed) = [
            sem(n) for n in ("cols_ready", "hot_ready", "same_ready", "sel_done",
                             "prod_ready", "sum_done", "adst_ready", "diff_ready", "w_ready", "msg_ready", "merged",
                             "put_ready", "put_idx_ready", "gathers", "landed", "half_landed")]
        block = ctx.enter_context(nc.Block())
        unit_at = lambda n: (n // (HEADS // PAIR) * QUAD, n % (HEADS // PAIR) * PAIR)

        @block.sync
        def _(sp):
            def rows(it, u):
                for to, of in ((drow, D["dst_row"]), (lrow, D["lo_row"]), (hrow, D["hi_row"])):
                    sp.dma_start(to[u][:, :, :],
                                 of[bass.ds(it * G, G), :].partition_broadcast(P)).then_inc(rows_in[u], 16)

            rows(0, 0)
            rows(1, 1)
            with sp.Fori(0, STEPS_E // 2 - 1) as i:
                for u in range(2):
                    sp.wait_ge(same_ready, 2 * i + u + 1)
                    rows(2 * i + u + 2, u)

        @block.gpsimd
        def _(pool):
            def gather(it, u, h):
                if h == 0:
                    pool.wait_ge(cols_ready, it + 1)
                    pool.sem_inc(gathers, 1)
                for c in range(h * COPIES, (h + 1) * COPIES):
                    pool.indirect_dma_start(got[u][:, c, :], None, D["table"],
                                            bass.IndirectOffsetOnAxis(ap=src_idx[u][:, c:c + 1], axis=0)
                                            ).then_inc(gathered[u], 16)

            def scatter(it, u, k, h):
                if h == 0:
                    pool.wait_ge(put_ready, it + 2)
                    pool.wait_ge(put_idx_ready, it + 1)
                    if u or not isinstance(k, int):
                        pool.wait_ge(added[1 - u][1], 16 * COPIES * (k + u))
                    pool.sem_inc(landed, 1)
                else:
                    pool.wait_ge(added[u][0], 16 * COPIES * (k + 1))
                    pool.sem_inc(half_landed, 1)
                for c in range(h * COPIES, (h + 1) * COPIES):
                    pool.indirect_dma_start(D["acc"][c % COPIES],
                                            bass.IndirectOffsetOnAxis(ap=put_idx[u][:, c:c + 1], axis=0),
                                            put[u][:, c, :], None, compute_op=ALU.add).then_inc(added[u][h], 16)

            def both(to_gather, to_scatter):
                for h in range(2):
                    if to_gather:
                        gather(*to_gather, h)
                    if to_scatter:
                        scatter(*to_scatter, h)

            pool.sem_inc(landed, 1)
            both((0, 0), None)
            both((1, 1), (0, 0, 0))
            with pool.Fori(0, STEPS_E // 2 - 1) as i:
                both((2 * i + 2, 0), (2 * i + 1, 1, i))
                both((2 * i + 3, 1), (2 * i + 2, 0, i + 1))
            both(None, (STEPS_E - 1, 1, STEPS_E // 2 - 1))
            pool.wait_ge(added[1][1], 16 * COPIES * STEPS_E // 2)

        @block.scalar
        def _(act):
            def columns(it, u):
                cols = bass.ds(it * G, G)
                act.activation(src_idx[u][:, :], C.src[:, cols], ACT.Copy)
                act.activation(dcol[u][:, :], C.dst[:, cols], ACT.Copy)
                act.activation(wcol[u][:, :], C.where[:, cols], ACT.Copy)
                act.drain().then_inc(cols_ready, 1)

            def keep_adst(it, u):
                act.wait_ge(sum_done, UNITS * (it + 1))
                act.activation(adst[u][:, :, :], ps_d[:, :, :], ACT.Copy).then_inc(adst_ready, 1)

            def weigh(it, u):
                act.wait_ge(diff_ready, it + 1)
                act.activation(msg[:, :, 0:HEADS], diff[:, :, :], ACT.Exp).then_inc(w_ready, 1)
                act.wait_ge(merged, it + 1)
                act.wait_ge(landed, it + 1)
                act.activation(put[u][:, :, :], ps_m[:, :, :], ACT.Copy).then_inc(put_ready, 1)

            act.sem_inc(put_ready, 1)
            columns(0, 0)
            columns(1, 1)
            keep_adst(0, 0)
            with act.Fori(0, STEPS_E // 2 - 1) as i:
                for u in range(2):
                    keep_adst(2 * i + u + 1, 1 - u)
                    weigh(2 * i + u, u)
                    columns(2 * i + u + 2, u)
            keep_adst(STEPS_E - 1, 1)
            weigh(STEPS_E - 2, 0)
            weigh(STEPS_E - 1, 1)

        @block.tensor
        def _(pe):
            def total(it, n):
                at_least(pe, prod_ready, UNITS * it + n + 1)
                c0, h0 = unit_at(n)
                for j in range(PAIR):
                    for c in range(QUAD):
                        ins = pe.matmul(ps_d[:, c0 + c, h0 + j:h0 + j + 1], prod[n % 2][:, j, c * P:(c + 1) * P],
                                        K.ones[:, 0:1], start=True, stop=True)
                ins.then_inc(sum_done, 1)

            def select(it, u):
                at_least(pe, adst_ready, it)
                pe.wait_ge(hot_ready, it + 1)
                for n in range(UNITS):
                    at_least(pe, prod_ready, UNITS * it + n - RING + 1)
                    c0, h0 = unit_at(n)
                    for j in range(PAIR):
                        for t in range(3):
                            ins = pe.matmul(ps_a[n % RING][:, j, :], K.AD[:, t, h0 + j, :],
                                            hot[:, c0:c0 + QUAD, :].rearrange("p c e -> p (c e)"), start=t == 0,
                                            stop=t == 2)
                    ins.then_inc(sel_done, 1)
                    if n:
                        total(it, n - 1)
                total(it, UNITS - 1)

            def merge(it, u):
                pe.wait_ge(msg_ready, it + 1)
                pe.wait_ge(put_ready, it + 1)
                for c in range(G):
                    ins = pe.matmul(ps_m[:, c, :], same[u][:, c, :], msg[:, c, :], start=True, stop=True)
                ins.then_inc(merged, 1)

            select(0, 0)
            with pe.Fori(0, STEPS_E // 2 - 1) as i:
                select(2 * i + 1, 1)
                merge(2 * i, 0)
                select(2 * i + 2, 0)
                merge(2 * i + 1, 1)
            select(STEPS_E - 1, 1)
            merge(STEPS_E - 2, 0)
            merge(STEPS_E - 1, 1)

        @block.vector
        def _(dve):
            def prepare(it, u, k):
                dve.wait_ge(rows_in[u], 48 * (k + 1))
                at_least(dve, sel_done, UNITS * it)
                dve.tensor_scalar(hot[:, :, :], lrow[u][:, :, :], K.part, None, ALU.is_equal)
                dve.tensor_scalar(hot_b[:, :, :], hrow[u][:, :, :], K.part, None, ALU.is_equal)
                dve.drain().then_inc(hot_ready, 1)
                dve.wait_ge(cols_ready, it + 1)
                at_least(dve, merged, it - 1)
                for n in range(UNITS):
                    for c in range(2 * n, 2 * n + 2):
                        ins = dve.scalar_tensor_tensor(out=same[u][:, c, :], in0=drow[u][:, c, :],
                                                       scalar=dcol[u][:, c:c + 1], in1=K.upto, op0=ALU.is_equal,
                                                       op1=ALU.mult, accum_out=rank[u][:, c:c + 1])
                    dve.wait_ge(sel_done, UNITS * it + n + 1)
                    at_least(dve, sum_done, UNITS * it + n - 1)
                    c0, _ = unit_at(n)
                    dve.tensor_tensor(prod[n % 2][:, :, :], ps_a[n % RING][:, :, :],
                                      hot_b[:, c0:c0 + QUAD, :].rearrange("p c e -> p (c e)").unsqueeze(1)
                                      .to_broadcast([P, PAIR, QUAD * P]), ALU.mult).then_inc(prod_ready, 1)
                dve.drain().then_inc(same_ready, 1)

            def weigh(it, u, k):
                dve.scalar_tensor_tensor(out=rank[u][:, :], in0=rank[u][:, :], scalar=1.0, in1=wcol[u][:, :],
                                         op0=ALU.is_equal, op1=ALU.mult)
                top = K.top[:, :].unsqueeze(1).to_broadcast([P, G, HEADS])
                dve.wait_ge(adst_ready, it + 1)
                dve.tensor_tensor(bound[:, :, :], adst[u][:, :, :], top, ALU.add)
                dve.wait_ge(gathered[u], 16 * G * (k + 1))
                dve.tensor_tensor(sc[:, :, :], adst[u][:, :, :], got[u][:, :, 0:HEADS], ALU.add)
                dve.drain()
                for t in (bound, sc):
                    dve.scalar_tensor_tensor(out=t[:, :, :], in0=t[:, :, :], scalar=0.2, in1=t[:, :, :],
                                             op0=ALU.mult, op1=ALU.max)
                dve.drain()
                dve.tensor_tensor(diff[:, :, :], sc[:, :, :], bound[:, :, :], ALU.subtract).then_inc(diff_ready, 1)
                dve.wait_ge(w_ready, it + 1)
                dve.tensor_tensor(msg[:, :, HEADS:ROW].rearrange("p c (h e) -> p c h e", e=GE),
                                  got[u][:, :, HEADS:ROW].rearrange("p c (h e) -> p c h e", e=GE),
                                  msg[:, :, 0:HEADS].unsqueeze(3).to_broadcast([P, G, HEADS, GE]),
                                  ALU.mult).then_inc(msg_ready, 1)
                dve.wait_ge(landed, it + 1)
                dve.tensor_scalar(put_idx[u][:, :], rank[u][:, :], K.trash, None, ALU.add).then_inc(put_idx_ready, 1)

            prepare(0, 0, 0)
            prepare(1, 1, 0)
            weigh(0, 0, 0)
            with dve.Fori(0, STEPS_E // 2 - 1) as i:
                prepare(2 * i + 2, 0, i + 1)
                weigh(2 * i + 1, 1, i)
                prepare(2 * i + 3, 1, i + 1)
                weigh(2 * i + 2, 0, i + 1)
            weigh(STEPS_E - 1, 1, STEPS_E // 2 - 1)
            dve.drain()


def combine_stage(nc, K, D):
    with ExitStack() as ctx:
        sb = lambda n, s, d=F32: ctx.enter_context(nc.sbuf_tensor("cb_" + n, s, d))
        sem = lambda n: ctx.enter_context(nc.semaphore("cb_" + n))
        total = sb("total", [P, B, ROW])
        part = [sb(f"part{k}", [P, B, ROW]) for k in range(2)]
        e, bound = sb("e", [P, B, HEADS]), sb("bound", [P, B, HEADS])
        w = sb("w", [P, B, HEADS])
        agg, sq = sb("agg", [P, B, HE]), sb("sq", [P, B, HE])
        mean, var = sb("mean", [P, B]), sb("var", [P, B])
        rows = sb("rows", [P, 3, HE])
        in_sem, summed, diff_ready, w_ready, var_ready, std_ready = [
            sem(n) for n in ("in", "summed", "diff_ready", "w_ready", "var_ready", "std_ready")]
        block = ctx.enter_context(nc.Block())
        rows_in = sem("rows_in")

        @block.sync
        def _(sp):
            for t, v in enumerate((D["b_gat"], D["ln_gamma"], D["ln_beta"])):
                sp.dma_start(rows[:, t, :], v.partition_broadcast(P)).then_inc(rows_in, 16)
            for k in range(COPIES):
                if k >= 2:
                    sp.wait_ge(summed, k - 1)
                sp.dma_start(part[k % 2][:, :, :].rearrange("p b c -> p (b c)"),
                             D["acc"][k][0:M, :].rearrange("(n b) c -> n (b c)", b=B)).then_inc(in_sem, 16)
                sp.wait_ge(in_sem, 16 * (k + 1))

        @block.scalar
        def _(act):
            act.wait_ge(diff_ready, 1)
            act.activation(w[:, :, :], e[:, :, :], ACT.Exp).then_inc(w_ready, 1)
            act.wait_ge(var_ready, 1)
            act.activation(var[:, :], var[:, :], ACT.Sqrt, bias=K.eps[:, :], scale=1.0 / HE).then_inc(std_ready, 1)

        @block.vector
        def _(dve):
            def step(ins):
                dve.drain()
            h_view = lambda t: t.rearrange("p b (h e) -> p b h e", e=GE)
            over_e = lambda t: t.unsqueeze(3).to_broadcast([P, B, HEADS, GE])
            over_c = lambda t: t.unsqueeze(2).to_broadcast([P, B, HE])
            over_b = lambda t, n: t.unsqueeze(1).to_broadcast([P, B, n])
            dve.tensor_tensor(bound[:, :, :], K.TAD[:, :, :], over_b(K.top[:, :], HEADS), ALU.add)
            step(dve.tensor_tensor(e[:, :, :], K.TAD[:, :, :], K.TA[:, :, 0:HEADS], ALU.add))
            for t in (bound, e):
                step(dve.scalar_tensor_tensor(out=t[:, :, :], in0=t[:, :, :], scalar=0.2, in1=t[:, :, :],
                                              op0=ALU.mult, op1=ALU.max))
            dve.tensor_tensor(e[:, :, :], e[:, :, :], bound[:, :, :], ALU.subtract).then_inc(diff_ready, 1)
            dve.wait_ge(w_ready, 1)
            dve.tensor_copy(total[:, :, 0:HEADS], w[:, :, :])
            step(dve.tensor_tensor(h_view(total[:, :, HEADS:ROW]), h_view(K.TA[:, :, HEADS:ROW]), over_e(w[:, :, :]),
                                   ALU.mult))
            for k in range(COPIES):
                dve.wait_ge(in_sem, 16 * (k + 1))
                dve.tensor_tensor(total[:, :, :], total[:, :, :], part[k % 2][:, :, :], ALU.add)
                dve.drain().then_inc(summed, 1)
            step(dve.tensor_scalar(w[:, :, :], total[:, :, 0:HEADS], 1e-16, None, ALU.add))
            step(dve.reciprocal(w[:, :, :], w[:, :, :]))
            step(dve.tensor_tensor(h_view(agg[:, :, :]), h_view(total[:, :, HEADS:ROW]), over_e(w[:, :, :]),
                                   ALU.mult))
            dve.wait_ge(rows_in, 48)
            step(dve.tensor_tensor(agg[:, :, :], agg[:, :, :], over_b(rows[:, 0, :], HE), ALU.add))
            step(dve.tensor_reduce(mean[:, :], agg[:, :, :], AX.X, ALU.add))
            step(dve.tensor_scalar(mean[:, :], mean[:, :], 1.0 / HE, None, ALU.mult))
            step(dve.tensor_tensor(agg[:, :, :], agg[:, :, :], over_c(mean[:, :]), ALU.subtract))
            step(dve.tensor_tensor(sq[:, :, :], agg[:, :, :], agg[:, :, :], ALU.mult))
            dve.tensor_reduce(var[:, :], sq[:, :, :], AX.X, ALU.add).then_inc(var_ready, 1)
            dve.wait_ge(std_ready, 1)
            step(dve.reciprocal(var[:, :], var[:, :]))
            step(dve.tensor_tensor(agg[:, :, :], agg[:, :, :], over_c(var[:, :]), ALU.mult))
            step(dve.tensor_tensor(agg[:, :, :], agg[:, :, :], over_b(rows[:, 1, :], HE), ALU.mult))
            step(dve.tensor_tensor(agg[:, :, :], agg[:, :, :], over_b(rows[:, 2, :], HE), ALU.add))
            step(dve.tensor_reduce(K.gates4[:, :, :], agg[:, :, :].rearrange("p b (h e) -> p b e h", e=GE), AX.X,
                                   ALU.add))
            step(dve.tensor_scalar(K.gates4[:, :, :], K.gates4[:, :, :], 1.0 / HEADS, None, ALU.mult))


def top2(dve, K, gates, E, T, gap_ready, exp_ready, count, nb=B):
    over = lambda t: t[:, :].unsqueeze(2).to_broadcast([P, nb, E])

    def pick(scores, top, out):
        dve.tensor_reduce(top[:, :], scores[:, :, :], AX.X, ALU.max)
        dve.drain()
        dve.tensor_tensor(T.key[:, :, :], scores[:, :, :], over(top), ALU.is_ge)
        dve.drain()
        dve.tensor_tensor(T.key[:, :, :], T.key[:, :, :], T.rev[:, :].unsqueeze(1).to_broadcast([P, nb, E]), ALU.mult)
        dve.drain()
        dve.tensor_reduce(T.k1[:, :], T.key[:, :, :], AX.X, ALU.max)
        dve.drain()
        dve.tensor_tensor(out[:, :, :], T.key[:, :, :], over(T.k1), ALU.is_equal)
        dve.drain()

    pick(gates, T.m1, T.first)
    dve.scalar_tensor_tensor(out=T.rest[:, :, :], in0=T.first[:, :, :], scalar=-1e30, in1=gates[:, :, :],
                             op0=ALU.mult, op1=ALU.add)
    dve.drain()
    pick(T.rest, T.m2, T.rest)
    dve.tensor_tensor(T.m2[:, :], T.m2[:, :], T.m1[:, :], ALU.subtract).then_inc(gap_ready, 1)
    dve.wait_ge(exp_ready, count)
    dve.tensor_scalar(T.m1[:, :], T.m2[:, :], 1.0, None, ALU.add)
    dve.drain()
    dve.reciprocal(T.m1[:, :], T.m1[:, :])
    dve.drain()
    dve.tensor_tensor(T.m2[:, :], T.m2[:, :], T.m1[:, :], ALU.mult)
    dve.tensor_tensor(T.first[:, :, :], T.first[:, :, :], over(T.m1), ALU.mult)
    dve.drain()
    dve.tensor_tensor(T.rest[:, :, :], T.rest[:, :, :], over(T.m2), ALU.mult)
    dve.drain()
    dve.tensor_tensor(gates[:, :, :], T.first[:, :, :], T.rest[:, :, :], ALU.add)


def top2_scratch(sb, E, nb=B):
    T = Buffers()
    T.key, T.rest, T.first = (sb(n, [P, nb, E]) for n in ("key", "rest", "first"))
    T.m1, T.m2, T.k1 = (sb(n, [P, nb]) for n in ("m1", "m2", "k1"))
    T.rev = sb("rev", [P, E])
    return T


def top2_stage(nc, K, gates, E, tag, ahead):
    with ExitStack() as ctx:
        T = top2_scratch(lambda n, s: ctx.enter_context(nc.sbuf_tensor(tag + n, s, F32)), E)
        gap_ready = ctx.enter_context(nc.semaphore(tag + "gap_ready"))
        exp_ready = ctx.enter_context(nc.semaphore(tag + "exp_ready"))
        ahead_in = ctx.enter_context(nc.semaphore(tag + "ahead_in"))
        block = ctx.enter_context(nc.Block())

        @block.sync
        def _(sp):
            bring(sp, ahead_in, ahead)

        @block.scalar
        def _(act):
            act.wait_ge(gap_ready, 1)
            act.activation(T.m2[:, :], T.m2[:, :], ACT.Exp).then_inc(exp_ready, 1)

        @block.vector
        def _(dve):
            dve.tensor_scalar(T.rev[:, :], K.iota[:, 0:E], -1.0, float(E), ALU.mult, ALU.add)
            dve.drain()
            top2(dve, K, gates, E, T, gap_ready, exp_ready, 1)
            dve.drain()


def expert_weights(nc, ctx, tag, E, w1, b1, w2, b2):
    sb = lambda n, s: ctx.enter_context(nc.sbuf_tensor(tag + n, s, F32))
    C2 = HID // P
    V = Buffers()
    V.W1, V.W2 = sb("W1", [P, E, HID]), sb("W2", [P, E, C2, F])
    V.B1, V.B2 = sb("B1", [P, E, C2]), sb("B2", [E, F])
    V.loads = [(V.W1[:, :, :], w1.rearrange("e d f -> d e f")), (V.B2[:, :], b2), (V.B1[:, :, :], b1)]
    V.loads += [(V.W2[:, :, c, :], w2[:, c * P:(c + 1) * P, :].rearrange("e f d -> f e d")) for c in range(C2)]
    return V


def gcn_weights(nc, ctx, D):
    sb = lambda n, s: ctx.enter_context(nc.sbuf_tensor("gc_" + n, s, F32))
    C2 = HID // P
    V = Buffers()
    V.adjn, V.adjt = sb("adjn", [NN, B, NN]), sb("adjt", [NN, B, NN])
    V.W1, V.W2 = sb("W1", [P, NG, HID]), sb("W2", [P, NG, C2, F])
    V.B1, V.B2, V.fw = sb("B1", [P, NG, C2]), sb("B2", [NN, NG, F]), sb("fw", [NN, NG])
    V.loads = [(V.adjn[:, :, :], D["adj"][:, 0:NN, 0:NN].rearrange("b n m -> n b m")),
               (V.adjt[:, :, :], D["adjT"][:, 0:NN, 0:NN].rearrange("b m n -> m b n")),
               (V.fw[:, :], D["fusion_w"].partition_broadcast(NN)), (V.W1[:, :, :], D["gW1"].rearrange("e d f -> d e f")),
               (V.B2[:, :, :], D["gb2"].partition_broadcast(NN)), (V.B1[:, :, :], D["gb1"])]
    V.loads += [(V.W2[:, :, c, :], D["gW2"][:, c * P:(c + 1) * P, :].rearrange("e f d -> f e d")) for c in range(C2)]
    return V


def experts_stage(nc, K, D, tag, E, V, func, gates=None, router=None, affine=None, ahead=()):
    with ExitStack() as ctx:
        sb = lambda n, s, d=F32: ctx.enter_context(nc.sbuf_tensor(tag + n, s, d))
        pb = lambda n, s: ctx.enter_context(nc.psum_tensor(tag + n, s, F32))
        sem = lambda n: ctx.enter_context(nc.semaphore(tag + n))
        pair = lambda n, s: [sb(f"{n}{k}", s) for k in range(2)]
        C2 = HID // P
        W1, W2, B1, B2 = V.W1, V.W2, V.B1, V.B2
        y, yT = pair("y", [P, U, F]), pair("yT", [P, U, P])
        g, gT = pair("g", [P, U, E]), pair("gT", [E, U, P])
        stats, mv, std = sb("stats", [P, U, 6]), pair("mv", [P, U, 2]), pair("std", [P, U])
        hid = pair("hid", [P, C2, U * P])
        ps_T, ps_b = pb("ps_T", [P, U, P]), pb("ps_b", [P, U, P])
        ps_h = [[pb(f"ps_h{k}{c}", [P, U * P]) for c in range(C2)] for k in range(2)]
        ps_o = [pb(f"ps_o{k}", [P, U, F]) for k in range(2)]
        (w_in, stats_done, std_ready, y_ready, yT_done, yT_ready, g_ready, gT_done, gT_ready, b_done, b_used,
         h_done, h_ready, o_done, o_used) = [
            sem(n) for n in ("w_in", "stats_done", "std_ready", "y_ready", "yT_done", "yT_ready", "g_ready",
                             "gT_done", "gT_ready", "b_done", "b_used", "h_done", "h_ready", "o_done", "o_used")]
        loads, ahead_in = 0, sem("ahead_in")
        if router:
            gw, gb = sb("gw", [P, E]), sb("gb", [P, E])
            T = top2_scratch(sb, E, U)
            logits_done, gap_ready, exp_ready = sem("logits_done"), sem("gap_ready"), sem("exp_ready")
            loads += 2
        if affine:
            gamma, beta = sb("gamma", [P, F]), sb("beta", [P, F])
            z, fmv, fstd = sb("z", [P, U, F]), sb("fmv", [P, U, 2]), sb("fstd", [P, U])
            fstats_done, fstd_ready, z_ready, out_ready, stored = (
                sem(n) for n in ("fstats_done", "fstd_ready", "z_ready", "out_ready", "stored"))
            loads += 2
        at = [1, 2, 3, 4, 5, 6, 8, 10] if router else [0, 1, 2, 3, 9, 9, 2, 3]
        STATS, NORM, TRANSPOSE, COPY, SCORE, PICK, GATES_T, GATES_COPY = at
        last = STEPS - 1
        block = ctx.enter_context(nc.Block())

        @block.sync
        def _(sp):
            if router:
                sp.dma_start(gw[:, :], router[0]).then_inc(w_in, 16)
                sp.dma_start(gb[:, :], router[1].partition_broadcast(P)).then_inc(w_in, 16)
            if affine:
                sp.dma_start(gamma[:, :], affine[0].partition_broadcast(P)).then_inc(w_in, 16)
                sp.dma_start(beta[:, :], affine[1].partition_broadcast(P)).then_inc(w_in, 16)
                sp.sem_inc(stored, 16)
                with sp.Fori(0, STEPS) as i:
                    sp.wait_ge(out_ready, i + 1)
                    sp.dma_start(D["out"][bass.ds(U * i, U)].rearrange("b n f -> n b f"),
                                 z[:, :, :]).then_inc(stored, 16)
                sp.wait_ge(stored, 16 * (STEPS + 1))
            if ahead:
                bring(sp, ahead_in, ahead)

        @block.gpsimd
        def _(pool):
            if gates is not None:
                def gates_of(it, k):
                    at_least(pool, gT_done, it - 1)
                    at_least(pool, o_used, E * (it - 1))
                    pool.tensor_copy(g[k][:, :, :], gates[:, bass.ds(U * it, U), :]).then_inc(g_ready, 1)

                gates_of(0, 0)
                gates_of(1, 1)
                with pool.Fori(0, STEPS // 2 - 1) as i:
                    gates_of(2 * i + 2, 0)
                    gates_of(2 * i + 3, 1)
            if affine:
                pool.wait_ge(w_in, 16 * loads)
                over = lambda t: t[:, :].unsqueeze(1).to_broadcast([P, U, F])
                with pool.Fori(0, STEPS) as i:
                    pool.wait_ge(z_ready, i + 1)
                    pool.tensor_tensor(z[:, :, :], z[:, :, :], over(gamma), ALU.mult)
                    pool.drain()
                    pool.tensor_tensor(z[:, :, :], z[:, :, :], over(beta), ALU.add)
                    pool.drain()
                    pool.tensor_tensor(z[:, :, :], z[:, :, :], K.X[:, bass.ds(U * i, U), :],
                                       ALU.add).then_inc(out_ready, 1)

        @block.tensor
        def _(pe):
            def transpose_rows(it, k):
                pe.wait_ge(y_ready, it + 1)
                if router:
                    at_least(pe, g_ready, it)
                for u in range(U):
                    ins = pe.transpose(ps_T[:, u, :], y[k][:, u, :], K.ident)
                ins.then_inc(yT_done, 1)

            def score(it, k):
                pe.wait_ge(yT_ready, it + 1)
                for u in range(U):
                    ins = pe.matmul(ps_T[:, u, 0:E], yT[k][:, u, :], gw[:, :], start=True, stop=True)
                ins.then_inc(logits_done, 1)

            def transpose_gates(it, k):
                pe.wait_ge(g_ready, it + 1)
                at_least(pe, b_used, it)
                for u in range(U):
                    ins = pe.transpose(ps_b[0:E, u, :], g[k][:, u, :], K.ident)
                ins.then_inc(gT_done, 1)

            def second(it, e):
                n = E * it + e
                pe.wait_ge(h_ready, n + 1)
                at_least(pe, o_used, n - 1)
                for u in range(U):
                    for c in range(C2):
                        ins = pe.matmul(ps_o[e % 2][:, u, :], hid[e % 2][:, c, u * P:(u + 1) * P],
                                        W2[:, e % E, c, :], start=c == 0, stop=c == C2 - 1)
                ins.then_inc(o_done, 1)

            def step(it, k, more=True, former=True):
                pe.wait_ge(yT_ready, it + 1)
                pe.wait_ge(gT_ready, it + 1)
                for u in range(U):
                    ins = pe.matmul(ps_b[:, u, :], gT[k][:, u, :], B2[:, :], start=True, stop=True)
                ins.then_inc(b_done, 1)
                for e in range(E):
                    at_least(pe, h_ready, E * it + e - 1)
                    for c in range(C2):
                        ins = pe.matmul(ps_h[e % 2][c][:, :], W1[:, e, c * P:(c + 1) * P],
                                        yT[k][:, :, :].rearrange("p u n -> p (u n)"), start=True, stop=True)
                    ins.then_inc(h_done, 1)
                    if e or former:
                        second(it, e - 1)
                    if more and e == TRANSPOSE:
                        transpose_rows(it + 1, 1 - k)
                    if more and router and e == SCORE:
                        score(it + 1, 1 - k)
                    if more and e == GATES_T:
                        transpose_gates(it + 1, 1 - k)

            at_least(pe, w_in, 16 * loads)
            transpose_rows(0, 0)
            if router:
                score(0, 0)
            transpose_gates(0, 0)
            step(0, 0, former=False)
            with pe.Fori(0, STEPS // 2 - 1) as i:
                step(2 * i + 1, 1)
                step(2 * i + 2, 0)
            step(last, 1, more=False)
            second(last, E - 1)

        @block.scalar
        def _(act):
            def root(it, k):
                act.wait_ge(stats_done, it + 1)
                act.activation(std[k][:, :], mv[k][:, :, 1], ACT.Sqrt, bias=K.eps[:, :]).then_inc(std_ready, 1)

            def copy_rows(it, k):
                act.wait_ge(yT_done, it + 1)
                act.activation(yT[k][:, :, :], ps_T[:, :, :], ACT.Copy).then_inc(yT_ready, 1)

            def exponential(it, k):
                act.wait_ge(gap_ready, it + 1)
                act.activation(T.m2[:, :], T.m2[:, :], ACT.Exp).then_inc(exp_ready, 1)

            def copy_gates(it, k):
                act.wait_ge(gT_done, it + 1)
                act.activation(gT[k][:, :, :], ps_b[0:E, :, :], ACT.Copy).then_inc(gT_ready, 1)

            def final_root(it):
                act.wait_ge(fstats_done, it + 1)
                act.activation(fstd[:, :], fmv[:, :, 1], ACT.Sqrt, bias=K.eps[:, :]).then_inc(fstd_ready, 1)

            def step(it, k, more=True, former=True):
                for e in range(E):
                    if more and e == NORM:
                        root(it + 1, 1 - k)
                    if affine and former and e == 1:
                        final_root(it - 1)
                    if more and e == COPY:
                        copy_rows(it + 1, 1 - k)
                    if more and router and e == PICK + 1:
                        exponential(it + 1, 1 - k)
                    if more and e == GATES_COPY:
                        copy_gates(it + 1, 1 - k)
                    n = E * it + e
                    act.wait_ge(h_done, n + 1)
                    at_least(act, o_done, n - 1)
                    for c in range(C2):
                        ins = act.activation(hid[e % 2][:, c, :], ps_h[e % 2][c][:, :], func,
                                             bias=B1[:, e, c:c + 1])
                    ins.then_inc(h_ready, 1)

            root(0, 0)
            copy_rows(0, 0)
            if router:
                exponential(0, 0)
            copy_gates(0, 0)
            step(0, 0, former=False)
            with act.Fori(0, STEPS // 2 - 1) as i:
                step(2 * i + 1, 1)
                step(2 * i + 2, 0)
            step(last, 1, more=False)
            if affine:
                final_root(last)

        @block.vector
        def _(dve):
            def row_stats(it, k):
                for u in range(U):
                    dve.bn_stats(out=stats[:, u, :], in_=cast_col(K.X, U * it + u))
                dve.drain()
                for u in range(U):
                    dve.bn_aggr(out=mv[k][:, u, :], in_=stats[:, u, :])
                dve.drain().then_inc(stats_done, 1)

            def normalise(it, k):
                dve.wait_ge(std_ready, it + 1)
                dve.reciprocal(std[k][:, :], std[k][:, :])
                dve.drain()
                for u in range(U):
                    dve.tensor_scalar(y[k][:, u, :], cast_col(K.X, U * it + u), mv[k][:, u, 0:1], std[k][:, u:u + 1],
                                      ALU.subtract, ALU.mult)
                dve.drain().then_inc(y_ready, 1)

            def gate(it, k):
                dve.wait_ge(logits_done, it + 1)
                dve.tensor_tensor(g[k][:, :, :], ps_T[:, :, 0:E], gb[:, :].unsqueeze(1).to_broadcast([P, U, E]),
                                  ALU.add)
                dve.drain()
                top2(dve, K, g[k], E, T, gap_ready, exp_ready, it + 1, U)
                dve.drain().then_inc(g_ready, 1)

            def final_stats(it, k):
                for u in range(U):
                    dve.bn_stats(out=stats[:, u, :], in_=y[k][:, u, :])
                dve.drain()
                for u in range(U):
                    dve.bn_aggr(out=fmv[:, u, :], in_=stats[:, u, :])
                dve.drain().then_inc(fstats_done, 1)

            def final_rows(it, k):
                dve.wait_ge(fstd_ready, it + 1)
                dve.reciprocal(fstd[:, :], fstd[:, :])
                dve.drain()
                dve.wait_ge(stored, 16 * (it + 1))
                for u in range(U):
                    dve.tensor_scalar(z[:, u, :], y[k][:, u, :], fmv[:, u, 0:1], fstd[:, u:u + 1], ALU.subtract,
                                      ALU.mult)
                dve.drain().then_inc(z_ready, 1)

            def step(it, k, more=True, former=True):
                total = lambda u: y[k][:, u, :] if affine else cast_col(K.X, U * it + u)
                dve.wait_ge(b_done, it + 1)
                whole = y[k][:, :, :] if affine else K.X[:, bass.ds(U * it, U), :]
                dve.tensor_tensor(whole, whole, ps_b[:, :, :], ALU.add)
                dve.drain().then_inc(b_used, 1)
                for e in range(E):
                    if affine and former and e == 1:
                        final_rows(it - 1, 1 - k)
                    if more and e == STATS:
                        row_stats(it + 1, 1 - k)
                    if more and e == NORM:
                        normalise(it + 1, 1 - k)
                    if more and router and e == PICK:
                        gate(it + 1, 1 - k)
                    dve.wait_ge(o_done, E * it + e + 1)
                    for u in range(U):
                        dve.scalar_tensor_tensor(out=total(u), in0=ps_o[e % 2][:, u, :], scalar=g[k][:, u, e:e + 1],
                                                 in1=total(u), op0=ALU.mult, op1=ALU.add)
                    dve.drain().then_inc(o_used, 1)
                if affine:
                    final_stats(it, k)

            if router:
                dve.tensor_scalar(T.rev[:, :], K.iota[:, 0:E], -1.0, float(E), ALU.mult, ALU.add)
                dve.wait_ge(w_in, 16 * loads)
            else:
                dve.wait_ge(g_ready, 2)
            row_stats(0, 0)
            normalise(0, 0)
            if router:
                gate(0, 0)
            step(0, 0, former=False)
            with dve.Fori(0, STEPS // 2 - 1) as i:
                step(2 * i + 1, 1)
                step(2 * i + 2, 0)
            step(last, 1, more=False)
            if affine:
                final_rows(last, 1)


def grouped_gcn_stage(nc, K, D, V, ahead):
    with ExitStack() as ctx:
        sb = lambda n, s, d=F32: ctx.enter_context(nc.sbuf_tensor("gc_" + n, s, d))
        pb = lambda n, s: ctx.enter_context(nc.psum_tensor("gc_" + n, s, F32))
        sem = lambda n: ctx.enter_context(nc.semaphore("gc_" + n))
        pair = lambda n, s: [sb(f"{n}{k}", s) for k in range(2)]
        C2 = HID // P
        GU, UN = NG * U, U * NN
        WIDE = 64
        adjn, adjt, W1, W2, B1, B2, fw = V.adjn, V.adjt, V.W1, V.W2, V.B1, V.B2, V.fw
        fx, wm = sb("fx", [NN, 4]), sb("wm", [NN, NG])
        tmp, an = sb("tmp", [NN, 2, U, NN]), sb("an", [NN, NG, U, NN])
        at_pad = pair("at", [NN, GUN + WIDE - NN])
        at = [t[:, 0:GUN].rearrange("p (g u n) -> p g u n", g=NG, u=U) for t in at_pad]
        deg, dinv, diag = sb("deg", [NN, GU]), sb("dinv", [NN, GU]), sb("diag", [NN, NG, U, NN])
        stats, mv, std = sb("stats", [NN, U, 6]), sb("mv", [NN, U, 2]), sb("std", [NN, U])
        y = pair("y", [NN, U, F])
        ax, hid = sb("ax", [P, GUN]), sb("hid", [P, C2, GUN])
        s2, t2, r2 = pair("s2", [NN, U, F]), pair("t2", [NN, U, F]), pair("r2", [NN, U, F])
        fused = sb("fused", [NN, U, F])
        ps_dd, ps_ax = pb("ps_dd", [WIDE, 512]), pb("ps_ax", [P, 512])
        ps_h = [pb(f"ps_h{c}", [P, 512]) for c in range(C2)]
        ps_s = [pb(f"ps_s{k}", [NN, U, F]) for k in range(2)]
        ps_o = [pb(f"ps_o{k}", [WIDE, U, F]) for k in range(2)]
        (ahead_in, fw_shift, fw_exp, deg_ready, root_ready, diag_ready, diag_done, norm_ready, ax_done, ax_ready,
         h_done, h_ready, s_done, s_ready, o_done, t_ready, r_ready, r_used) = [
            sem(n) for n in ("ahead_in", "fw_shift", "fw_exp", "deg_ready", "root_ready", "diag_ready",
                             "diag_done", "norm_ready", "ax_done", "ax_ready", "h_done", "h_ready", "s_done",
                             "s_ready", "o_done", "t_ready", "r_ready", "r_used")]
        last = STEPS - 1
        block = ctx.enter_context(nc.Block())
        gun = "p g u n -> p (g u n)"
        mask = K.groups[0:NN, :].rearrange("p (g n) -> p g n", g=NG)
        cols = lambda g: slice(g * UN, (g + 1) * UN)
        buf = lambda k, g: (k * NG + g) % 2

        @block.sync
        def _(sp):
            bring(sp, ahead_in, ahead)

        @block.vector
        def _(dve):
            def degrees(it, k):
                eye = K.eye[0:NN, :].unsqueeze(1).to_broadcast([NN, U, NN])
                for t, a in enumerate((adjt, adjn)):
                    dve.tensor_tensor(tmp[:, t], a[:, bass.ds(U * it, U), :], eye, ALU.add)
                for u in range(U):
                    dve.bn_stats(out=stats[:, u, :], in_=cast_col(K.X[0:NN], U * it + u))
                dve.drain()
                for u in range(U):
                    dve.bn_aggr(out=mv[:, u, :], in_=stats[:, u, :])
                wide = [NN, NG, U, NN]
                dve.tensor_tensor(an[:, :, :, :], tmp[:, 1].unsqueeze(1).to_broadcast(wide),
                                  mask.unsqueeze(2).to_broadcast(wide), ALU.mult)
                dve.tensor_tensor(at[k], tmp[:, 0].unsqueeze(1).to_broadcast(wide),
                                  mask.unsqueeze(2).to_broadcast(wide), ALU.mult)
                dve.drain()
                dve.tensor_reduce(deg[:, :], an[:, :, :, :].rearrange("p g u n -> p (g u) n"), AX.X, ALU.add)
                dve.drain()
                dve.scalar_tensor_tensor(out=dinv[:, :], in0=deg[:, :], scalar=0.0, in1=deg[:, :],
                                         op0=ALU.is_equal, op1=ALU.add)
                dve.drain().then_inc(deg_ready, 1)

            def scale_rows(it, k):
                dve.wait_ge(root_ready, it + 1)
                dve.reciprocal(dinv[:, :], dinv[:, :])
                dve.reciprocal(std[:, :], std[:, :])
                dve.drain()
                dve.scalar_tensor_tensor(out=dinv[:, :], in0=deg[:, :], scalar=0.0, in1=dinv[:, :],
                                         op0=ALU.not_equal, op1=ALU.mult)
                for u in range(U):
                    dve.tensor_scalar(y[k][:, u, :], cast_col(K.X[0:NN], U * it + u), mv[:, u, 0:1], std[:, u:u + 1],
                                      ALU.subtract, ALU.mult)
                dve.drain()
                over = dinv[:, :].unsqueeze(2).to_broadcast([NN, GU, NN])
                dve.tensor_tensor(diag[:, :, :, :].rearrange("p g u n -> p (g u) n"),
                                  K.eye[0:NN, :].unsqueeze(1).to_broadcast([NN, GU, NN]), over,
                                  ALU.mult).then_inc(diag_ready, 1)
                rows = at[k].rearrange("p g u n -> p (g u) n")
                dve.tensor_tensor(rows, rows, over, ALU.mult)
                dve.drain()

            def scale_columns(it, k):
                dve.wait_ge(diag_done, it + 1)
                flat = at_pad[k][:, 0:GUN]
                dve.tensor_tensor(flat, flat, ps_dd[0:NN, 0:GUN], ALU.mult)
                dve.drain().then_inc(norm_ready, 1)

            def bias(it, k, g):
                n = NG * it + g
                dve.wait_ge(o_done, n + 1)
                at_least(dve, r_ready, n - 1)
                dve.tensor_tensor(t2[buf(k, g)][:, :, :], ps_o[buf(k, g)][0:NN, :, :],
                                  B2[:, g, :].unsqueeze(1).to_broadcast([NN, U, F]), ALU.add)
                dve.drain().then_inc(t_ready, 1)

            def add(it, k, g):
                n = NG * it + g
                dve.wait_ge(r_ready, n + 1)
                r = r2[buf(k, g)][:, :, :]
                if g == 0:
                    dve.tensor_copy(fused[:, :, :], r)
                else:
                    dve.tensor_tensor(fused[:, :, :], fused[:, :, :], r, ALU.add)
                dve.drain().then_inc(r_used, 1)

            def step(it, k, more=True):
                if more:
                    degrees(it + 1, 1 - k)
                bias(it, k, 0)
                bias(it, k, 1)
                add(it, k, 0)
                if more:
                    scale_rows(it + 1, 1 - k)
                bias(it, k, 2)
                if more:
                    scale_columns(it + 1, 1 - k)
                add(it, k, 1)
                bias(it, k, 3)
                add(it, k, 2)
                bias(it, k, 4)
                add(it, k, 3)
                add(it, k, 4)
                x4 = K.X[0:NN, bass.ds(U * it, U), :]
                dve.tensor_tensor(x4, x4, fused[:, :, :], ALU.add)
                dve.drain()

            dve.tensor_reduce(fx[:, 0:1], fw[:, :], AX.X, ALU.max, negate=True).then_inc(fw_shift, 1)
            dve.wait_ge(fw_exp, 1)
            dve.reciprocal(fx[:, 2:3], fx[:, 1:2])
            dve.drain()
            dve.scalar_tensor_tensor(out=wm[:, :], in0=fw[:, :], scalar=fx[:, 2:3], in1=K.member[0:NN, :],
                                     op0=ALU.mult, op1=ALU.mult)
            for k in range(2):
                dve.memset(at_pad[k][:, GUN:GUN + WIDE - NN], 0.0)
            dve.drain()
            degrees(0, 0)
            scale_rows(0, 0)
            scale_columns(0, 0)
            step(0, 0)
            with dve.Fori(0, STEPS // 2 - 1) as i:
                step(2 * i + 1, 1)
                step(2 * i + 2, 0)
            step(last, 1, more=False)

        @block.scalar
        def _(act):
            def roots(it):
                act.wait_ge(deg_ready, it + 1)
                act.activation(dinv[:, :], dinv[:, :], ACT.Sqrt)
                act.activation(std[:, :], mv[:, :, 1], ACT.Sqrt, bias=K.eps[0:NN, :])
                act.drain().then_inc(root_ready, 1)

            def copy_ax(it):
                act.wait_ge(ax_done, it + 1)
                act.activation(ax[:, :], ps_ax[:, 0:GUN], ACT.Copy).then_inc(ax_ready, 1)

            def hidden(it, g):
                for c in range(C2):
                    ins = act.activation(hid[:, c, cols(g)], ps_h[c][:, cols(g)], ACT.Relu, bias=B1[:, g, c:c + 1])
                ins.then_inc(h_ready, 1)

            def copy_s(it, k, g):
                n = NG * it + g
                act.wait_ge(s_done, n + 1)
                at_least(act, o_done, n - 1)
                act.activation(s2[buf(k, g)][:, :, :], ps_s[buf(k, g)][:, :, :], ACT.Copy).then_inc(s_ready, 1)

            def weigh(it, k, g):
                n = NG * it + g
                act.wait_ge(t_ready, n + 1)
                at_least(act, r_used, n - 1)
                act.activation(r2[buf(k, g)][:, :, :], t2[buf(k, g)][:, :, :], ACT.Relu,
                               scale=wm[:, g:g + 1]).then_inc(r_ready, 1)

            def step(it, k, more=True):
                act.wait_ge(h_done, it + 1)
                for g in range(NG):
                    hidden(it, g)
                copy_s(it, k, 0)
                copy_s(it, k, 1)
                if more:
                    roots(it + 1)
                for g in range(2, NG):
                    weigh(it, k, g - 2)
                    copy_s(it, k, g)
                if more:
                    copy_ax(it + 1)
                weigh(it, k, 3)
                weigh(it, k, 4)

            act.wait_ge(fw_shift, 1)
            act.activation(fw[:, :], fw[:, :], ACT.Exp, bias=fx[:, 0:1], accum_out=fx[:, 1:2])
            act.drain().then_inc(fw_exp, 1)
            roots(0)
            copy_ax(0)
            step(0, 0)
            with act.Fori(0, STEPS // 2 - 1) as i:
                step(2 * i + 1, 1)
                step(2 * i + 2, 0)
            step(last, 1, more=False)

        @block.tensor
        def _(pe):
            def diagonal(it):
                pe.wait_ge(diag_ready, it + 1)
                pe.matmul(ps_dd[:, 0:GUN], K.ones[0:NN, 0:WIDE], diag[:, :, :, :].rearrange(gun), start=True,
                          stop=True).then_inc(diag_done, 1)

            def aggregate(it, k):
                pe.wait_ge(norm_ready, it + 1)
                out = ps_ax[:, 0:GUN].rearrange("p (g u n) -> p g u n", g=NG, u=U)
                for u in range(U):
                    ins = pe.matmul(out[:, :, u, :], y[k][:, u, :], at[k][:, :, u, :], start=True, stop=True)
                ins.then_inc(ax_done, 1)

            def second(it, k, g):
                n = NG * it + g
                pe.wait_ge(h_ready, n + 1)
                at_least(pe, s_ready, n - 1)
                for u in range(U):
                    for c in range(C2):
                        ins = pe.matmul(ps_s[buf(k, g)][:, u, :], hid[:, c, (g * U + u) * NN:(g * U + u + 1) * NN],
                                        W2[:, g, c, :], start=c == 0, stop=c == C2 - 1)
                ins.then_inc(s_done, 1)

            def spread(it, k, g):
                n = NG * it + g
                pe.wait_ge(s_ready, n + 1)
                at_least(pe, t_ready, n - 1)
                for u in range(U):
                    ins = pe.matmul(ps_o[buf(k, g)][:, u, :], at_pad[k][:, (g * U + u) * NN:(g * U + u) * NN + WIDE],
                                    s2[buf(k, g)][:, u, :], start=True, stop=True)
                ins.then_inc(o_done, 1)

            def step(it, k, more=True):
                pe.wait_ge(ax_ready, it + 1)
                at_least(pe, h_ready, NG * it)
                for g in range(NG):
                    for c in range(C2):
                        ins = pe.matmul(ps_h[c][:, cols(g)], W1[:, g, c * P:(c + 1) * P], ax[:, cols(g)], start=True,
                                        stop=True)
                ins.then_inc(h_done, 1)
                second(it, k, 0)
                for g in range(1, NG - 1):
                    second(it, k, g)
                    spread(it, k, g - 1)
                if more:
                    diagonal(it + 1)
                second(it, k, NG - 1)
                if more:
                    aggregate(it + 1, 1 - k)
                spread(it, k, NG - 2)
                spread(it, k, NG - 1)

            diagonal(0)
            aggregate(0, 0)
            step(0, 0)
            with pe.Fori(0, STEPS // 2 - 1) as i:
                step(2 * i + 1, 1)
                step(2 * i + 2, 0)
            step(last, 1, more=False)


def build(nc, D):
    with ExitStack() as ctx:
        sb = lambda n, s, d=F32: ctx.enter_context(nc.sbuf_tensor(n, s, d))
        K = Buffers()
        K.X = sb("X", [P, B, F])
        layout, width = const_layout()
        K.const = sb("const", [P, width])
        view = {name: K.const[:, at:at + n] for name, (at, n) in layout.items()}
        K.ident, K.upto, K.iota, K.part, K.trash = (view[n] for n in ("ident", "upto", "iota", "part", "trash"))
        K.member, K.groups, K.eye, K.ones = (view[n] for n in ("member", "groups", "eye", "ones"))
        K.eps = sb("eps", [P, 1])
        K.gates4 = sb("gates4", [P, B, GE])
        D["table"] = nc.dram_tensor("source_table", [M, ROW], F32, kind="Internal").ap()
        D["acc"] = [nc.dram_tensor(f"accumulator{k}", [M + P, ROW], F32, kind="Internal").ap() for k in range(COPIES)]
        D["hi_row"] = nc.dram_tensor("hi_row", list(D["dst_row"].shape), BF16, kind="Internal").ap()
        D["lo_row"] = nc.dram_tensor("lo_row", list(D["dst_row"].shape), BF16, kind="Internal").ap()
        with ExitStack() as gat:
            gb = lambda n, s, d=F32: gat.enter_context(nc.sbuf_tensor(n, s, d))
            K.wgat, K.top = gb("wgat", [P, ROW + HEADS]), gb("top", [P, HEADS])
            K.zeros = gb("zeros", [P, (M + P) * ROW // P // ZP])
            K.TA, K.AD, K.TAD = gb("TA", [P, B, ROW]), gb("AD", [P, 3, HEADS, B], BF16), gb("TAD", [P, B, HEADS])
            with nc.sbuf_tensor("Y", [P, B, F], F32) as K.Y:
                dense_attention_stage(nc, K, D)
                gat_weights_stage(nc, K, D)
                gelu_and_projection_stage(nc, K, D)
                table_stage(nc, K, D)
            with ExitStack() as edges:
                eb = lambda n, d=F32: edges.enter_context(nc.sbuf_tensor(n, [P, D["dst_col"].shape[1]], d))
                C = Buffers()
                C.src, C.dst, C.where = eb("e_src", I32), eb("e_dst"), eb("e_where")
                C.chunks = D["dst_col"].shape[1]
                edge_index_stage(nc, K, D, C)
                edge_stage(nc, K, D, C)
            combine_stage(nc, K, D)
        X4 = expert_weights(nc, ctx, "x4_", GE, D["W1"], D["b1"], D["W2"], D["b2"])
        top2_stage(nc, K, K.gates4, GE, "t4_", X4.loads)
        CV = gcn_weights(nc, ctx, D)
        experts_stage(nc, K, D, "x4_", GE, X4, ACT.Gelu, gates=K.gates4, ahead=CV.loads)
        X16 = expert_weights(nc, ctx, "x16_", E2, D["fw1"], D["fb1"], D["fw2"], D["fb2"])
        grouped_gcn_stage(nc, K, D, CV, X16.loads)
        experts_stage(nc, K, D, "x16_", E2, X16, ACT.Relu, router=(D["gate_w"], D["gate_b"]),
                      affine=(D["f_gamma"], D["f_beta"]))


NAMES = {"x": "x", "adj": "adj", "gnn_W": "L0_gnn_W", "gnn_a": "L0_gnn_a", "gnn_gamma": "L0_gnn_gamma",
         "gnn_beta": "L0_gnn_beta", "W_gat": "L0_ffn_W_gat", "att_src": "L0_ffn_att_src",
         "att_dst": "L0_ffn_att_dst", "b_gat": "L0_ffn_b_gat", "ln_gamma": "L0_ffn_ln_gamma",
         "ln_beta": "L0_ffn_ln_beta", "W1": "L0_ffn_W1", "b1": "L0_ffn_b1", "W2": "L0_ffn_W2", "b2": "L0_ffn_b2",
         "gW1": "L1_gnn_W1", "gb1": "L1_gnn_b1", "gW2": "L1_gnn_W2", "gb2": "L1_gnn_b2",
         "fusion_w": "L1_gnn_fusion_w", "gate_w": "L1_ffn_gate_w", "gate_b": "L1_ffn_gate_b", "fw1": "L1_ffn_w1",
         "fb1": "L1_ffn_b1", "fw2": "L1_ffn_w2", "fb2": "L1_ffn_b2", "f_gamma": "L1_ffn_gamma",
         "f_beta": "L1_ffn_beta"}


def host_arrays(inputs):
    import numpy as np
    arrays = {k: np.ascontiguousarray(inputs[v]) for k, v in NAMES.items()}
    arrays["adjT"] = np.ascontiguousarray(np.transpose(arrays["adj"], (0, 2, 1)))
    arrays["gnn_a"] = np.ascontiguousarray(arrays["gnn_a"].reshape(2, F).T)
    for name in ("b1", "gb1", "fb1"):
        b = arrays[name]
        arrays[name] = np.ascontiguousarray(b.reshape(len(b), HID // P, P).transpose(2, 0, 1))
    edges = np.ascontiguousarray(inputs["L0_ffn_edge_index"])
    arrays["src_col"] = np.ascontiguousarray(edges[0].reshape(P, -1))
    arrays["dst_col"] = np.ascontiguousarray(edges[1].reshape(P, -1))
    arrays["dst_row"] = np.ascontiguousarray(edges[1].reshape(P, -1).T)
    layout, width = const_layout()
    consts = np.zeros((P, width), np.float32)
    put = lambda name, v: consts.__setitem__((slice(0, len(v)), slice(layout[name][0], sum(layout[name]))), v)
    put("ident", np.eye(P))
    put("upto", np.tril(np.ones((P, P))))
    put("iota", np.tile(np.arange(P), (P, 1)))
    put("part", np.arange(P)[:, None])
    put("trash", M + np.arange(P)[:, None])
    member = np.array([[float(n in g) for g in GROUPS] for n in range(NN)])
    put("member", member)
    put("groups", np.einsum("mg,ng->mgn", member, member).reshape(NN, NG * NN))
    put("eye", np.eye(NN))
    put("ones", np.ones((P, P)))
    arrays["consts"] = consts
    return arrays


def kernel(**inputs):
    import numpy as np
    import concourse.bacc as bacc
    from concourse.bass_utils import run_bass_kernel_spmd

    nc = bacc.Bacc("TRN2", target_bir_lowering=False, num_devices=1)
    arrays = host_arrays(inputs)
    D = {name: nc.dram_tensor(f"in_{name}", a.shape, mybir.dt.from_np(a.dtype), kind="ExternalInput").ap()
         for name, a in arrays.items()}
    D["out"] = nc.dram_tensor("out_x", [B, P, F], F32, kind="ExternalOutput").ap()
    build(nc, D)
    result = run_bass_kernel_spmd(nc, [{f"in_{k}": a for k, a in arrays.items()}], core_ids=[0])
    return np.asarray(result.results[0]["out_x"])
```
